# Optimizing a Trainium2 kernel written in Bass

```python
import numpy as np
import jax
import jax.numpy as jnp

def _softmax(x, axis=-1):
    return jax.nn.softmax(x, axis=axis)

def _gelu(x):
    return jax.nn.gelu(x, approximate=True)

def _silu(x):
    return jax.nn.silu(x)

def _sigmoid(x):
    return jax.nn.sigmoid(x)

def _layernorm(x, axis=-1, eps=1e-05):
    m = jnp.mean(x, axis=axis, keepdims=True)
    v = jnp.var(x, axis=axis, keepdims=True)
    return (x - m) / jnp.sqrt(v + eps)

def _scatter_add(tgt, idx, src, axis=0):
    return tgt.at[idx].add(src)

def _segment_sum(src, seg, n):
    return jax.ops.segment_sum(src, seg, n)
kernel_name = 'mk_adj_resnorm_d2_adj_r2_b7c9b6'

def setup_inputs(seed: int=0):
    np.random.seed(seed)
    _w = jnp.asarray

    def _rec_inputs():
        import jax
        import jax.numpy as jnp
        _gk = jax.random.key(seed)
        x = -0.0002928 + 1 * jax.random.normal(jax.random.fold_in(_gk, 1), (16, 512, 128), jnp.float32)
        _a = jax.random.bernoulli(jax.random.fold_in(_gk, 2), 0.03125, (512, 512))
        _a = jnp.logical_or(_a, jnp.swapaxes(_a, -1, -2))
        _a = jnp.logical_or(_a, jnp.eye(512, dtype=bool))
        adj = _a.astype(jnp.int32)
        return (x, adj)
    x, adj = _rec_inputs()

    def _L0_gnn_setup():
        import jax, jax.numpy as jnp
        import numpy as np
        ALPHA = 0.2
        NEG_INF = -9000000000000000.0

        def _gat(inp, adj_mask, W, a):
            h = jnp.matmul(inp, W)
            F_ = h.shape[-1]
            f1 = jnp.matmul(h, a[:F_, 0])
            f2 = jnp.matmul(h, a[F_:, 0])
            e = jax.nn.leaky_relu(f1[:, :, None] + f2[:, None, :], ALPHA)
            if adj_mask is not None:
                e = jnp.where(adj_mask[None, :, :] > 0, e, NEG_INF)
            att = jax.nn.softmax(e, axis=2)
            h_prime = jnp.einsum('bij,bjf->bif', att, h)
            return jax.nn.elu(h_prime)
        key = jax.random.key(seed)
        ks = jax.random.split(key, 10)
        B, N, Fin, H, O = (16, 512, 128, 256, 128)

        def xavier(k, shape):
            fan_in, fan_out = (shape[0], shape[-1])
            bound = 1.414 * np.sqrt(6.0 / (fan_in + fan_out))
            return jax.random.uniform(k, shape, jnp.float32, -bound, bound)
        return {'x': jax.random.normal(ks[0], (B, N, Fin), jnp.float32), 'adj': jax.random.randint(ks[1], (N, N), 0, 2, jnp.int32), 'mlp1_w': xavier(ks[2], (Fin, H)), 'mlp1_b': jnp.zeros((H,), jnp.float32), 'mlp2_w': xavier(ks[3], (H, O)), 'mlp2_b': jnp.zeros((O,), jnp.float32), 'W_fc': xavier(ks[4], (H, H)), 'a_fc': xavier(ks[5], (2 * H, 1)), 'W_hand': xavier(ks[6], (O, O)), 'a_hand': xavier(ks[7], (2 * O, 1))}
    _L0_gnn_all = _L0_gnn_setup()
    _L0_gnn_in = {k: v for k, v in _L0_gnn_all.items() if k in ('mlp1_w', 'mlp1_b', 'mlp2_w', 'mlp2_b', 'W_fc', 'a_fc', 'W_hand', 'a_hand')}
    del _L0_gnn_all

    def _L1_gnn_setup():
        import jax, jax.numpy as jnp
        import numpy as np
        EPS = 1e-05

        def _layernorm(x, g, b):
            mu = jnp.mean(x, axis=-1, keepdims=True)
            var = jnp.mean(jnp.square(x - mu), axis=-1, keepdims=True)
            return (x - mu) * jax.lax.rsqrt(var + EPS) * g + b
        key = jax.random.key(seed)
        ks = jax.random.split(key, 8)
        F, N, C, H = (2048, 64, 128, 8)
        x = jax.random.normal(ks[0], (F, N, C), dtype=jnp.float32)
        adj = jax.random.randint(ks[1], (N, N), 0, 2, dtype=jnp.int32)
        adj = jnp.maximum(adj, jnp.eye(N, dtype=jnp.int32))
        s = 1.0 / np.sqrt(C)
        w_qkv = jax.random.normal(ks[2], (C, 3 * C), dtype=jnp.float32) * s
        w1 = jax.random.normal(ks[3], (C, C), dtype=jnp.float32) * s
        b1 = jnp.zeros((C,), dtype=jnp.float32)
        w2 = jax.random.normal(ks[4], (C, C), dtype=jnp.float32) * s
        b2 = jnp.zeros((C,), dtype=jnp.float32)
        ln1_g = jnp.ones((C,), jnp.float32)
        ln1_b = jnp.zeros((C,), jnp.float32)
        ln2_g = jnp.ones((C,), jnp.float32)
        ln2_b = jnp.zeros((C,), jnp.float32)
        return {'x': x, 'adj': adj, 'w_qkv': w_qkv, 'ln1_g': ln1_g, 'ln1_b': ln1_b, 'ln2_g': ln2_g, 'ln2_b': ln2_b, 'w1': w1, 'b1': b1, 'w2': w2, 'b2': b2}
    _L1_gnn_all = _L1_gnn_setup()
    _L1_gnn_in = {k: v for k, v in _L1_gnn_all.items() if k in ('w_qkv', 'ln1_g', 'ln1_b', 'ln2_g', 'ln2_b', 'w1', 'b1', 'w2', 'b2')}
    del _L1_gnn_all
    return {'x': x, 'adj': adj, 'L0_gnn_mlp1_w': _L0_gnn_in['mlp1_w'], 'L0_gnn_mlp1_b': _L0_gnn_in['mlp1_b'], 'L0_gnn_mlp2_w': _L0_gnn_in['mlp2_w'], 'L0_gnn_mlp2_b': _L0_gnn_in['mlp2_b'], 'L0_gnn_W_fc': _L0_gnn_in['W_fc'], 'L0_gnn_a_fc': _L0_gnn_in['a_fc'], 'L0_gnn_W_hand': _L0_gnn_in['W_hand'], 'L0_gnn_a_hand': _L0_gnn_in['a_hand'], 'L1_gnn_w_qkv': _L1_gnn_in['w_qkv'], 'L1_gnn_ln1_g': _L1_gnn_in['ln1_g'], 'L1_gnn_ln1_b': _L1_gnn_in['ln1_b'], 'L1_gnn_ln2_g': _L1_gnn_in['ln2_g'], 'L1_gnn_ln2_b': _L1_gnn_in['ln2_b'], 'L1_gnn_w1': _L1_gnn_in['w1'], 'L1_gnn_b1': _L1_gnn_in['b1'], 'L1_gnn_w2': _L1_gnn_in['w2'], 'L1_gnn_b2': _L1_gnn_in['b2']}

def reference(x, adj, L0_gnn_mlp1_w, L0_gnn_mlp1_b, L0_gnn_mlp2_w, L0_gnn_mlp2_b, L0_gnn_W_fc, L0_gnn_a_fc, L0_gnn_W_hand, L0_gnn_a_hand, L1_gnn_w_qkv, L1_gnn_ln1_g, L1_gnn_ln1_b, L1_gnn_ln2_g, L1_gnn_ln2_b, L1_gnn_w1, L1_gnn_b1, L1_gnn_w2, L1_gnn_b2):
    import jax
    import jax.numpy as jnp

    def _L0_gnn_ref(x, adj, mlp1_w, mlp1_b, mlp2_w, mlp2_b, W_fc, a_fc, W_hand, a_hand):
        import jax, jax.numpy as jnp
        import numpy as np
        ALPHA = 0.2
        NEG_INF = -9000000000000000.0

        def _gat(inp, adj_mask, W, a):
            h = jnp.matmul(inp, W)
            F_ = h.shape[-1]
            f1 = jnp.matmul(h, a[:F_, 0])
            f2 = jnp.matmul(h, a[F_:, 0])
            e = jax.nn.leaky_relu(f1[:, :, None] + f2[:, None, :], ALPHA)
            if adj_mask is not None:
                e = jnp.where(adj_mask[None, :, :] > 0, e, NEG_INF)
            att = jax.nn.softmax(e, axis=2)
            h_prime = jnp.einsum('bij,bjf->bif', att, h)
            return jax.nn.elu(h_prime)
        out = jax.nn.relu(jnp.matmul(x, mlp1_w) + mlp1_b)
        residual = out
        out = _gat(jax.nn.relu(out), None, W_fc, a_fc)
        out = jax.nn.elu(out) + residual
        out = jax.nn.relu(jnp.matmul(out, mlp2_w) + mlp2_b)
        residual = out
        out = _gat(jax.nn.relu(out), adj, W_hand, a_hand)
        out = jax.nn.elu(out) + residual
        return jax.nn.relu(out)

    def _L1_gnn_ref(x, adj, w_qkv, ln1_g, ln1_b, ln2_g, ln2_b, w1, b1, w2, b2):
        import jax, jax.numpy as jnp
        import numpy as np
        EPS = 1e-05

        def _layernorm(x, g, b):
            mu = jnp.mean(x, axis=-1, keepdims=True)
            var = jnp.mean(jnp.square(x - mu), axis=-1, keepdims=True)
            return (x - mu) * jax.lax.rsqrt(var + EPS) * g + b
        F, N, C = x.shape
        H = 8
        D = C // H
        qkv = jnp.einsum('fnc,ck->fnk', x, w_qkv)
        q, k, v = jnp.split(qkv, 3, axis=-1)
        q = q.reshape(F, N, H, D)
        k = k.reshape(F, N, H, D)
        v = v.reshape(F, N, H, D)
        scores = jnp.einsum('fnhd,fmhd->fhnm', q, k) / jnp.sqrt(jnp.asarray(D, x.dtype))
        mask = (adj > 0)[None, None, :, :]
        scores = jnp.where(mask, scores, jnp.asarray(-1000000000.0, x.dtype))
        attn = jax.nn.softmax(scores, axis=-1)
        t = jnp.einsum('fhnm,fmhd->fnhd', attn, v).reshape(F, N, C)
        x = _layernorm(x + t, ln1_g, ln1_b)
        h = jax.nn.relu(jnp.einsum('fnc,cd->fnd', x, w1) + b1)
        f_out = jnp.einsum('fnd,dc->fnc', h, w2) + b2
        x = _layernorm(x + f_out, ln2_g, ln2_b)
        return x
    x = _layernorm(x + _L0_gnn_ref(x, adj, L0_gnn_mlp1_w, L0_gnn_mlp1_b, L0_gnn_mlp2_w, L0_gnn_mlp2_b, L0_gnn_W_fc, L0_gnn_a_fc, L0_gnn_W_hand, L0_gnn_a_hand), axis=-1)
    x = _layernorm(x + _L1_gnn_ref(x, adj, L1_gnn_w_qkv, L1_gnn_ln1_g, L1_gnn_ln1_b, L1_gnn_ln2_g, L1_gnn_ln2_b, L1_gnn_w1, L1_gnn_b1, L1_gnn_w2, L1_gnn_b2), axis=-1)
    return x

_drawn_inputs = setup_inputs


def setup_inputs(seed=0):
    import zlib

    import numpy as np

    out = dict(_drawn_inputs(seed))
    spreads = {'L0_gnn_mlp1_b': (0.0, 0.1),
     'L0_gnn_mlp2_b': (0.0, 0.1),
     'L1_gnn_ln1_g': (1.0, 0.2),
     'L1_gnn_ln1_b': (0.0, 0.1),
     'L1_gnn_ln2_g': (1.0, 0.2),
     'L1_gnn_ln2_b': (0.0, 0.1),
     'L1_gnn_b1': (0.0, 0.1),
     'L1_gnn_b2': (0.0, 0.1)}
    factors = {}
    for name, (base, spread) in spreads.items():
        noise = np.random.default_rng([zlib.crc32(name.encode()), seed]).standard_normal(out[name].shape)
        drawn = base * np.exp(spread * noise) if base else spread * noise
        out[name] = jnp.asarray(drawn.astype(out[name].dtype))
    for name, factor in factors.items():
        out[name] = (out[name] * factor).astype(out[name].dtype)
    return out
```

```python
from contextlib import ExitStack

import concourse.bass as bass
from concourse import mybir

P = 128
B, N, C = 16, 512, 128
T = N // P
H = 256
HC = H // P
HEADS, D = 8, 16
GROUPS, GH = 2, 4
STRIP = 32
ALPHA = 0.2
EPS = 1e-5
SCALE = D ** -0.5
NEG = -1e30
Q_TERMS = (0, 1, 2, 0, 1, 0)
K_TERMS = (0, 0, 0, 1, 1, 2)
KS = len(Q_TERMS) * D

ALU = mybir.AluOpType
ACT = mybir.ActivationFunctionType
F32 = mybir.dt.float32
BF16 = mybir.dt.bfloat16
I32 = mybir.dt.int32
AX_X = mybir.AxisListType.X


def gnn_kernel(nc, x, adj, mlp1_w, mlp1_b, mlp2_w, mlp2_b, W_fc, a_fc, W_hand, a_hand,
               w_qkv, ln1_g, ln1_b, ln2_g, ln2_b, w1, b1, w2, b2, out):
    x_dram = x.rearrange("b (p t) c -> b p t c", t=T)
    out_dram = out.rearrange("b (p t) c -> b p t c", t=T)
    split_dram = nc.dram_tensor("qk_split_dram", (2, 2, 3, HEADS, D, N), BF16).ap()

    with ExitStack() as ctx:
        def sb(name, shape, dt=F32):
            return ctx.enter_context(nc.sbuf_tensor(name, shape, dt))

        def psum(name, shape, dt=F32):
            return ctx.enter_context(nc.psum_tensor(name, shape, dt))

        def sem(name):
            return ctx.enter_context(nc.semaphore(name))

        ident = sb("ident", [P, P])
        ones = sb("ones", [P, 1])
        minus_half = sb("minus_half", [P, T])
        minus_one = sb("minus_one", [P, 1])
        neg_nat = sb("neg_nat", [P, T, N])
        neg_T = sb("neg_T", [P, T, N])
        row_count = sb("row_count", [P, T])
        empty = sb("empty", [P, T])
        empty_b = sb("empty_b", [P, N])
        W1 = sb("W1", [P, H])
        b1c = sb("b1c", [P, HC])
        Wfc = sb("Wfc", [P, HC, 2 + H])
        W2 = sb("W2", [P, HC, C])
        b2c = sb("b2c", [P, 1])
        Wh = sb("Wh", [P, 2 + C])
        a_fc_b = sb("a_fc_b", [P, 2 * H])
        a_hand_b = sb("a_hand_b", [P, 2 * C])
        Wqkv = sb("Wqkv", [P, 3 * C])
        M1 = sb("M1", [P, C])
        m1c = sb("m1c", [P, 1])
        M2 = sb("M2", [P, C])
        g1_b = sb("g1_b", [P, C])
        be1_b = sb("be1_b", [P, C])
        g2_b = sb("g2_b", [P, C])
        be2_b = sb("be2_b", [P, C])
        m2_b = sb("m2_b", [P, C])
        wa_tmp = sb("wa_tmp", [P, H])

        x_nat = [sb(f"x_nat{i}", [P, T, C]) for i in range(2)]
        xT = sb("xT", [P, N])
        out1 = sb("out1", [P, HC, N])
        h1 = sb("h1", [P, T, 2 + H + 1])
        f1 = h1[:, :, 0:2]
        fmax1 = sb("fmax1", [P, 1])
        arg1 = sb("arg1", [P, 4, T])
        fac1 = sb("fac1", [P, 4, T])
        low = sb("low", [P, T, N])
        att = sb("att", [P, T, N])
        adj_i = low[:, :, :].bitcast(I32)
        mask_nat = att
        rz1 = sb("rz1", [P, T])
        neg1 = sb("neg1", [P, T, H])
        pos1 = sb("pos1", [P, T, H])
        out2 = sb("out2", [P, N])
        h2 = sb("h2", [P, T, 2 + C + 1])
        h2sum = sb("h2sum", [P, 2, C + 1])
        f2 = h2[:, :, 0:2]
        fmax2 = sb("fmax2", [P, T])
        s2 = sb("s2", [P, T])
        m2 = sb("m2", [P, T])
        row2 = sb("row2", [P, 2, T])
        f2s = sb("f2s", [P, T])
        rz2 = sb("rz2", [P, T])
        neg2 = sb("neg2", [P, T, C])
        pos2 = sb("pos2", [P, T, C])
        y0 = sb("y0", [P, T, C])
        stat = [sb(f"stat{i}", [P, T, 6]) for i in range(4)]
        mv = [sb(f"mv{i}", [P, T, 2]) for i in range(4)]
        var = [sb(f"var{i}", [P, T]) for i in range(4)]
        rstd = [sb(f"rstd{i}", [P, T]) for i in range(4)]
        x1 = [sb(f"x1_{i}", [P, T, C]) for i in range(2)]
        x1T = sb("x1T", [P, N])
        qk_parts = sb("qk_parts", [P, 2, 3, N], BF16)
        qk_rest = sb("qk_rest", [P, 2, N])
        Qs = [sb(f"Qs{i}", [KS, HEADS, N], BF16) for i in range(2)]
        Ks = [sb(f"Ks{i}", [KS, HEADS, N], BF16) for i in range(2)]
        v = [sb(f"v{i}", [P, T, GROUPS, GH, STRIP]) for i in range(2)]
        vsum = sb("vsum", [P, 2, GROUPS * P])
        vcol = [sb(f"vcol{i}", [P, GROUPS]) for i in range(2)]
        masked = sb("masked", [P, 2, 2, N])
        probs = sb("probs", [P, 2, GH, 2, N])
        oT = sb("oT", [P, GROUPS, N])
        rzh = sb("rzh", [P, GROUPS, T, GH])
        attn = sb("attn", [P, T, C])
        y1n = sb("y1n", [P, T, C])
        y1m = sb("y1m", [P, T, C])
        y1T = sb("y1T", [P, N])
        hid = sb("hid", [P, N])
        y2 = sb("y2", [P, T, C])
        y2n = sb("y2n", [P, T, C])
        x1b = sb("x1b", [P, T, C])
        o_nat = sb("o_nat", [P, T, C])

        sc = [psum(f"sc{i}", [P, 2, N]) for i in range(2)]
        oacc = psum("oacc", [P, N])
        s0, s1, s2p = psum("s0", [P, N]), psum("s1", [P, N]), psum("s2p", [P, N])
        bank = [s0, s1, s2p]

        w_loaded = sem("w_loaded")
        const_set = sem("const_set")
        prep = sem("prep")
        adj_T = sem("adj_T")
        waits_passed = sem("waits_passed")
        minus_one_set = sem("minus_one_set")
        x_loaded = [sem("x_loaded0"), sem("x_loaded1")]
        names = """xT_made xT_copied out1_made out1_ready h1_made h1_copied f1b_made fmax1_ready
        arg1_ready fac1_ready rows1_made low1_ready att1_ready gat1_made rz1_ready neg1_ready
        pos1_ready u1_ready w1_ready gat1_ready gat1T_made res1_ready out2_made out2_ready h2_made h2_copied
        f2b_made fmax2_ready s2_ready m2_ready row2_ready rows2_made low2_ready arg2_ready argm_ready
        att2_ready h2sum_ready gat2_made rz2_ready neg2_ready pos2_ready u2_ready w2_ready sum2_ready
        out2T_made sum2b_ready y0_ready x1T_made x1T_copied q_made k_made v_made high_ready rest_ready
        mid_ready low_ready parts_stored stacked v_copied vsum_ready vcol_made vcol_ready
        scores_made masked_ready probs_ready pv_made oT_ready oTT_made rzh_ready attn_ready y1_ready
        y1n_ready y1g_ready y1b_ready y1m_ready y1T_made y1T_copied hid_made hid_ready ff_made y2_ready
        y2n_ready y2g_ready x1b_ready y3_ready o_ready neg0 f2s_ready x0n_ready""".split()
        S = {name: sem(name) for name in names}
        stored = sem("stored")
        bn_done = [sem(f"bn_done{i}") for i in range(4)]
        mv_done = [sem(f"mv_done{i}") for i in range(4)]
        var_done = [sem(f"var_done{i}") for i in range(4)]
        rstd_done = [sem(f"rstd_done{i}") for i in range(4)]
        x1_ready = sem("x1_ready")

        def done(eng, name, n, per=1, k=None):
            eng.wait_ge(S[name], n * per + (per if k is None else k))

        def free(eng, name, n, per=1, k=None, back=1):
            if isinstance(n, int) and n < back:
                return
            eng.wait_ge(S[name], (n - back) * per + (per if k is None else k))

        def done_apart(eng, semaphore, value):
            eng.wait_ge(semaphore, value)
            eng.sem_inc(waits_passed, 1)

        block = ctx.enter_context(nc.Block())

        def bc(ap, shape):
            return ap.to_broadcast(shape)

        weights = [(W1[:, :], mlp1_w), (b1c[:, 0:1], mlp1_b[0:P].rearrange("(p o) -> p o", o=1)),
                   (b1c[:, 1:2], mlp1_b[P:H].rearrange("(p o) -> p o", o=1)),
                   (Wfc[:, :, 2:2 + H], W_fc.rearrange("(k p) n -> p k n", p=P)),
                   (W2[:, :, :], mlp2_w.rearrange("(k p) n -> p k n", p=P)),
                   (b2c[:, :], mlp2_b.rearrange("(p o) -> p o", o=1)),
                   (Wh[:, 2:2 + C], W_hand),
                   (a_fc_b[:, :], a_fc.rearrange("a o -> o a").broadcast_to((P, 2 * H))),
                   (a_hand_b[:, :], a_hand.rearrange("a o -> o a").broadcast_to((P, 2 * C))),
                   (Wqkv[:, :], w_qkv), (M1[:, :], w1), (M2[:, :], w2),
                   (m1c[:, :], b1.rearrange("(p o) -> p o", o=1))]
        for dst, src in ((g1_b, ln1_g), (be1_b, ln1_b), (g2_b, ln2_g), (be2_b, ln2_b), (m2_b, b2)):
            weights.append((dst[:, :], src.rearrange("(o n) -> o n", o=1).broadcast_to((P, C))))
        PREP = 4 * HC + 4 + 3 + T + T + 1
        W_ALL = 16 * (len(weights) + 1)

        @block.sync
        def _(sp):
            def load_x(n, par):
                free(sp, "y0_ready", n, back=2)
                free(sp, "xT_made", n, back=2)
                sp.dma_start(x_nat[par][:, :, :], x_dram[bass.ds(n, 1), :, :, :].rearrange("o p t c -> (o p) t c")
                             ).then_inc(x_loaded[par], 16)

            def stack_qk(n, par):
                done(sp, "high_ready", n, 2)
                done(sp, "mid_ready", n, 2)
                done(sp, "low_ready", n, 2)
                for i in range(2):
                    sp.dma_start(split_dram[par, i].rearrange("s h d n -> (h d) s n"),
                                 qk_parts[:, i, :, :]).then_inc(S["parts_stored"], 16)
                done(sp, "parts_stored", n, 32)
                free(sp, "scores_made", n, 16, back=2)
                for i, (dst, terms) in enumerate(((Qs[par], Q_TERMS), (Ks[par], K_TERMS))):
                    for r, part in enumerate(terms):
                        sp.dma_start(dst[r * D:(r + 1) * D, :, :],
                                     split_dram[par, i, part].rearrange("h d n -> d h n")
                                     ).then_inc(S["stacked"], 16)

            def store_out(n):
                done(sp, "o_ready", n)
                sp.dma_start(out_dram[bass.ds(n, 1), :, :, :].rearrange("o p t c -> (o p) t c"),
                             o_nat[:, :, :]).then_inc(stored, 16)

            sp.dma_start(adj_i[:, :, :], adj.rearrange("(p t) j -> p t j", t=T)).then_inc(w_loaded, 16)
            for dst, src in weights:
                sp.dma_start(dst, src).then_inc(w_loaded, 16)

            def batch(n, par):
                load_x(n, par)
                stack_qk(n, par)
                store_out(n)

            for n in range(2):
                batch(n, n)
            with sp.Fori(1, B // 2) as pair:
                for par in range(2):
                    batch(2 * pair + par, par)
            sp.wait_ge(stored, 16 * B)

        @block.gpsimd
        def _(pool):
            nc.gpsimd.memset(ident[:, :], 0.0).then_inc(const_set, 1)
            nc.gpsimd.memset(ones[:, :], 1.0).then_inc(const_set, 1)
            nc.gpsimd.memset(minus_half[:, :], -0.5).then_inc(const_set, 1)
            nc.gpsimd.memset(h1[:, :, 2 + H:], 1.0).then_inc(const_set, 1)
            nc.gpsimd.memset(h2[:, :, 2 + C:], 1.0).then_inc(const_set, 1)
            for i in range(2):
                nc.gpsimd.memset(v[i][:, :, :, :, :], 0.0).then_inc(const_set, 1)
            pool.wait_ge(const_set, 7)
            nc.gpsimd.affine_select(out=ident[:, :], in_=ident[:, :], compare_op=ALU.not_equal, fill=1.0,
                                    base=0, pattern=[[-1, P]], channel_multiplier=1).then_inc(const_set, 1)
            for i in range(2):
                nc.gpsimd.memset(v[i][:, :, :, :, D:D + 1], 1.0).then_inc(const_set, 1)
            pool.wait_ge(const_set, 10)
            pool.wait_ge(w_loaded, W_ALL)

            def finish_gat1(n):
                done(pool, "pos1_ready", n, T)
                done(pool, "w1_ready", n)
                nc.gpsimd.tensor_tensor(pos1[:, :, :], pos1[:, :, :], neg1[:, :, :], ALU.add
                                        ).then_inc(S["gat1_ready"], 1)

            def sum_h2(n):
                done(pool, "h2_copied", n, 2)
                free(pool, "gat2_made", n, 2)
                for i in range(2):
                    nc.gpsimd.tensor_tensor(h2sum[:, i, :], h2[:, i, 2:], h2[:, i + 2, 2:], ALU.add
                                            ).then_inc(S["h2sum_ready"], 1)
                done(pool, "h2sum_ready", n, 3, 2)
                nc.gpsimd.tensor_tensor(h2sum[:, 0, :], h2sum[:, 0, :], h2sum[:, 1, :], ALU.add
                                        ).then_inc(S["h2sum_ready"], 1)

            def inverse_deviation(n, i):
                if not isinstance(n, int) or n:
                    pool.wait_ge(rstd_done[i], n)
                done_apart(pool, mv_done[i], n * T + T)
                nc.gpsimd.tensor_scalar(var[i][:, :], mv[i][:, :, 1], EPS, None, ALU.add
                                        ).then_inc(var_done[i], 1)
                pool.wait_ge(var_done[i], n + 1)
                nc.gpsimd.tensor_tensor(rstd[i][:, :], var[i][:, :], minus_half[:, :], ALU.pow
                                        ).then_inc(rstd_done[i], 1)

            def split_qk(n, i):
                done_apart(pool, S["rest_ready"], 2 * n + i + 1)
                nc.gpsimd.tensor_copy(qk_parts[:, i, 1, :], qk_rest[:, i, :]).then_inc(S["mid_ready"], 1)
                done(pool, "mid_ready", n, 2, i + 1)
                nc.gpsimd.tensor_tensor(qk_parts[:, i, 2, :], qk_rest[:, i, :], qk_parts[:, i, 1, :],
                                        ALU.subtract).then_inc(S["low_ready"], 1)

            def sum_v(n, par):
                done(pool, "v_copied", n, 1)
                free(pool, "vcol_made", n)
                flat = v[par][:, :, :, :, :].rearrange("p t g h s -> p t (g h s)")
                for i in range(2):
                    nc.gpsimd.tensor_tensor(vsum[:, i, :], flat[:, i, :], flat[:, i + 2, :], ALU.add
                                            ).then_inc(S["vsum_ready"], 1)
                done(pool, "vsum_ready", n, 3, 2)
                nc.gpsimd.tensor_tensor(vsum[:, 0, :], vsum[:, 0, :], vsum[:, 1, :], ALU.add
                                        ).then_inc(S["vsum_ready"], 1)

            def over_tiles(row):
                return row[:, :].unsqueeze(1).to_broadcast([P, T, C])

            def residual1(n, par):
                done(pool, "attn_ready", n, 2)
                nc.gpsimd.tensor_tensor(attn[:, :, :], attn[:, :, :], x1[par][:, :, :], ALU.add
                                        ).then_inc(S["y1_ready"], 1)

            def affine1(n):
                done(pool, "y1n_ready", n)
                nc.gpsimd.tensor_tensor(y1n[:, :, :], y1n[:, :, :], over_tiles(g1_b), ALU.mult
                                        ).then_inc(S["y1g_ready"], 1)
                done(pool, "y1g_ready", n)
                nc.gpsimd.tensor_tensor(y1n[:, :, :], y1n[:, :, :], over_tiles(be1_b), ALU.add
                                        ).then_inc(S["y1b_ready"], 1)
                done(pool, "y1b_ready", n)
                free(pool, "y2_ready", n)
                nc.gpsimd.tensor_tensor(y1m[:, :, :], y1n[:, :, :], over_tiles(m2_b), ALU.add
                                        ).then_inc(S["y1m_ready"], 1)

            def affine2(n, par):
                free(pool, "y3_ready", n)
                nc.gpsimd.tensor_tensor(x1b[:, :, :], x1[par][:, :, :], over_tiles(be2_b), ALU.add
                                        ).then_inc(S["x1b_ready"], 1)
                done(pool, "y2n_ready", n)
                nc.gpsimd.tensor_tensor(y2n[:, :, :], y2n[:, :, :], over_tiles(g2_b), ALU.mult
                                        ).then_inc(S["y2g_ready"], 1)

            def batch(n, par):
                finish_gat1(n)
                sum_h2(n)
                inverse_deviation(n, 0)
                for i in range(2):
                    split_qk(n, i)
                sum_v(n, par)
                residual1(n, par)
                inverse_deviation(n, 1)
                affine1(n)
                inverse_deviation(n, 2)
                affine2(n, par)
                inverse_deviation(n, 3)

            for n in range(2):
                batch(n, n)
            with pool.Fori(1, B // 2) as pair:
                for par in range(2):
                    batch(2 * pair + par, par)

        @block.scalar
        def _(act):
            act.wait_ge(w_loaded, W_ALL)

            def copy_xT(n):
                done(act, "xT_made", n)
                free(act, "out1_made", n, HC)
                nc.scalar.copy(xT[:, :], s0[:, :]).then_inc(S["xT_copied"], 1)

            def relu_out1(n):
                for f in range(HC):
                    done(act, "out1_made", n, HC, f + 1)
                    if f == 0:
                        free(act, "out2_made", n)
                    nc.scalar.activation(out1[:, f, :], bank[1 + f][:, :], ACT.Relu, bias=b1c[:, f:f + 1]
                                         ).then_inc(S["out1_ready"], 1)

            def copy_h1(n, t):
                done(act, "h1_made", n, T, t + 1)
                if t == 0:
                    free(act, "gat1_made", n, T)
                nc.scalar.copy(h1[:, t, 0:2 + H], bank[t % 3][:, 0:2 + H]).then_inc(S["h1_copied"], 1)

            def factors1(n):
                done(act, "arg1_ready", n, 4)
                free(act, "rows1_made", n, 2)
                free(act, "att1_ready", n, T)
                nc.scalar.activation(fac1[:, :, :], arg1[:, :, :], ACT.Exp).then_inc(S["fac1_ready"], 1)

            def low_branch1(n):
                done(act, "rows1_made", n, 2)
                for j in range(T):
                    nc.scalar.activation(low[:, j, :], s0[:, :], ACT.Copy, scale=fac1[:, 3, j:j + 1]
                                         ).then_inc(S["low1_ready"], 1)

            def elu_twice1(n):
                done(act, "pos1_ready", n, T)
                nc.scalar.activation(neg1[:, :, :], neg1[:, :, :], ACT.Exp).then_inc(S["u1_ready"], 1)
                done(act, "u1_ready", n)
                nc.scalar.activation(neg1[:, :, :], neg1[:, :, :], ACT.Exp, bias=minus_one[:, 0:1]
                                     ).then_inc(S["w1_ready"], 1)

            def relu_out2(n):
                done(act, "out2_made", n)
                free(act, "out2T_made", n)
                nc.scalar.activation(out2[:, :], s1[:, :], ACT.Relu, bias=b2c[:, 0:1]
                                     ).then_inc(S["out2_ready"], 1)

            def low_branch2(n):
                done(act, "rows2_made", n, 2)
                for j in range(T):
                    nc.scalar.activation(low[:, j, :], s2p[:, :], ACT.Identity, bias=f2s[:, j:j + 1]
                                         ).then_inc(S["low2_ready"], 1)

            def exp_att2(n):
                done(act, "argm_ready", n)
                free(act, "gat2_made", n, 2)
                nc.scalar.activation(att[:, :, :], low[:, :, :], ACT.Exp).then_inc(S["att2_ready"], 1)

            def elu_twice2(n):
                done(act, "pos2_ready", n, T)
                nc.scalar.activation(neg2[:, :, :], neg2[:, :, :], ACT.Exp).then_inc(S["u2_ready"], 1)
                done(act, "u2_ready", n)
                nc.scalar.activation(neg2[:, :, :], neg2[:, :, :], ACT.Exp, bias=minus_one[:, 0:1]
                                     ).then_inc(S["w2_ready"], 1)

            def copy_x1T(n):
                done(act, "x1T_made", n)
                nc.scalar.copy(x1T[:, :], s1[:, :]).then_inc(S["x1T_copied"], 1)

            def high_parts(n):
                for i, (made, src) in enumerate((("q_made", s0), ("k_made", s2p))):
                    done(act, made, n)
                    free(act, "parts_stored", n, 32)
                    nc.scalar.copy(qk_parts[:, i, 0, :], src[:, :]).then_inc(S["high_ready"], 1)

            def copy_v(n, par):
                done(act, "v_made", n)
                free(act, "pv_made", n, 4, back=2)
                nc.scalar.copy(v[par][:, :, :, :, 0:D].rearrange("p t g h d -> p t (g h) d"),
                               s1[:, :].rearrange("p (t e d) -> p t e d", t=T, d=D)
                               ).then_inc(S["v_copied"], 1)

            def exp_scores(n, unit, s):
                k = unit * GH + s
                done(act, "masked_ready", n, 16, k + 1)
                if s == 0:
                    if unit >= 2:
                        done(act, "pv_made", n, 4, unit - 1)
                    else:
                        free(act, "pv_made", n, 4, unit + 3)
                nc.scalar.activation(probs[:, unit % 2, s, :, :], masked[:, k % 2, :, :], ACT.Exp,
                                     scale=SCALE).then_inc(S["probs_ready"], 1)

            def copy_y1T(n):
                done(act, "y1T_made", n)
                nc.scalar.copy(y1T[:, :], s1[:, :]).then_inc(S["y1T_copied"], 1)

            def relu_hid(n):
                done(act, "hid_made", n)
                nc.scalar.activation(hid[:, :], s0[:, :], ACT.Relu, bias=m1c[:, 0:1]
                                     ).then_inc(S["hid_ready"], 1)

            def batch(n, par):
                copy_xT(n)
                relu_out1(n)
                for t in range(T):
                    copy_h1(n, t)
                factors1(n)
                low_branch1(n)
                elu_twice1(n)
                relu_out2(n)
                low_branch2(n)
                exp_att2(n)
                elu_twice2(n)
                copy_x1T(n)
                high_parts(n)
                copy_v(n, par)
                for unit in range(4):
                    for s in range(GH):
                        exp_scores(n, unit, s)
                copy_y1T(n)
                relu_hid(n)

            act.wait_ge(minus_one_set, 1)
            for n in range(2):
                batch(n, n)
            with act.Fori(1, B // 2) as pair:
                for par in range(2):
                    batch(2 * pair + par, par)

        @block.vector
        def _(dve):
            nc.vector.memset(minus_one[:, :], -1.0).then_inc(minus_one_set, 1)
            dve.wait_ge(w_loaded, W_ALL)
            dve.wait_ge(const_set, 10)
            chain = [0]

            def link(ins):
                ins.then_inc(prep, 1)
                chain[0] += 1
                dve.wait_ge(prep, chain[0])

            for W, a, width, ks in ((Wfc, a_fc_b, H, range(HC)), (Wh, a_hand_b, C, (None,))):
                for k in ks:
                    Wk = W[:, :] if k is None else W[:, k, :]
                    for side in range(2):
                        link(nc.vector.tensor_tensor(wa_tmp[:, 0:width], Wk[:, 2:2 + width],
                                                     a[:, side * width:(side + 1) * width], ALU.mult))
                        link(nc.vector.tensor_reduce(Wk[:, side:side + 1],
                                                     wa_tmp[:, 0:width], AX_X, ALU.add))
            link(nc.vector.tensor_scalar(mask_nat[:, :, :],
                                         adj_i[:, :, :], 0.0, None, ALU.is_gt))
            link(nc.vector.tensor_reduce(row_count[:, :], mask_nat[:, :, :], AX_X, ALU.add))
            link(nc.vector.tensor_scalar(empty[:, :], row_count[:, :], 0.5, None, ALU.is_lt))
            for t in range(T):
                link(nc.vector.tensor_scalar(
                    neg_nat[:, t, :].rearrange("p (u q) -> p u q", u=T),
                    mask_nat[:, t, :].rearrange("p (q u) -> p u q", u=T), -NEG, NEG, ALU.mult, ALU.add))
            for k in range(T + 1):
                dve.wait_ge(adj_T, k + 1)
                dst = neg_T[:, k, :] if k < T else empty_b[:, :]
                nc.vector.tensor_copy(dst, bank[k % 3][:, :]).then_inc(prep, 1)
            chain[0] += T + 1
            assert chain[0] == PREP
            dve.wait_ge(prep, PREP)

            def arguments1(n):
                done(dve, "f1b_made", n)
                nc.vector.reduce_max(fmax1[:, :], s1[:, :], AX_X).then_inc(S["fmax1_ready"], 1)
                done(dve, "fmax1_ready", n)
                free(dve, "fac1_ready", n)
                nc.vector.tensor_scalar(arg1[:, 0, :], f1[:, :, 0], fmax1[:, 0:1], 1.0 - ALPHA,
                                        ALU.add, ALU.mult).then_inc(S["arg1_ready"], 1)
                nc.vector.tensor_scalar(arg1[:, 1, :], f1[:, :, 1], fmax1[:, 0:1], None,
                                        ALU.subtract).then_inc(S["arg1_ready"], 1)
                done(dve, "arg1_ready", n, 4, 2)
                nc.vector.tensor_scalar(arg1[:, 2, :], arg1[:, 0, :], -1.0, 0.0, ALU.mult, ALU.min
                                        ).then_inc(S["arg1_ready"], 1)
                nc.vector.tensor_scalar(arg1[:, 3, :], arg1[:, 1, :], ALPHA, None, ALU.mult
                                        ).then_inc(S["neg0"], 1)
                done(dve, "neg0", n)
                done(dve, "arg1_ready", n, 4, 3)
                nc.vector.tensor_scalar(arg1[:, 0, :], arg1[:, 0, :], 0.0, None, ALU.min
                                        ).then_inc(S["arg1_ready"], 1)

            def weights1(n):
                done(dve, "rows1_made", n, 2)
                free(dve, "gat2_made", n, 2)
                for j in range(T):
                    done(dve, "low1_ready", n, T, j + 1)
                    nc.vector.scalar_tensor_tensor(att[:, j, :], s2p[:, :], fac1[:, 1, j:j + 1],
                                                   low[:, j, :], ALU.mult, ALU.max
                                                   ).then_inc(S["att1_ready"], 1)

            def normalise1(n, t):
                ps = bank[(1, 0, 2, 1)[t]]
                done(dve, "gat1_made", n, T, t + 1)
                nc.vector.reciprocal(rz1[:, t:t + 1], ps[:, H:H + 1]).then_inc(S["rz1_ready"], 1)
                done(dve, "rz1_ready", n, T, t + 1)
                if t == 0:
                    free(dve, "gat1T_made", n, HC)
                    free(dve, "gat1_ready", n)
                nc.vector.tensor_scalar(neg1[:, t, :], ps[:, 0:H], rz1[:, t:t + 1], 0.0, ALU.mult,
                                        ALU.min).then_inc(S["neg1_ready"], 1)
                done(dve, "neg1_ready", n, T, t + 1)
                nc.vector.scalar_tensor_tensor(pos1[:, t, :], ps[:, 0:H], rz1[:, t:t + 1],
                                               neg1[:, t, :], ALU.mult, ALU.subtract
                                               ).then_inc(S["pos1_ready"], 1)

            def residual0(n):
                for f in range(HC):
                    done(dve, "gat1T_made", n, HC, f + 1)
                    nc.vector.scalar_tensor_tensor(out1[:, f, :], (s0, s2p)[f][:, :], -1.0,
                                                   out1[:, f, :], ALU.add, ALU.add
                                                   ).then_inc(S["res1_ready"], 1)

            def copy_h2(n):
                for i in range(2):
                    done(dve, "h2_made", n, 2, i + 1)
                    src = (s0, s2p)[i][:, 0:2 * (C + 2)].rearrange("p (t c) -> p t c", t=2)
                    if i == 0:
                        free(dve, "gat2_made", n, 2)
                        free(dve, "h2sum_ready", n, 3)
                        free(dve, "f2b_made", n)
                        free(dve, "row2_ready", n, 2)
                    nc.vector.tensor_copy(h2[:, 2 * i:2 * i + 2, 0:2 + C], src
                                          ).then_inc(S["h2_copied"], 1)

            def rows2(n):
                free(dve, "rows2_made", n, 2)
                done_apart(dve, S["f2b_made"], n + 1)
                for t in range(T):
                    nc.vector.tensor_tensor_reduce(out=low[:, t, :], in0=s1[:, :], in1=neg_nat[:, t, :],
                                                   scale=1.0, scalar=3 * NEG, op0=ALU.add, op1=ALU.max,
                                                   accum_out=fmax2[:, t:t + 1]).then_inc(S["fmax2_ready"], 1)
                done(dve, "fmax2_ready", n, T)
                nc.vector.tensor_tensor(s2[:, :], f2[:, :, 0], fmax2[:, :], ALU.add).then_inc(S["s2_ready"], 1)
                done(dve, "s2_ready", n)
                nc.vector.scalar_tensor_tensor(m2[:, :], s2[:, :], ALPHA, s2[:, :], ALU.mult, ALU.max
                                               ).then_inc(S["m2_ready"], 1)
                free(dve, "low2_ready", n, T)
                nc.vector.tensor_scalar(f2s[:, :], f2[:, :, 1], ALPHA, None, ALU.mult
                                        ).then_inc(S["f2s_ready"], 1)
                done(dve, "m2_ready", n)
                nc.vector.tensor_tensor(row2[:, 0, :], f2[:, :, 0], m2[:, :], ALU.subtract
                                        ).then_inc(S["row2_ready"], 1)
                nc.vector.scalar_tensor_tensor(row2[:, 1, :], f2[:, :, 0], ALPHA, m2[:, :], ALU.mult,
                                               ALU.subtract).then_inc(S["row2_ready"], 1)

            def arguments2(n):
                done(dve, "rows2_made", n, 2)
                for j in range(T):
                    done(dve, "low2_ready", n, T, j + 1)
                    nc.vector.scalar_tensor_tensor(low[:, j, :], s0[:, :], f2[:, j, 1:2],
                                                   low[:, j, :], ALU.add, ALU.max
                                                   ).then_inc(S["arg2_ready"], 1)
                done(dve, "arg2_ready", n, T)
                nc.vector.tensor_tensor(low[:, :, :], low[:, :, :], neg_T[:, :, :], ALU.add
                                        ).then_inc(S["argm_ready"], 1)

            def normalise2(n):
                for i in range(2):
                    ps = (s1, s0)[i][:, 0:2 * (C + 1)].rearrange("p (t c) -> p t c", t=2)
                    done(dve, "gat2_made", n, 2, i + 1)
                    nc.vector.reciprocal(rz2[:, 2 * i:2 * i + 2], ps[:, :, C]).then_inc(S["rz2_ready"], 1)
                    done(dve, "rz2_ready", n, 2, i + 1)
                    if i == 0:
                        free(dve, "y0_ready", n)
                    for k in range(2):
                        t = 2 * i + k
                        nc.vector.tensor_scalar(neg2[:, t, :], ps[:, k, 0:C], rz2[:, t:t + 1], 0.0,
                                                ALU.mult, ALU.min).then_inc(S["neg2_ready"], 1)
                        done(dve, "neg2_ready", n, T, t + 1)
                        nc.vector.scalar_tensor_tensor(pos2[:, t, :], ps[:, k, 0:C], rz2[:, t:t + 1],
                                                       neg2[:, t, :], ALU.mult, ALU.subtract
                                                       ).then_inc(S["pos2_ready"], 1)

            def finish_gat2(n, par):
                done(dve, "pos2_ready", n, T)
                done(dve, "w2_ready", n)
                nc.vector.tensor_tensor(pos2[:, :, :], pos2[:, :, :], neg2[:, :, :], ALU.add
                                        ).then_inc(S["sum2_ready"], 1)
                done(dve, "sum2_ready", n)
                done(dve, "out2T_made", n)
                nc.vector.scalar_tensor_tensor(
                    pos2[:, :, :].rearrange("p t c -> p (t c)"), s2p[:, :], -1.0,
                    pos2[:, :, :].rearrange("p t c -> p (t c)"), ALU.add, ALU.add
                ).then_inc(S["sum2b_ready"], 1)
                done(dve, "sum2b_ready", n)
                dve.wait_ge(x_loaded[par], (n - par) * 8 + 16)
                free(dve, "x0n_ready", n)
                nc.vector.scalar_tensor_tensor(y0[:, :, :].rearrange("p t c -> p (t c)"),
                                               pos2[:, :, :].rearrange("p t c -> p (t c)"), 0.0,
                                               x_nat[par][:, :, :].rearrange("p t c -> p (t c)"),
                                               ALU.max, ALU.add).then_inc(S["y0_ready"], 1)

            def normalise(n, i, ready, src, dst, signal, waits):
                done(dve, ready, n)
                if not isinstance(n, int) or n:
                    dve.wait_ge(var_done[i], n)
                for t in range(T):
                    nc.vector.bn_stats(stat[i][:, t, :], src[:, t, :]).then_inc(bn_done[i], 1)
                for t in range(T):
                    done_apart(dve, bn_done[i], n * T + t + 1)
                    nc.vector.bn_aggr(mv[i][:, t, :], stat[i][:, t, :]).then_inc(mv_done[i], 1)
                dve.wait_ge(rstd_done[i], n + 1)
                waits()
                for t in range(T):
                    last = nc.vector.tensor_scalar(dst[:, t, :], src[:, t, :], mv[i][:, t, 0:1],
                                                   rstd[i][:, t:t + 1], ALU.subtract, ALU.mult)
                last.then_inc(S[signal], 1)

            def rests(n):
                for i, src in enumerate((s0, s2p)):
                    done(dve, "high_ready", n, 2, i + 1)
                    if i == 0:
                        free(dve, "low_ready", n, 2)
                    nc.vector.tensor_tensor(qk_rest[:, i, :], src[:, :], qk_parts[:, i, 0, :],
                                            ALU.subtract).then_inc(S["rest_ready"], 1)

            def copy_vcol(n, par):
                done(dve, "vcol_made", n)
                free(dve, "oT_ready", n, 2, back=2)
                nc.vector.tensor_copy(vcol[par][:, :], s1[:, 0:GROUPS]).then_inc(S["vcol_ready"], 1)

            def mask_scores(n, unit, s):
                k = unit * GH + s
                done(dve, "scores_made", n, 16, k + 1)
                if k >= 2:
                    done(dve, "probs_ready", n, 16, k - 1)
                else:
                    free(dve, "probs_ready", n, 16, k + 15)
                jp = unit % 2
                nc.vector.tensor_tensor(masked[:, k % 2, :, :], sc[k % 2][:, :, :],
                                        neg_T[:, 2 * jp:2 * jp + 2, :], ALU.add
                                        ).then_inc(S["masked_ready"], 1)

            def take_group(n, par, g):
                done(dve, "pv_made", n, 4, 2 * g + 2)
                done(dve, "vcol_ready", n)
                if g == 0:
                    free(dve, "oTT_made", n, 2)
                nc.vector.scalar_tensor_tensor(oT[:, g, :], empty_b[:, :], vcol[par][:, g:g + 1],
                                               oacc[:, :], ALU.mult, ALU.add).then_inc(S["oT_ready"], 1)

            def normalise_heads(n):
                for g in range(GROUPS):
                    ps = (s0, s2p)[g][:, :].rearrange("p (t h s) -> p t h s", t=T, s=STRIP)
                    done(dve, "oTT_made", n, 2, g + 1)
                    nc.vector.reciprocal(rzh[:, g, :, :], ps[:, :, :, D]).then_inc(S["rzh_ready"], 1)
                    done(dve, "rzh_ready", n, 2, g + 1)
                    nc.vector.tensor_tensor(
                        attn[:, :, g * GH * D:(g + 1) * GH * D].rearrange("p t (h d) -> p t h d", d=D),
                        ps[:, :, :, 0:D], rzh[:, g, :, :].unsqueeze(3).to_broadcast([P, T, GH, D]),
                        ALU.mult).then_inc(S["attn_ready"], 1)

            def residual2(n):
                done(dve, "ff_made", n)
                done(dve, "y1m_ready", n)
                free(dve, "y2n_ready", n)
                nc.vector.tensor_tensor(y2[:, :, :].rearrange("p t c -> p (t c)"), s2p[:, :],
                                        y1m[:, :, :].rearrange("p t c -> p (t c)"), ALU.add
                                        ).then_inc(S["y2_ready"], 1)

            def residual3(n):
                done(dve, "y2g_ready", n)
                done(dve, "x1b_ready", n)
                nc.vector.tensor_tensor(y2n[:, :, :], y2n[:, :, :], x1b[:, :, :], ALU.add
                                        ).then_inc(S["y3_ready"], 1)

            def wait_stored(n):
                if not isinstance(n, int) or n:
                    dve.wait_ge(stored, 16 * n)

            def batch(n, par):
                arguments1(n)
                weights1(n)
                for t in range(T):
                    normalise1(n, t)
                residual0(n)
                copy_h2(n)
                rows2(n)
                arguments2(n)
                normalise2(n)
                finish_gat2(n, par)
                normalise(n, 0, "y0_ready", y0, x1[par], "x0n_ready",
                          lambda: free(dve, "y3_ready", n, back=2))
                rests(n)
                copy_vcol(n, par)
                for unit in range(4):
                    for s in range(GH):
                        mask_scores(n, unit, s)
                    if unit == 2:
                        take_group(n, par, 0)
                take_group(n, par, 1)
                normalise_heads(n)
                normalise(n, 1, "y1_ready", attn, y1n, "y1n_ready", lambda: (free(dve, "y1T_made", n), free(dve, "y1m_ready", n)))
                residual2(n)
                normalise(n, 2, "y2_ready", y2, y2n, "y2n_ready", lambda: free(dve, "o_ready", n))
                residual3(n)
                normalise(n, 3, "y3_ready", y2n, o_nat, "o_ready", lambda: wait_stored(n))

            for n in range(2):
                batch(n, n)
            with dve.Fori(1, B // 2) as pair:
                for par in range(2):
                    batch(2 * pair + par, par)

        @block.tensor
        def _(pe):
            pe.wait_ge(const_set, 10)
            pe.wait_ge(prep, PREP - T - 1)
            for k in range(T + 1):
                if k >= 3:
                    pe.wait_ge(prep, PREP - T - 1 + k - 2)
                for t in range(T):
                    src = neg_nat[:, t, k * P:(k + 1) * P] if k < T else bc(empty[:, t:t + 1], [P, P])
                    last = nc.tensor.transpose(bank[k % 3][:, t * P:(t + 1) * P], src, ident[:, :])
                last.then_inc(adj_T, 1)
            pe.wait_ge(prep, PREP)

            def transpose_tiles(dst, src):
                for t in range(T):
                    last = nc.tensor.transpose(dst[:, t * P:(t + 1) * P], src(t), ident[:, :])
                return last

            def transpose_x(n, par):
                pe.wait_ge(x_loaded[par], (n - par) * 8 + 16)
                free(pe, "attn_ready", n, 2)
                free(pe, "hid_ready", n)
                transpose_tiles(s0, lambda t: x_nat[par][:, t, :]).then_inc(S["xT_made"], 1)

            def hidden1(n):
                done(pe, "xT_copied", n)
                for f in range(HC):
                    if f == 0:
                        free(pe, "y1T_copied", n)
                    else:
                        free(pe, "y2_ready", n)
                    nc.tensor.matmul(bank[1 + f][:, :], W1[:, f * P:(f + 1) * P], xT[:, :],
                                     start=True, stop=True).then_inc(S["out1_made"], 1)

            def project1(n):
                done(pe, "out1_ready", n, HC)
                for t in range(T):
                    if t == 3:
                        done(pe, "h1_copied", n, T, 1)
                    for k in range(HC):
                        last = nc.tensor.matmul(bank[t % 3][:, 0:H + 2], out1[:, k, t * P:(t + 1) * P],
                                                Wfc[:, k, :], start=(k == 0), stop=(k == HC - 1))
                    last.then_inc(S["h1_made"], 1)

            def rows_of_f1(n):
                done(pe, "h1_copied", n, T)
                transpose_tiles(s1, lambda t: bc(h1[:, t, 1:2], [P, P])).then_inc(S["f1b_made"], 1)
                done(pe, "fac1_ready", n)
                for i, dst in ((0, s2p), (2, s0)):
                    transpose_tiles(dst, lambda t: bc(fac1[:, i, t:t + 1], [P, P])
                                    ).then_inc(S["rows1_made"], 1)

            def attend1(n):
                done(pe, "att1_ready", n, T)
                for t in range(T):
                    if t == 3:
                        done(pe, "pos1_ready", n, T, 1)
                    for j in range(T):
                        last = nc.tensor.matmul(bank[(1, 0, 2, 1)[t]][:, 0:H + 1],
                                                att[:, j, t * P:(t + 1) * P], h1[:, j, 2:],
                                                start=(j == 0), stop=(j == T - 1))
                    last.then_inc(S["gat1_made"], 1)

            def transpose_gat1(n):
                done(pe, "gat1_ready", n)
                for f in range(HC):
                    transpose_tiles((s0, s2p)[f], lambda t: pos1[:, t, f * P:(f + 1) * P]
                                    ).then_inc(S["gat1T_made"], 1)

            def hidden2(n):
                done(pe, "res1_ready", n, HC)
                for k in range(HC):
                    last = nc.tensor.matmul(s1[:, :], W2[:, k, :], out1[:, k, :], start=(k == 0),
                                            stop=(k == HC - 1))
                last.then_inc(S["out2_made"], 1)

            def project2(n):
                done(pe, "out2_ready", n)
                for i in range(2):
                    for k in range(2):
                        t = 2 * i + k
                        last = nc.tensor.matmul((s0, s2p)[i][:, k * (C + 2):(k + 1) * (C + 2)],
                                                out2[:, t * P:(t + 1) * P], Wh[:, :], start=True, stop=True)
                    last.then_inc(S["h2_made"], 1)

            def rows_of_f2(n):
                done(pe, "h2_copied", n, 2)
                transpose_tiles(s1, lambda t: bc(h2[:, t, 1:2], [P, P])).then_inc(S["f2b_made"], 1)
                done(pe, "row2_ready", n, 2)
                for i, dst in ((0, s0), (1, s2p)):
                    transpose_tiles(dst, lambda t: bc(row2[:, i, t:t + 1], [P, P])
                                    ).then_inc(S["rows2_made"], 1)

            def attend2(n):
                done(pe, "att2_ready", n)
                done(pe, "h2sum_ready", n, 3)
                for i in range(2):
                    for k in range(2):
                        t = 2 * i + k
                        dst = (s1, s0)[i][:, k * (C + 1):(k + 1) * (C + 1)]
                        for j in range(T):
                            nc.tensor.matmul(dst, att[:, j, t * P:(t + 1) * P], h2[:, j, 2:],
                                             start=(j == 0), stop=False)
                        last = nc.tensor.matmul(dst, empty_b[:, t * P:(t + 1) * P], h2sum[:, 0, :],
                                                start=False, stop=True)
                    last.then_inc(S["gat2_made"], 1)
                transpose_tiles(s2p, lambda t: out2[:, t * P:(t + 1) * P]).then_inc(S["out2T_made"], 1)

            def project_qkv(n, par):
                done(pe, "x0n_ready", n)
                transpose_tiles(s1, lambda t: x1[par][:, t, :]).then_inc(S["x1T_made"], 1)
                done(pe, "x1T_copied", n)
                nc.tensor.matmul(s0[:, :], Wqkv[:, 0:C], x1T[:, :], start=True, stop=True
                                 ).then_inc(S["q_made"], 1)
                nc.tensor.matmul(s2p[:, :], Wqkv[:, C:2 * C], x1T[:, :], start=True, stop=True
                                 ).then_inc(S["k_made"], 1)
                for t in range(T):
                    last = nc.tensor.matmul(s1[:, t * P:(t + 1) * P], x1T[:, t * P:(t + 1) * P],
                                            Wqkv[:, 2 * C:3 * C], start=True, stop=True)
                last.then_inc(S["v_made"], 1)

            def columns_of_v(n):
                done(pe, "vsum_ready", n, 3)
                for g in range(GROUPS):
                    last = nc.tensor.matmul(s1[:, g:g + 1], vsum[:, 0, g * P:(g + 1) * P], ones[:, :],
                                            start=True, stop=True)
                last.then_inc(S["vcol_made"], 1)

            def scores(n, par, unit, s):
                k = unit * GH + s
                g, jp = unit // 2, unit % 2
                if k == 0:
                    done(pe, "stacked", n, 16 * 2 * len(Q_TERMS))
                if k >= 2:
                    done(pe, "masked_ready", n, 16, k - 1)
                else:
                    free(pe, "masked_ready", n, 16, k + 15)
                for i in range(2):
                    j = 2 * jp + i
                    last = nc.tensor.matmul(sc[k % 2][:, i, :], Ks[par][:, g * GH + s, j * P:(j + 1) * P],
                                            Qs[par][:, g * GH + s, :], start=True, stop=True)
                last.then_inc(S["scores_made"], 1)

            def attend_heads(n, par, unit):
                g, jp = unit // 2, unit % 2
                done(pe, "probs_ready", n, 16, unit * GH + GH)
                if jp == 0:
                    if g:
                        done(pe, "oT_ready", n, 2, 1)
                    else:
                        free(pe, "oT_ready", n, 2)
                for i in range(2):
                    for s in range(GH):
                        last = nc.tensor.matmul(oacc[s * STRIP:(s + 1) * STRIP, :],
                                                v[par][:, 2 * jp + i, g, s, :],
                                                probs[:, unit % 2, s, i, :],
                                                start=(jp == 0 and i == 0), stop=(jp == 1 and i == 1))
                last.then_inc(S["pv_made"], 1)

            def transpose_heads(n):
                for g in range(GROUPS):
                    done(pe, "oT_ready", n, 2, g + 1)
                    transpose_tiles((s0, s2p)[g], lambda t: oT[:, g, t * P:(t + 1) * P]
                                    ).then_inc(S["oTT_made"], 1)

            def feed_forward(n):
                done(pe, "y1b_ready", n)
                transpose_tiles(s1, lambda t: y1n[:, t, :]).then_inc(S["y1T_made"], 1)
                done(pe, "y1T_copied", n)
                nc.tensor.matmul(s0[:, :], M1[:, :], y1T[:, :], start=True, stop=True
                                 ).then_inc(S["hid_made"], 1)
                done(pe, "hid_ready", n)
                for t in range(T):
                    last = nc.tensor.matmul(s2p[:, t * P:(t + 1) * P], hid[:, t * P:(t + 1) * P],
                                            M2[:, :], start=True, stop=True)
                last.then_inc(S["ff_made"], 1)

            def batch(n, par):
                transpose_x(n, par)
                hidden1(n)
                project1(n)
                rows_of_f1(n)
                attend1(n)
                transpose_gat1(n)
                hidden2(n)
                project2(n)
                rows_of_f2(n)
                attend2(n)
                project_qkv(n, par)
                columns_of_v(n)
                for unit in range(4):
                    for s in range(GH):
                        scores(n, par, unit, s)
                    if unit:
                        attend_heads(n, par, unit - 1)
                attend_heads(n, par, 3)
                transpose_heads(n)
                feed_forward(n)

            for n in range(2):
                batch(n, n)
            with pe.Fori(1, B // 2) as pair:
                for par in range(2):
                    batch(2 * pair + par, par)


_INS = ["x", "adj", "L0_gnn_mlp1_w", "L0_gnn_mlp1_b", "L0_gnn_mlp2_w", "L0_gnn_mlp2_b", "L0_gnn_W_fc",
        "L0_gnn_a_fc", "L0_gnn_W_hand", "L0_gnn_a_hand", "L1_gnn_w_qkv", "L1_gnn_ln1_g", "L1_gnn_ln1_b",
        "L1_gnn_ln2_g", "L1_gnn_ln2_b", "L1_gnn_w1", "L1_gnn_b1", "L1_gnn_w2", "L1_gnn_b2"]


def kernel(**inputs):
    import numpy as _np
    import concourse.bacc as _bacc
    from concourse.bass_utils import run_bass_kernel_spmd as _run

    nc = _bacc.Bacc("TRN2", target_bir_lowering=False, num_devices=1)
    arrays, args = {}, []
    for name in _INS:
        a = _np.ascontiguousarray(inputs[name])
        arrays[f"in_{name}_dram"] = a
        args.append(nc.dram_tensor(f"in_{name}_dram", a.shape, mybir.dt.from_np(a.dtype),
                                   kind="ExternalInput").ap())
    out = nc.dram_tensor("out_dram", (B, N, C), F32, kind="ExternalOutput").ap()
    gnn_kernel(nc, *args, out)
    r = _run(nc, [arrays], core_ids=[0])
    return r.results[0]["out_dram"]
```

```python
from contextlib import ExitStack

import concourse.bass as bass
from concourse import mybir

P = 128
B, N, C = 16, 512, 128
T = N // P
H = 256
HC = H // P
HEADS, D = 8, 16
GROUPS, GH = 2, 4
STRIP = 32
ALPHA = 0.2
EPS = 1e-5
SCALE = D ** -0.5
NEG = -2.0 ** 100
Q_TERMS = (0, 1, 2, 0, 1, 0)
K_TERMS = (0, 0, 0, 1, 1, 2)
KS = len(Q_TERMS) * D

PE_MASKED = (1, 3, 4, 6, 7, 9, 11, 12, 14, 15)
DVE_MASKED = tuple(k for k in range(16) if k not in PE_MASKED)
MASKED_BY_DVE = len(DVE_MASKED)
SIDE = {
    "xT": (2, 1), "out1_0": (2, 2), "out1_1": (1, 2), "h1_0": (1, 2), "h1_1": (2, 0), "h1_2": (1,
    2), "h1_3": (1, 2), "f1_rows": (1, 2), "C_rows": (1, 2), "A_rows": (0, 1), "gat1_0": (0, 0),
    "gat1_1": (2, 1), "gat1_2": (1, 2), "gat1_3": (2, 1), "gat1T_0": (2, 2), "gat1T_1": (0, 2),
    "out2": (2, 1), "h2_0": (2, 1), "h2_1": (0, 1), "f2_rows": (0, 1), "R1_rows": (0, 2), "R2_rows":
    (2, 1), "gat2_0": (0, 0), "gat2_1": (1, 1), "out2T": (0, 1), "oT_0": (0, 2), "x1T": (1, 0),
    "oT_1": (2, 1), "q": (1, 0), "k": (2, 2), "v": (1, 2), "y1T": (0, 1), "vcol": (1, 2), "hid": (0,
    1), "ff": (0, 1),
}


INTERLEAVED = ("x_loaded", "parts_stored", "stacked", "stored", "gat1_made", "neg1_ready", "pos1_ready",
               "rz1_ready")


def masked_so_far(k):
    return sum(j <= k for j in DVE_MASKED)


ALU = mybir.AluOpType
ACT = mybir.ActivationFunctionType
F32 = mybir.dt.float32
BF16 = mybir.dt.bfloat16
I32 = mybir.dt.int32
AX_X = mybir.AxisListType.X


def gnn_kernel(nc, x, adj, mlp1_w, mlp1_b, mlp2_w, mlp2_b, W_fc, a_fc, W_hand, a_hand,
               w_qkv, ln1_g, ln1_b, ln2_g, ln2_b, w1, b1, w2, b2, out):
    x_dram = x.rearrange("b (p t) c -> b p t c", t=T)
    out_dram = out.rearrange("b (p t) c -> b p t c", t=T)
    split_dram = nc.dram_tensor("qk_split_dram", (2, 2, 3, HEADS, D, N), BF16).ap()

    with ExitStack() as ctx:
        def sb(name, shape, dt=F32):
            return ctx.enter_context(nc.sbuf_tensor(name, shape, dt))

        def psum(name, shape, dt=F32):
            return ctx.enter_context(nc.psum_tensor(name, shape, dt))

        def sem(name):
            return ctx.enter_context(nc.semaphore(name))

        def pair(name, shape, dt=F32):
            return [sb(f"{name}_{p}", shape, dt) for p in range(2)]

        ident = sb("ident", [P, P])
        ident_bf = sb("ident_bf", [P, P], BF16)
        ones = sb("ones", [P, 1])
        minus_half = sb("minus_half", [P, T])
        minus_one = sb("minus_one", [P, 1])
        zero_b = sb("zero_b", [P, T, C])
        neg_nat = sb("neg_nat", [P, T, N], BF16)
        neg_T = sb("neg_T", [P, T, N], BF16)
        row_count = sb("row_count", [P, T])
        occupied = sb("occupied", [P, T])
        empty = sb("empty", [P, T])
        empty_b = sb("empty_b", [P, N])
        W1 = sb("W1", [P, H])
        b1c = sb("b1c", [P, HC])
        Wfc = sb("Wfc", [P, HC, 2 + H])
        W2 = sb("W2", [P, HC, C])
        b2c = sb("b2c", [P, 1])
        Wh = sb("Wh", [P, 2 + C])
        Wqkv = sb("Wqkv", [P, 3 * C])
        M1 = sb("M1", [P, C])
        m1c = sb("m1c", [P, 1])
        M2 = sb("M2", [P, C])
        g1c = sb("g1c", [P, 1])
        be1c = sb("be1c", [P, 1])
        g1_b = sb("g1_b", [P, C])
        be1_b = sb("be1_b", [P, C])
        g2_b = sb("g2_b", [P, C])
        be2_b = sb("be2_b", [P, C])
        m2_b = sb("m2_b", [P, C])

        x_nat = pair("x_nat", [P, T, C])
        xT = pair("xT", [P, N])
        y0 = [xT[p][:, :].rearrange("p (t c) -> p t c", t=T) for p in range(2)]
        out1 = pair("out1", [P, HC, N])
        h1 = pair("h1", [P, T, 2 + H + 1])
        h2 = pair("h2", [P, T, 2 + C + 1])
        fmax1 = pair("fmax1", [P, 1])
        arg1 = pair("arg1", [P, 4, T])
        fac1 = pair("fac1", [P, 4, T])
        low = pair("low", [P, T, N])
        att = pair("att", [P, T, N])
        rz1 = pair("rz1", [P, T])
        neg1 = pair("neg1", [P, T, H])
        pos1 = pair("pos1", [P, T, H])
        out2 = pair("out2", [P, N])
        fmax2 = pair("fmax2", [P, T])
        s2 = pair("s2", [P, T])
        m2 = pair("m2", [P, T])
        row2 = pair("row2", [P, 2, T])
        f2s = pair("f2s", [P, T])
        rz2 = pair("rz2", [P, T])
        neg2 = [neg1[p][:, 0:2, :].rearrange("p a (b c) -> p (a b) c", c=C) for p in range(2)]
        pos2 = [pos1[p][:, 0:2, :].rearrange("p a (b c) -> p (a b) c", c=C) for p in range(2)]
        x1 = pair("x1", [P, T, C])
        x1T = out2
        qk_parts = [att[p][:, 0:3, :].bitcast(BF16).rearrange("p s (i n) -> p i s n", i=2) for p in range(2)]
        qk_rest = low
        Qs = pair("Qs", [KS, HEADS, N], BF16)
        Ks = pair("Ks", [KS, HEADS, N], BF16)
        v = pair("v", [P, T, GROUPS, GH, STRIP])
        vcol = pair("vcol", [P, GROUPS])
        probs = sb("probs", [P, 2, GH, 2, N])
        oT = sb("oT", [P, GROUPS, N])
        rzh = pair("rzh", [P, GROUPS, T, GH])
        attn = pair("attn", [P, T, C])
        y1n = pair("y1n", [P, T, C])
        xc = pair("xc", [P, T, C])
        y1T = pair("y1T", [P, N])
        hid = pair("hid", [P, N])
        stat = [pair(f"stat{i}", [P, T, 6]) for i in range(4)]
        mv = [pair(f"mv{i}", [P, T, 2]) for i in range(4)]
        var = [pair(f"var{i}", [P, T]) for i in range(4)]
        rstd = [pair(f"rstd{i}", [P, T]) for i in range(4)]
        neg_f32 = low[1]
        adj_i = low[0][:, :, :].bitcast(I32)
        mask_nat = att[0]
        a_fc_b = att[1][:, 0, :]
        a_hand_b = att[1][:, 1, 0:2 * C]
        wa_tmp = att[1][:, 2, 0:H]

        sc = [psum(f"sc{i}", [P, 2, N]) for i in range(2)]
        oacc = psum("oacc", [P, N])
        bank = [psum(f"side{i}", [P, N]) for i in range(3)]

        w_loaded = sem("w_loaded")
        const_set = sem("const_set")
        prep = sem("prep")
        adj_T = sem("adj_T")
        waits_passed = sem("waits_passed")
        minus_one_set = sem("minus_one_set")
        names = """x_loaded xT_made xT_copied out1_made out1_ready h1_made h1_copied f1b_made fmax1_ready
        arg1_ready fac1_ready rows1_made low1_ready att1_ready gat1_made rz1_ready neg1_ready
        pos1_ready u1_ready w1_ready gat1_ready gat1T_made res1_ready out2_made out2_ready h2_made h2_copied
        f2b_made fmax2_ready s2_ready row2_ready rows2_made low2_ready arg2_ready argm0_ready argm1_ready f2s_ready
        att2_ready gat2_made rz2_ready neg2_ready pos2_ready u2_ready w2_ready sum2_ready
        out2T_made sum2b_ready y0_ready x1_ready x1T_made x1T_copied q_made k_made v_made high_ready rest_ready
        mid_ready low_ready parts_stored stacked v_copied vcol_made vcol_ready
        scores_made masked_ready probs_ready pv_made oT_ready oTT_made rzh_ready attn_ready xc_ready y1_ready
        y1n_ready y1g_ready y1m_ready y1T_made y1T_copied hid_made hid_ready ff_made y2_ready
        y2n_ready y2g_ready x1b_ready y3_ready o_ready stored""".split()
        S = {name: [sem(f"{name}_{p}") for p in range(2)] if name in INTERLEAVED else [sem(name)] * 2
             for name in names}
        ln_step = [sem(f"ln{i}_step") for i in range(4)]
        ln_rstd = [sem(f"ln{i}_rstd") for i in range(4)]

        def passed(b, per, k):
            return (2 * b[0] + b[1]) * per + k

        def count(name, b, per=1, k=None):
            k = per if k is None else k
            return b[0] * per + k if name in INTERLEAVED else passed(b, per, k)

        def has_former(b):
            return not isinstance(b[0], int) or b[0] > 0

        def former(b):
            return (b[0] - 1, b[1])

        def probs_readers(b, unit):
            if unit >= 2:
                return [(S["pv_made"][b[1]], count("pv_made", b, 4, unit - 1))]
            if b[1]:
                return [(S["pv_made"][0], count("pv_made", (b[0], 0), 4, unit + 3))]
            if has_former(b):
                return [(S["pv_made"][1], count("pv_made", (b[0] - 1, 1), 4, unit + 3))]
            return []

        block = ctx.enter_context(nc.Block())

        def bc(ap, shape):
            return ap.to_broadcast(shape)

        def live(stage):
            return lambda b, *more: stage(b, *more) if b[2] else None

        def rounds(eng, one_round):
            for r in range(2):
                one_round([(r, p, True) for p in range(2)], [(r - 1, p, r > 0) for p in range(2)])
            with eng.Fori(2, B // 2) as r:
                one_round([(r, p, True) for p in range(2)], [(r - 1, p, True) for p in range(2)])
            one_round([(B // 2, p, False) for p in range(2)], [(B // 2 - 1, p, True) for p in range(2)])

        def row(ap):
            return ap.rearrange("(o n) -> o n", o=1).broadcast_to((P, C))

        def column(ap):
            return ap.rearrange("(p o) -> p o", o=1)

        weights = [(W1[:, :], mlp1_w), (b1c[:, 0:1], column(mlp1_b[0:P])), (b1c[:, 1:2], column(mlp1_b[P:H])),
                   (Wfc[:, :, 2:2 + H], W_fc.rearrange("(k p) n -> p k n", p=P)),
                   (W2[:, :, :], mlp2_w.rearrange("(k p) n -> p k n", p=P)), (b2c[:, :], column(mlp2_b)),
                   (Wh[:, 2:2 + C], W_hand),
                   (a_fc_b, a_fc.rearrange("a o -> o a").broadcast_to((P, 2 * H))),
                   (a_hand_b, a_hand.rearrange("a o -> o a").broadcast_to((P, 2 * C))),
                   (Wqkv[:, :], w_qkv), (M1[:, :], w1), (M2[:, :], w2), (m1c[:, :], column(b1)),
                   (g1c[:, :], column(ln1_g)), (be1c[:, :], column(ln1_b)),
                   (g1_b[:, :], row(ln1_g)), (be1_b[:, :], row(ln1_b)), (g2_b[:, :], row(ln2_g)),
                   (be2_b[:, :], row(ln2_b)), (m2_b[:, :], row(b2))]
        W_ALL = 16 * (len(weights) + 1)
        PREP = 4 * HC + 4 + 5 + 2 * T + 1 + T + 1
        PREP_T = PREP - T - 1

        def batch_of(ap, b):
            return ap[bass.ds(2 * b[0] + b[1], 1), :, :, :].rearrange("o p t c -> (o p) t c")

        @block.sync
        def _(sp):
            def load_x(r, p):
                if not isinstance(r, int) or r:
                    if has_former((r, p)):
                        sp.wait_ge(S["y0_ready"][p], count("y0_ready", former((r, p))))
                sp.dma_start(x_nat[p][:, :, :], batch_of(x_dram, (r, p))).then_inc(S["x_loaded"][p], 16)

            @live
            def stack_qk(a):
                p = a[1]
                sp.wait_ge(S["high_ready"][p], count("high_ready", a, 2))
                sp.wait_ge(S["mid_ready"][p], count("mid_ready", a, 2))
                sp.wait_ge(S["low_ready"][p], count("low_ready", a, 2))
                for i in range(2):
                    sp.dma_start(split_dram[p, i].rearrange("s h d n -> (h d) s n"),
                                 qk_parts[p][:, i, :, :]).then_inc(S["parts_stored"][p], 16)
                sp.wait_ge(S["parts_stored"][p], count("parts_stored", a, 32))
                if has_former(a):
                    sp.wait_ge(S["scores_made"][p], count("scores_made", former(a), 16))
                for i, (dst, terms) in enumerate(((Qs[p], Q_TERMS), (Ks[p], K_TERMS))):
                    for r, part in enumerate(terms):
                        sp.dma_start(dst[r * D:(r + 1) * D, :, :],
                                     split_dram[p, i, part].rearrange("h d n -> d h n")
                                     ).then_inc(S["stacked"][p], 16)

            @live
            def store_out(b):
                sp.wait_ge(S["o_ready"][p], count("o_ready", b, 2))
                sp.dma_start(batch_of(out_dram, b), y1n[b[1]][:, :, :]).then_inc(S["stored"][b[1]], 16)

            sp.dma_start(adj_i, adj.rearrange("(p t) j -> p t j", t=T)).then_inc(w_loaded, 16)
            for dst, src in weights:
                sp.dma_start(dst, src).then_inc(w_loaded, 16)
            for p in range(2):
                load_x(0, p)

            def one_round(a, b, last_load=False):
                for p in range(2):
                    if a[p][2] and not last_load:
                        load_x(a[p][0] + 1, p)
                for p in range(2):
                    stack_qk(a[p])
                for p in range(2):
                    store_out(b[p])

            for r in range(2):
                one_round([(r, p, True) for p in range(2)], [(r - 1, p, r > 0) for p in range(2)])
            with sp.Fori(2, B // 2 - 1) as r:
                one_round([(r, p, True) for p in range(2)], [(r - 1, p, True) for p in range(2)])
            r = B // 2 - 1
            one_round([(r, p, True) for p in range(2)], [(r - 1, p, True) for p in range(2)], True)
            one_round([(r + 1, p, False) for p in range(2)], [(r, p, True) for p in range(2)])
            for p in range(2):
                sp.wait_ge(S["stored"][p], 16 * (B // 2))

        @block.gpsimd
        def _(pool):
            nc.gpsimd.memset(ident[:, :], 0.0).then_inc(const_set, 1)
            nc.gpsimd.memset(ones[:, :], 1.0).then_inc(const_set, 1)
            nc.gpsimd.memset(minus_half[:, :], -0.5).then_inc(const_set, 1)
            for p in range(2):
                nc.gpsimd.memset(h1[p][:, :, 2 + H:], 1.0).then_inc(const_set, 1)
                nc.gpsimd.memset(h2[p][:, :, 2 + C:], 1.0).then_inc(const_set, 1)
                nc.gpsimd.memset(v[p][:, :, :, :, :], 0.0).then_inc(const_set, 1)
            pool.wait_ge(const_set, 9)
            nc.gpsimd.affine_select(out=ident[:, :], in_=ident[:, :], compare_op=ALU.not_equal, fill=1.0,
                                    base=0, pattern=[[-1, P]], channel_multiplier=1).then_inc(const_set, 1)
            for p in range(2):
                nc.gpsimd.memset(v[p][:, :, :, :, D:D + 1], 1.0).then_inc(const_set, 1)
            pool.wait_ge(const_set, 12)
            nc.gpsimd.tensor_copy(ident_bf[:, :], ident[:, :]).then_inc(const_set, 1)
            pool.wait_ge(w_loaded, W_ALL)
            pool.wait_ge(prep, PREP)

            @live
            def finish_gat1(a, h):
                p = a[1]
                pool.wait_ge(S["w1_ready"][p], count("w1_ready", a, 2, h + 1))
                nc.gpsimd.tensor_tensor(pos1[p][:, 2 * h:2 * h + 2, :], pos1[p][:, 2 * h:2 * h + 2, :],
                                        neg1[p][:, 2 * h:2 * h + 2, :], ALU.add
                                        ).then_inc(S["gat1_ready"][p], 1)

            @live
            def mask_arguments2(a):
                p = a[1]
                pool.wait_ge(S["arg2_ready"][p], count("arg2_ready", a, T, 2))
                nc.gpsimd.tensor_tensor(low[p][:, 0:2, :], low[p][:, 0:2, :], neg_T[:, 0:2, :], ALU.add
                                        ).then_inc(S["argm0_ready"][p], 1)

            @live
            def inverse_deviation(b, i):
                p = b[1]
                pool.wait_ge(ln_step[i], passed(b, 2 * T, 2 * T))
                pool.sem_inc(waits_passed, 1)
                nc.gpsimd.tensor_scalar(var[i][p][:, :], mv[i][p][:, :, 1], EPS, None, ALU.add
                                        ).then_inc(ln_rstd[i], 1)
                pool.wait_ge(ln_rstd[i], passed(b, 2, 1))
                nc.gpsimd.tensor_tensor(rstd[i][p][:, :], var[i][p][:, :], minus_half[:, :], ALU.pow
                                        ).then_inc(ln_rstd[i], 1)

            @live
            def low_part(a, i):
                p = a[1]
                pool.wait_ge(S["mid_ready"][p], count("mid_ready", a, 2, i + 1))
                nc.gpsimd.tensor_tensor(qk_parts[p][:, i, 2, :], qk_rest[p][:, i, :],
                                        qk_parts[p][:, i, 1, :], ALU.subtract
                                        ).then_inc(S["low_ready"][p], 1)

            def over_tiles(row):
                return row[:, :].unsqueeze(1).to_broadcast([P, T, C])

            @live
            def keep_x1(b):
                p = b[1]
                pool.wait_ge(S["x1_ready"][p], count("x1_ready", b, 2))
                if has_former(b):
                    pool.wait_ge(S["y3_ready"][p], count("y3_ready", former(b)))
                nc.gpsimd.tensor_tensor(xc[p][:, :, :], x1[p][:, :, :], zero_b[:, :, :], ALU.add
                                        ).then_inc(S["xc_ready"][p], 1)

            @live
            def add_bias2(b):
                p = b[1]
                pool.wait_ge(S["y1_ready"][p], count("y1_ready", b))
                nc.gpsimd.tensor_tensor(xc[p][:, :, :], xc[p][:, :, :], over_tiles(be2_b), ALU.add
                                        ).then_inc(S["x1b_ready"][p], 1)

            @live
            def affine1(b, step):
                p = b[1]
                if step == 0:
                    pool.wait_ge(S["y1T_made"][p], count("y1T_made", b))
                    nc.gpsimd.tensor_tensor(y1n[p][:, :, :], y1n[p][:, :, :], over_tiles(g1_b), ALU.mult
                                            ).then_inc(S["y1g_ready"][p], 1)
                else:
                    pool.wait_ge(S["y1g_ready"][p], count("y1g_ready", b))
                    nc.gpsimd.tensor_tensor(y1n[p][:, :, :], y1n[p][:, :, :], over_tiles(be1_b), ALU.add
                                            ).then_inc(S["y1m_ready"][p], 1)

            @live
            def affine2(b):
                p = b[1]
                pool.wait_ge(S["y2n_ready"][p], count("y2n_ready", b, 2))
                nc.gpsimd.tensor_tensor(attn[p][:, :, :], attn[p][:, :, :], over_tiles(g2_b), ALU.mult
                                        ).then_inc(S["y2g_ready"][p], 1)

            def one_round(a, b):
                a0, a1 = a
                b0, b1 = b
                keep_x1(b0)
                keep_x1(b1)
                finish_gat1(a0, 0)
                finish_gat1(a0, 1)
                finish_gat1(a1, 0)
                finish_gat1(a1, 1)
                mask_arguments2(a0)
                mask_arguments2(a1)
                inverse_deviation(a0, 0)
                inverse_deviation(a1, 0)
                low_part(a0, 0)
                low_part(a0, 1)
                inverse_deviation(b0, 1)
                add_bias2(b0)
                affine1(b0, 0)
                low_part(a1, 0)
                low_part(a1, 1)
                inverse_deviation(b1, 1)
                affine1(b0, 1)
                affine1(b1, 0)
                inverse_deviation(b0, 2)
                affine1(b1, 1)
                affine2(b0)
                add_bias2(b1)
                inverse_deviation(b1, 2)
                inverse_deviation(b0, 3)
                affine2(b1)
                inverse_deviation(b1, 3)
            rounds(pool, one_round)

        @block.scalar
        def _(act):
            act.wait_ge(w_loaded, W_ALL)
            act.wait_ge(minus_one_set, 1)
            act.wait_ge(prep, PREP)

            @live
            def copy_xT(a):
                p = a[1]
                act.wait_ge(S["xT_made"][p], count("xT_made", a))
                if has_former(a):
                    act.wait_ge(S["x1_ready"][p], count("x1_ready", former(a), 2))
                nc.scalar.copy(xT[p][:, :], bank[SIDE["xT"][p]][:, :]).then_inc(S["xT_copied"][p], 1)

            @live
            def relu_out1(a, f):
                p = a[1]
                act.wait_ge(S["out1_made"][p], count("out1_made", a, HC, f + 1))
                if has_former(a):
                    act.wait_ge(S["out2_made"][p], count("out2_made", former(a)))
                nc.scalar.activation(out1[p][:, f, :], bank[SIDE[f"out1_{f}"][p]][:, :], ACT.Relu,
                                     bias=b1c[:, f:f + 1]).then_inc(S["out1_ready"][p], 1)

            @live
            def copy_h1(a, t):
                p = a[1]
                act.wait_ge(S["h1_made"][p], count("h1_made", a, T, t + 1))
                if has_former(a):
                    act.wait_ge(S["gat1_made"][p], count("gat1_made", former(a), T))
                nc.scalar.copy(h1[p][:, t, 0:2 + H], bank[SIDE[f"h1_{t}"][p]][:, 0:2 + H]
                               ).then_inc(S["h1_copied"][p], 1)

            @live
            def factors1(a):
                p = a[1]
                act.wait_ge(S["arg1_ready"][p], count("arg1_ready", a, 5))
                nc.scalar.activation(fac1[p][:, :, :], arg1[p][:, :, :], ACT.Exp).then_inc(S["fac1_ready"][p], 1)

            @live
            def low_branch1(a, j):
                p = a[1]
                act.wait_ge(S["rows1_made"][p], count("rows1_made", a, 2))
                if has_former(a):
                    act.wait_ge(S["low_ready"][p], count("low_ready", former(a), 2))
                nc.scalar.activation(low[p][:, j, :], bank[SIDE["C_rows"][p]][:, :], ACT.Copy,
                                     scale=fac1[p][:, 3, j:j + 1]).then_inc(S["low1_ready"][p], 1)

            @live
            def elu_twice1(a, h, step):
                p = a[1]
                tiles = neg1[p][:, 2 * h:2 * h + 2, :]
                if step == 0:
                    act.wait_ge(S["pos1_ready"][p], count("pos1_ready", a, T, 2 * h + 2))
                    nc.scalar.activation(tiles, tiles, ACT.Exp).then_inc(S["u1_ready"][p], 1)
                else:
                    act.wait_ge(S["u1_ready"][p], count("u1_ready", a, 2, h + 1))
                    nc.scalar.activation(tiles, tiles, ACT.Exp, bias=minus_one[:, 0:1]
                                         ).then_inc(S["w1_ready"][p], 1)

            @live
            def relu_out2(a):
                p = a[1]
                act.wait_ge(S["out2_made"][p], count("out2_made", a))
                if has_former(a):
                    act.wait_ge(S["v_made"][p], count("v_made", former(a)))
                nc.scalar.activation(out2[p][:, :], bank[SIDE["out2"][p]][:, :], ACT.Relu, bias=b2c[:, 0:1]
                                     ).then_inc(S["out2_ready"][p], 1)

            @live
            def low_branch2(a, j):
                p = a[1]
                act.wait_ge(S["rows2_made"][p], count("rows2_made", a, 2))
                nc.scalar.activation(low[p][:, j, :], bank[SIDE["R2_rows"][p]][:, :], ACT.Identity,
                                     bias=f2s[p][:, j:j + 1]).then_inc(S["low2_ready"][p], 1)

            @live
            def exp_att2(a, h):
                p = a[1]
                act.wait_ge(S[f"argm{h}_ready"][p], count(f"argm{h}_ready", a))
                nc.scalar.activation(att[p][:, 2 * h:2 * h + 2, :], low[p][:, 2 * h:2 * h + 2, :], ACT.Exp
                                     ).then_inc(S["att2_ready"][p], 1)

            @live
            def elu_twice2(a, step):
                p = a[1]
                if step == 0:
                    act.wait_ge(S["pos2_ready"][p], count("pos2_ready", a, T))
                    nc.scalar.activation(neg2[p], neg2[p], ACT.Exp).then_inc(S["u2_ready"][p], 1)
                else:
                    act.wait_ge(S["u2_ready"][p], count("u2_ready", a))
                    nc.scalar.activation(neg2[p], neg2[p], ACT.Exp, bias=minus_one[:, 0:1]
                                         ).then_inc(S["w2_ready"][p], 1)

            @live
            def copy_x1T(a):
                p = a[1]
                act.wait_ge(S["x1T_made"][p], count("x1T_made", a))
                nc.scalar.copy(x1T[p][:, :], bank[SIDE["x1T"][p]][:, :]).then_inc(S["x1T_copied"][p], 1)

            @live
            def high_part(a, i):
                p = a[1]
                act.wait_ge(S[("q_made", "k_made")[i]][p], count(("q_made", "k_made")[i], a))
                nc.scalar.copy(qk_parts[p][:, i, 0, :], bank[SIDE["qk"[i]][p]][:, :]
                               ).then_inc(S["high_ready"][p], 1)

            @live
            def copy_v(a):
                p = a[1]
                act.wait_ge(S["v_made"][p], count("v_made", a))
                if has_former(a):
                    act.wait_ge(S["pv_made"][p], count("pv_made", former(a), 4))
                nc.scalar.copy(v[p][:, :, :, :, 0:D].rearrange("p t g h d -> p t (g h) d"),
                               bank[SIDE["v"][p]][:, :].rearrange("p (t e d) -> p t e d", t=T, d=D)
                               ).then_inc(S["v_copied"][p], 1)

            @live
            def exp_scores(b, k):
                p, unit, s = b[1], k // GH, k % GH
                if k in PE_MASKED:
                    act.wait_ge(S["scores_made"][p], count("scores_made", b, 16, k + 1))
                    src = sc[k % 2][:, :, :]
                else:
                    act.wait_ge(S["masked_ready"][p], count("masked_ready", b, MASKED_BY_DVE, masked_so_far(k)))
                    src = probs[:, unit % 2, s, :, :]
                if s == 0:
                    for made, value in probs_readers(b, unit):
                        act.wait_ge(made, value)
                nc.scalar.activation(probs[:, unit % 2, s, :, :], src, ACT.Exp,
                                     scale=SCALE).then_inc(S["probs_ready"][p], 1)

            @live
            def copy_y1T(b):
                p = b[1]
                act.wait_ge(S["y1T_made"][p], count("y1T_made", b))
                nc.scalar.activation(y1T[p][:, :], bank[SIDE["y1T"][p]][:, :], ACT.Identity,
                                     scale=g1c[:, 0:1], bias=be1c[:, 0:1]).then_inc(S["y1T_copied"][p], 1)

            @live
            def relu_hid(b):
                p = b[1]
                act.wait_ge(S["hid_made"][p], count("hid_made", b))
                nc.scalar.activation(hid[p][:, :], bank[SIDE["hid"][p]][:, :], ACT.Relu, bias=m1c[:, 0:1]
                                     ).then_inc(S["hid_ready"][p], 1)

            def one_round(a, b):
                a0, a1 = a
                b0, b1 = b
                copy_xT(a0)
                copy_xT(a1)
                relu_out1(a0, 0)
                relu_out1(a0, 1)
                relu_out1(a1, 0)
                copy_h1(a0, 0)
                copy_h1(a0, 1)
                copy_h1(a0, 2)
                relu_out1(a1, 1)
                copy_h1(a0, 3)
                copy_h1(a1, 0)
                copy_h1(a1, 1)
                factors1(a0)
                copy_h1(a1, 2)
                low_branch1(a0, 0)
                low_branch1(a0, 1)
                copy_h1(a1, 3)
                low_branch1(a0, 2)
                low_branch1(a0, 3)
                factors1(a1)
                low_branch1(a1, 0)
                low_branch1(a1, 1)
                low_branch1(a1, 2)
                low_branch1(a1, 3)
                elu_twice1(a0, 0, 0)
                elu_twice1(a0, 0, 1)
                exp_scores(b0, 0)
                exp_scores(b0, 1)
                elu_twice1(a0, 1, 0)
                elu_twice1(a0, 1, 1)
                elu_twice1(a1, 0, 0)
                exp_scores(b0, 2)
                exp_scores(b0, 3)
                exp_scores(b0, 4)
                elu_twice1(a1, 0, 1)
                exp_scores(b0, 5)
                elu_twice1(a1, 1, 0)
                exp_scores(b0, 6)
                elu_twice1(a1, 1, 1)
                exp_scores(b0, 7)
                relu_out2(a0)
                exp_scores(b0, 8)
                exp_scores(b0, 9)
                exp_scores(b0, 10)
                exp_scores(b0, 11)
                relu_out2(a1)
                exp_scores(b0, 12)
                exp_scores(b0, 13)
                exp_scores(b0, 14)
                exp_scores(b0, 15)
                low_branch2(a0, 0)
                low_branch2(a0, 1)
                low_branch2(a0, 2)
                low_branch2(a0, 3)
                low_branch2(a1, 0)
                exp_att2(a0, 0)
                low_branch2(a1, 1)
                exp_att2(a0, 1)
                exp_scores(b1, 0)
                low_branch2(a1, 2)
                exp_scores(b1, 1)
                low_branch2(a1, 3)
                exp_scores(b1, 2)
                exp_att2(a1, 0)
                exp_scores(b1, 3)
                exp_scores(b1, 4)
                exp_att2(a1, 1)
                exp_scores(b1, 5)
                elu_twice2(a0, 0)
                exp_scores(b1, 6)
                elu_twice2(a0, 1)
                exp_scores(b1, 7)
                exp_scores(b1, 8)
                exp_scores(b1, 9)
                elu_twice2(a1, 0)
                elu_twice2(a1, 1)
                exp_scores(b1, 10)
                exp_scores(b1, 11)
                exp_scores(b1, 12)
                exp_scores(b1, 13)
                exp_scores(b1, 14)
                copy_x1T(a0)
                exp_scores(b1, 15)
                high_part(a0, 0)
                high_part(a0, 1)
                copy_x1T(a1)
                copy_v(a0)
                high_part(a1, 0)
                high_part(a1, 1)
                copy_y1T(b0)
                relu_hid(b0)
                copy_v(a1)
                copy_y1T(b1)
                relu_hid(b1)
            rounds(act, one_round)

        @block.vector
        def _(dve):
            nc.vector.memset(minus_one[:, :], -1.0).then_inc(minus_one_set, 1)
            nc.vector.memset(zero_b[:, :, :], 0.0).then_inc(minus_one_set, 1)
            dve.wait_ge(w_loaded, W_ALL)
            dve.wait_ge(const_set, 13)
            chain = [0]

            def link(ins):
                ins.then_inc(prep, 1)
                chain[0] += 1
                dve.wait_ge(prep, chain[0])

            for W, a, width, ks in ((Wfc, a_fc_b, H, range(HC)), (Wh, a_hand_b, C, (None,))):
                for k in ks:
                    Wk = W[:, :] if k is None else W[:, k, :]
                    for side in range(2):
                        link(nc.vector.tensor_tensor(wa_tmp, Wk[:, 2:2 + width],
                                                     a[:, side * width:(side + 1) * width], ALU.mult)
                             if width == H else
                             nc.vector.tensor_tensor(wa_tmp[:, 0:width], Wk[:, 2:2 + width],
                                                     a[:, side * width:(side + 1) * width], ALU.mult))
                        link(nc.vector.tensor_reduce(Wk[:, side:side + 1], wa_tmp[:, 0:width], AX_X, ALU.add))
            link(nc.vector.tensor_tensor(be1_b[:, :], be1_b[:, :], m2_b[:, :], ALU.add))
            link(nc.vector.tensor_scalar(mask_nat[:, :, :], adj_i, 0.0, None, ALU.is_gt))
            link(nc.vector.tensor_reduce(row_count[:, :], mask_nat[:, :, :], AX_X, ALU.add))
            link(nc.vector.tensor_scalar(empty[:, :], row_count[:, :], 0.5, None, ALU.is_lt))
            link(nc.vector.tensor_scalar(occupied[:, :], empty[:, :], -1.0, 1.0, ALU.mult, ALU.add))
            for t in range(T):
                link(nc.vector.tensor_scalar(
                    neg_f32[:, t, :].rearrange("p (u q) -> p u q", u=T),
                    mask_nat[:, t, :].rearrange("p (q u) -> p u q", u=T), -NEG, NEG, ALU.mult, ALU.add))
            for t in range(T):
                link(nc.vector.tensor_scalar(neg_nat[:, t, :], neg_f32[:, t, :], occupied[:, t:t + 1], None,
                                             ALU.mult))
            link(nc.vector.memset(fmax1[0][:, :], 0.0))
            for k in range(T + 1):
                dve.wait_ge(adj_T, k + 1)
                dst = neg_T[:, k, :] if k < T else empty_b[:, :]
                nc.vector.tensor_copy(dst, bank[k % 3][:, :]).then_inc(prep, 1)
            chain[0] += T + 1
            assert chain[0] == PREP
            dve.wait_ge(prep, PREP)

            @live
            def arguments1(a):
                p = a[1]
                g = arg1[p]
                dve.wait_ge(S["f1b_made"][p], count("f1b_made", a))
                nc.vector.reduce_max(fmax1[p][:, :], bank[SIDE["f1_rows"][p]][:, :], AX_X
                                     ).then_inc(S["fmax1_ready"][p], 1)
                dve.wait_ge(S["fmax1_ready"][p], count("fmax1_ready", a))
                nc.vector.tensor_scalar(g[:, 0, :], h1[p][:, :, 0], fmax1[p][:, 0:1], 1.0 - ALPHA,
                                        ALU.add, ALU.mult).then_inc(S["arg1_ready"][p], 1)
                nc.vector.tensor_scalar(g[:, 1, :], h1[p][:, :, 1], fmax1[p][:, 0:1], None,
                                        ALU.subtract).then_inc(S["arg1_ready"][p], 1)
                dve.wait_ge(S["arg1_ready"][p], count("arg1_ready", a, 5, 2))
                nc.vector.tensor_scalar(g[:, 2, :], g[:, 0, :], -1.0, 0.0, ALU.mult, ALU.min
                                        ).then_inc(S["arg1_ready"][p], 1)
                nc.vector.tensor_scalar(g[:, 3, :], g[:, 1, :], ALPHA, None, ALU.mult
                                        ).then_inc(S["arg1_ready"][p], 1)
                dve.wait_ge(S["arg1_ready"][p], count("arg1_ready", a, 5, 3))
                nc.vector.tensor_scalar(g[:, 0, :], g[:, 0, :], 0.0, None, ALU.min
                                        ).then_inc(S["arg1_ready"][p], 1)

            @live
            def weights1(a, j):
                p = a[1]
                dve.wait_ge(S["low1_ready"][p], count("low1_ready", a, T, j + 1))
                if j == 0:
                    if has_former(a):
                        dve.wait_ge(S["parts_stored"][p], count("parts_stored", former(a), 32))
                nc.vector.scalar_tensor_tensor(att[p][:, j, :], bank[SIDE["A_rows"][p]][:, :],
                                               fac1[p][:, 1, j:j + 1], low[p][:, j, :], ALU.mult, ALU.max
                                               ).then_inc(S["att1_ready"][p], 1)

            @live
            def normalise1(a, t):
                p = a[1]
                ps = bank[SIDE[f"gat1_{t}"][p]]
                dve.wait_ge(S["gat1_made"][p], count("gat1_made", a, T, t + 1))
                nc.vector.reciprocal(rz1[p][:, t:t + 1], ps[:, H:H + 1]).then_inc(S["rz1_ready"][p], 1)
                dve.wait_ge(S["rz1_ready"][p], count("rz1_ready", a, T, t + 1))
                nc.vector.tensor_scalar(neg1[p][:, t, :], ps[:, 0:H], rz1[p][:, t:t + 1], 0.0, ALU.mult,
                                        ALU.min).then_inc(S["neg1_ready"][p], 1)
                dve.wait_ge(S["neg1_ready"][p], count("neg1_ready", a, T, t + 1))
                nc.vector.scalar_tensor_tensor(pos1[p][:, t, :], ps[:, 0:H], rz1[p][:, t:t + 1],
                                               neg1[p][:, t, :], ALU.mult, ALU.subtract
                                               ).then_inc(S["pos1_ready"][p], 1)

            @live
            def residual0(a, f):
                p = a[1]
                dve.wait_ge(S["gat1T_made"][p], count("gat1T_made", a, HC, f + 1))
                nc.vector.scalar_tensor_tensor(out1[p][:, f, :], bank[SIDE[f"gat1T_{f}"][p]][:, :], -1.0,
                                               out1[p][:, f, :], ALU.add, ALU.add
                                               ).then_inc(S["res1_ready"][p], 1)

            @live
            def copy_h2(a, i):
                p = a[1]
                src = bank[SIDE[f"h2_{i}"][p]][:, 0:2 * (C + 2)].rearrange("p (t c) -> p t c", t=2)
                dve.wait_ge(S["h2_made"][p], count("h2_made", a, 2, i + 1))
                nc.vector.tensor_copy(h2[p][:, 2 * i:2 * i + 2, 0:2 + C], src).then_inc(S["h2_copied"][p], 1)

            @live
            def neighbour_max(a, h):
                p = a[1]
                if h == 0:
                    dve.wait_ge(S["f2b_made"][p], count("f2b_made", a, 1, 1))
                    dve.sem_inc(waits_passed, 1)
                for t in (2 * h, 2 * h + 1):
                    nc.vector.tensor_tensor_reduce(out=low[p][:, t, :], in0=bank[SIDE["f2_rows"][p]][:, :],
                                                   in1=neg_nat[:, t, :], scale=1.0, scalar=3 * NEG,
                                                   op0=ALU.add, op1=ALU.max, accum_out=fmax2[p][:, t:t + 1]
                                                   ).then_inc(S["fmax2_ready"][p], 1)

            @live
            def row_terms2(a):
                p = a[1]
                dve.wait_ge(S["fmax2_ready"][p], count("fmax2_ready", a, T))
                nc.vector.tensor_tensor(s2[p][:, :], h2[p][:, :, 0], fmax2[p][:, :], ALU.add
                                        ).then_inc(S["s2_ready"][p], 1)
                dve.wait_ge(S["s2_ready"][p], count("s2_ready", a, 3, 1))
                nc.vector.scalar_tensor_tensor(m2[p][:, :], s2[p][:, :], ALPHA, s2[p][:, :], ALU.mult, ALU.max
                                               ).then_inc(S["s2_ready"][p], 1)
                nc.vector.tensor_scalar(f2s[p][:, :], h2[p][:, :, 1], ALPHA, None, ALU.mult
                                        ).then_inc(S["f2s_ready"][p], 1)
                dve.wait_ge(S["s2_ready"][p], count("s2_ready", a, 3, 2))
                nc.vector.scalar_tensor_tensor(m2[p][:, :], empty[:, :], NEG, m2[p][:, :], ALU.mult, ALU.add
                                               ).then_inc(S["s2_ready"][p], 1)
                dve.wait_ge(S["s2_ready"][p], count("s2_ready", a, 3, 3))
                nc.vector.tensor_tensor(row2[p][:, 0, :], h2[p][:, :, 0], m2[p][:, :], ALU.subtract
                                        ).then_inc(S["row2_ready"][p], 1)
                nc.vector.scalar_tensor_tensor(row2[p][:, 1, :], h2[p][:, :, 0], ALPHA, m2[p][:, :], ALU.mult,
                                               ALU.subtract).then_inc(S["row2_ready"][p], 1)

            @live
            def arguments2(a, j):
                p = a[1]
                dve.wait_ge(S["low2_ready"][p], count("low2_ready", a, T, j + 1))
                nc.vector.scalar_tensor_tensor(low[p][:, j, :], bank[SIDE["R1_rows"][p]][:, :],
                                               h2[p][:, j, 1:2], low[p][:, j, :], ALU.add, ALU.max
                                               ).then_inc(S["arg2_ready"][p], 1)

            @live
            def mask_arguments2(a):
                p = a[1]
                dve.wait_ge(S["arg2_ready"][p], count("arg2_ready", a, T))
                nc.vector.tensor_tensor(low[p][:, 2:4, :], low[p][:, 2:4, :], neg_T[:, 2:4, :], ALU.add
                                        ).then_inc(S["argm1_ready"][p], 1)

            @live
            def normalise2(a, i):
                p = a[1]
                ps = bank[SIDE[f"gat2_{i}"][p]][:, 0:2 * (C + 1)].rearrange("p (t c) -> p t c", t=2)
                dve.wait_ge(S["gat2_made"][p], count("gat2_made", a, 2, i + 1))
                nc.vector.reciprocal(rz2[p][:, 2 * i:2 * i + 2], ps[:, :, C]).then_inc(S["rz2_ready"][p], 1)
                dve.wait_ge(S["rz2_ready"][p], count("rz2_ready", a, 2, i + 1))
                for k in range(2):
                    t = 2 * i + k
                    nc.vector.tensor_scalar(neg2[p][:, t, :], ps[:, k, 0:C], rz2[p][:, t:t + 1], 0.0,
                                            ALU.mult, ALU.min).then_inc(S["neg2_ready"][p], 1)
                for k in range(2):
                    t = 2 * i + k
                    dve.wait_ge(S["neg2_ready"][p], count("neg2_ready", a, T, t + 1))
                    nc.vector.scalar_tensor_tensor(pos2[p][:, t, :], ps[:, k, 0:C], rz2[p][:, t:t + 1],
                                                   neg2[p][:, t, :], ALU.mult, ALU.subtract
                                                   ).then_inc(S["pos2_ready"][p], 1)

            def flat(ap):
                return ap.rearrange("p t c -> p (t c)")

            @live
            def finish_gat2(a, step):
                p = a[1]
                if step == 0:
                    dve.wait_ge(S["w2_ready"][p], count("w2_ready", a))
                    nc.vector.tensor_tensor(pos2[p], pos2[p], neg2[p], ALU.add).then_inc(S["sum2_ready"][p], 1)
                elif step == 1:
                    dve.wait_ge(S["sum2_ready"][p], count("sum2_ready", a))
                    dve.wait_ge(S["out2T_made"][p], count("out2T_made", a))
                    nc.vector.scalar_tensor_tensor(flat(pos2[p]), bank[SIDE["out2T"][p]][:, :], -1.0,
                                                   flat(pos2[p]), ALU.add, ALU.add
                                                   ).then_inc(S["sum2b_ready"][p], 1)
                else:
                    dve.wait_ge(S["sum2b_ready"][p], count("sum2b_ready", a))
                    dve.wait_ge(S["x_loaded"][p], count("x_loaded", a, 16))
                    nc.vector.scalar_tensor_tensor(flat(y0[p]), flat(pos2[p]), 0.0, flat(x_nat[p][:, :, :]),
                                                   ALU.max, ALU.add).then_inc(S["y0_ready"][p], 1)

            norms = ((("y0_ready", 1), y0, x1, "x1_ready"), (("y1_ready", 1), attn, y1n, "y1n_ready"),
                     (("y2_ready", 1), y1n, attn, "y2n_ready"), (("y3_ready", 1), attn, y1n, "o_ready"))

            @live
            def statistics(b, i):
                p = b[1]
                (ready, per), src, _, _ = norms[i]
                dve.wait_ge(S[ready][p], count(ready, b, per))
                for t in range(T):
                    nc.vector.bn_stats(stat[i][p][:, t, :], src[p][:, t, :]).then_inc(ln_step[i], 1)
                for t in range(T):
                    dve.wait_ge(ln_step[i], passed(b, 2 * T, t + 1))
                    dve.sem_inc(waits_passed, 1)
                    nc.vector.bn_aggr(mv[i][p][:, t, :], stat[i][p][:, t, :]).then_inc(ln_step[i], 1)

            @live
            def normalise(b, i, h):
                p = b[1]
                _, src, dst, signal = norms[i]
                dve.wait_ge(ln_rstd[i], passed(b, 2, 2))
                if i == 0:
                    if has_former(b):
                        dve.wait_ge(S["xc_ready"][p], count("xc_ready", former(b)))
                if i == 1:
                    if has_former(b):
                        dve.wait_ge(S["stored"][p], count("stored", former(b), 16))
                for t in (2 * h, 2 * h + 1):
                    last = nc.vector.tensor_scalar(dst[p][:, t, :], src[p][:, t, :], mv[i][p][:, t, 0:1],
                                                   rstd[i][p][:, t:t + 1], ALU.subtract, ALU.mult)
                last.then_inc(S[signal][p], 1)

            @live
            def rest(a, i):
                p = a[1]
                dve.wait_ge(S["high_ready"][p], count("high_ready", a, 2, i + 1))
                nc.vector.tensor_tensor(qk_rest[p][:, i, :], bank[SIDE["qk"[i]][p]][:, :],
                                        qk_parts[p][:, i, 0, :], ALU.subtract).then_inc(S["rest_ready"][p], 1)

            @live
            def middle_part(a, i):
                p = a[1]
                dve.wait_ge(S["rest_ready"][p], count("rest_ready", a, 2, i + 1))
                nc.vector.tensor_copy(qk_parts[p][:, i, 1, :], qk_rest[p][:, i, :]
                                      ).then_inc(S["mid_ready"][p], 1)

            @live
            def copy_vcol(a):
                p = a[1]
                dve.wait_ge(S["vcol_made"][p], count("vcol_made", a))
                if has_former(a):
                    dve.wait_ge(S["oT_ready"][p], count("oT_ready", former(a), 2))
                nc.vector.tensor_copy(vcol[p][:, :], bank[SIDE["vcol"][p]][:, 0:GROUPS]
                                      ).then_inc(S["vcol_ready"][p], 1)

            @live
            def mask_scores(b, k):
                p, unit, s = b[1], k // GH, k % GH
                dve.wait_ge(S["scores_made"][p], count("scores_made", b, 16, k + 1))
                if not any(j in DVE_MASKED for j in range(unit * GH, k)):
                    for made, value in probs_readers(b, unit):
                        dve.wait_ge(made, value)
                jp = unit % 2
                nc.vector.tensor_tensor(probs[:, unit % 2, s, :, :], sc[k % 2][:, :, :],
                                        neg_T[:, 2 * jp:2 * jp + 2, :], ALU.add
                                        ).then_inc(S["masked_ready"][p], 1)

            @live
            def take_group(b, g):
                p = b[1]
                dve.wait_ge(S["pv_made"][p], count("pv_made", b, 4, 2 * g + 2))
                dve.wait_ge(S["vcol_ready"][p], count("vcol_ready", b))
                if p:
                    dve.wait_ge(S["oTT_made"][0], count("oTT_made", (b[0], 0), 2, g + 1))
                else:
                    if has_former((b[0], 1)):
                        dve.wait_ge(S["oTT_made"][1], count("oTT_made", former((b[0], 1)), 2, g + 1))
                nc.vector.scalar_tensor_tensor(oT[:, g, :], empty_b[:, :], vcol[p][:, g:g + 1],
                                               oacc[:, :], ALU.mult, ALU.add).then_inc(S["oT_ready"][p], 1)

            @live
            def normalise_heads(b, g):
                p = b[1]
                ps = bank[SIDE[f"oT_{g}"][p]][:, :].rearrange("p (t h s) -> p t h s", t=T, s=STRIP)
                dve.wait_ge(S["oTT_made"][p], count("oTT_made", b, 2, g + 1))
                nc.vector.reciprocal(rzh[p][:, g, :, :], ps[:, :, :, D]).then_inc(S["rzh_ready"][p], 1)
                dve.wait_ge(S["rzh_ready"][p], count("rzh_ready", b, 2, g + 1))
                nc.vector.tensor_tensor(
                    attn[p][:, :, g * GH * D:(g + 1) * GH * D].rearrange("p t (h d) -> p t h d", d=D),
                    ps[:, :, :, 0:D], rzh[p][:, g, :, :].unsqueeze(3).to_broadcast([P, T, GH, D]),
                    ALU.mult).then_inc(S["attn_ready"][p], 1)

            @live
            def residual1(b):
                p = b[1]
                dve.wait_ge(S["attn_ready"][p], count("attn_ready", b, 2))
                dve.wait_ge(S["xc_ready"][p], count("xc_ready", b))
                nc.vector.tensor_tensor(attn[p][:, :, :], attn[p][:, :, :], xc[p][:, :, :], ALU.add
                                        ).then_inc(S["y1_ready"][p], 1)

            @live
            def residual2(b):
                p = b[1]
                dve.wait_ge(S["ff_made"][p], count("ff_made", b))
                dve.wait_ge(S["y1m_ready"][p], count("y1m_ready", b))
                nc.vector.tensor_tensor(flat(y1n[p][:, :, :]), bank[SIDE["ff"][p]][:, :],
                                        flat(y1n[p][:, :, :]), ALU.add).then_inc(S["y2_ready"][p], 1)

            @live
            def residual3(b):
                p = b[1]
                dve.wait_ge(S["y2g_ready"][p], count("y2g_ready", b))
                dve.wait_ge(S["x1b_ready"][p], count("x1b_ready", b))
                nc.vector.tensor_tensor(attn[p][:, :, :], attn[p][:, :, :], xc[p][:, :, :], ALU.add
                                        ).then_inc(S["y3_ready"][p], 1)

            def one_round(a, b):
                a0, a1 = a
                b0, b1 = b
                arguments1(a0)
                weights1(a0, 0)
                weights1(a0, 1)
                arguments1(a1)
                weights1(a0, 2)
                weights1(a0, 3)
                weights1(a1, 0)
                weights1(a1, 1)
                weights1(a1, 2)
                weights1(a1, 3)
                normalise1(a0, 0)
                normalise1(a0, 1)
                mask_scores(b0, 0)
                normalise1(a0, 2)
                normalise1(a1, 0)
                normalise1(a0, 3)
                normalise1(a1, 1)
                mask_scores(b0, 2)
                normalise1(a1, 2)
                mask_scores(b0, 5)
                normalise1(a1, 3)
                residual0(a0, 0)
                residual0(a0, 1)
                mask_scores(b0, 8)
                copy_h2(a0, 0)
                copy_h2(a0, 1)
                residual0(a1, 0)
                mask_scores(b0, 10)
                neighbour_max(a0, 0)
                residual0(a1, 1)
                neighbour_max(a0, 1)
                row_terms2(a0)
                take_group(b0, 0)
                mask_scores(b0, 13)
                copy_h2(a1, 0)
                copy_h2(a1, 1)
                neighbour_max(a1, 0)
                arguments2(a0, 0)
                neighbour_max(a1, 1)
                arguments2(a0, 1)
                row_terms2(a1)
                arguments2(a0, 2)
                arguments2(a0, 3)
                mask_arguments2(a0)
                mask_scores(b1, 0)
                arguments2(a1, 0)
                take_group(b0, 1)
                arguments2(a1, 1)
                mask_scores(b1, 2)
                arguments2(a1, 2)
                arguments2(a1, 3)
                normalise2(a0, 0)
                mask_arguments2(a1)
                mask_scores(b1, 5)
                normalise2(a0, 1)
                normalise2(a1, 0)
                finish_gat2(a0, 0)
                mask_scores(b1, 8)
                finish_gat2(a0, 1)
                normalise2(a1, 1)
                finish_gat2(a0, 2)
                mask_scores(b1, 10)
                statistics(a0, 0)
                finish_gat2(a1, 0)
                take_group(b1, 0)
                finish_gat2(a1, 1)
                normalise(a0, 0, 0)
                mask_scores(b1, 13)
                normalise(a0, 0, 1)
                finish_gat2(a1, 2)
                statistics(a1, 0)
                normalise_heads(b0, 0)
                normalise_heads(b0, 1)
                residual1(b0)
                normalise(a1, 0, 0)
                rest(a0, 0)
                rest(a0, 1)
                middle_part(a0, 0)
                middle_part(a0, 1)
                statistics(b0, 1)
                normalise(a1, 0, 1)
                take_group(b1, 1)
                normalise_heads(b1, 0)
                normalise(b0, 1, 0)
                normalise(b0, 1, 1)
                rest(a1, 0)
                normalise_heads(b1, 1)
                rest(a1, 1)
                residual1(b1)
                middle_part(a1, 0)
                middle_part(a1, 1)
                statistics(b1, 1)
                copy_vcol(a0)
                normalise(b1, 1, 0)
                normalise(b1, 1, 1)
                residual2(b0)
                statistics(b0, 2)
                copy_vcol(a1)
                normalise(b0, 2, 0)
                normalise(b0, 2, 1)
                residual2(b1)
                statistics(b1, 2)
                residual3(b0)
                statistics(b0, 3)
                normalise(b1, 2, 0)
                normalise(b1, 2, 1)
                normalise(b0, 3, 0)
                normalise(b0, 3, 1)
                residual3(b1)
                statistics(b1, 3)
                normalise(b1, 3, 0)
                normalise(b1, 3, 1)
            rounds(dve, one_round)

        @block.tensor
        def _(pe):
            pe.wait_ge(const_set, 13)
            pe.wait_ge(prep, PREP_T)
            for k in range(T + 1):
                if k >= 3:
                    pe.wait_ge(prep, PREP_T + k - 2)
                for t in range(T):
                    src = neg_f32[:, t, k * P:(k + 1) * P] if k < T else bc(empty[:, t:t + 1], [P, P])
                    last = nc.tensor.transpose(bank[k % 3][:, t * P:(t + 1) * P], src, ident[:, :])
                last.then_inc(adj_T, 1)
            pe.wait_ge(prep, PREP)

            def last_reader(*users):
                for name, b, per, k, back in users:
                    r = b[0] - back
                    if (back == 0 and not b[2]) or (isinstance(r, int) and r < 0):
                        continue
                    return [(S[name][b[1]], count(name, (r, b[1]), per, k))]
                return []

            def transpose_tiles(dst, src):
                for t in range(T):
                    last = nc.tensor.transpose(dst[:, t * P:(t + 1) * P], src(t), ident[:, :])
                return last

            def side(name, b):
                return bank[SIDE[name][b[1]]]

            @live
            def transpose_x(a):
                p = a[1]
                pe.wait_ge(S["x_loaded"][p], count("x_loaded", a, 16))
                transpose_tiles(side("xT", a), lambda t: x_nat[p][:, t, :]).then_inc(S["xT_made"][p], 1)

            @live
            def hidden1(a, f):
                p = a[1]
                pe.wait_ge(S["xT_copied"][p], count("xT_copied", a))
                nc.tensor.matmul(side(f"out1_{f}", a)[:, :], W1[:, f * P:(f + 1) * P], xT[p][:, :],
                                 start=True, stop=True).then_inc(S["out1_made"][p], 1)

            @live
            def project1(a, t):
                p = a[1]
                pe.wait_ge(S["out1_ready"][p], count("out1_ready", a, HC))
                for k in range(HC):
                    last = nc.tensor.matmul(side(f"h1_{t}", a)[:, 0:2 + H], out1[p][:, k, t * P:(t + 1) * P],
                                            Wfc[:, k, :], start=(k == 0), stop=(k == HC - 1))
                last.then_inc(S["h1_made"][p], 1)

            @live
            def rows_of_f1(a):
                p = a[1]
                pe.wait_ge(S["h1_copied"][p], count("h1_copied", a, T))
                transpose_tiles(side("f1_rows", a), lambda t: bc(h1[p][:, t, 1:2], [P, P])
                                ).then_inc(S["f1b_made"][p], 1)

            @live
            def rows_of_factors1(a, i):
                p = a[1]
                pe.wait_ge(S["fac1_ready"][p], count("fac1_ready", a))
                name, which = (("A_rows", 0), ("C_rows", 2))[i]
                transpose_tiles(side(name, a), lambda t: bc(fac1[p][:, which, t:t + 1], [P, P])
                                ).then_inc(S["rows1_made"][p], 1)

            @live
            def attend1(a, t, h):
                p = a[1]
                pe.wait_ge(S["att1_ready"][p], count("att1_ready", a, T, 2 * h + 2 if t == 0 else T))
                for j in (2 * h, 2 * h + 1):
                    last = nc.tensor.matmul(side(f"gat1_{t}", a)[:, 0:H + 1], att[p][:, j, t * P:(t + 1) * P],
                                            h1[p][:, j, 2:], start=(j == 0), stop=(j == T - 1))
                if h:
                    last.then_inc(S["gat1_made"][p], 1)

            @live
            def transpose_gat1(a, f):
                p = a[1]
                pe.wait_ge(S["gat1_ready"][p], count("gat1_ready", a, 2))
                transpose_tiles(side(f"gat1T_{f}", a), lambda t: pos1[p][:, t, f * P:(f + 1) * P]
                                ).then_inc(S["gat1T_made"][p], 1)

            @live
            def hidden2(a, k):
                p = a[1]
                pe.wait_ge(S["res1_ready"][p], count("res1_ready", a, HC, k + 1))
                last = nc.tensor.matmul(side("out2", a)[:, :], W2[:, k, :], out1[p][:, k, :], start=(k == 0),
                                        stop=(k == HC - 1))
                if k:
                    last.then_inc(S["out2_made"][p], 1)

            @live
            def project2(a, i):
                p = a[1]
                pe.wait_ge(S["out2_ready"][p], count("out2_ready", a))
                for k in range(2):
                    t = 2 * i + k
                    last = nc.tensor.matmul(side(f"h2_{i}", a)[:, k * (C + 2):(k + 1) * (C + 2)],
                                            out2[p][:, t * P:(t + 1) * P], Wh[:, :], start=True, stop=True)
                last.then_inc(S["h2_made"][p], 1)

            @live
            def rows_of_f2(a):
                p = a[1]
                pe.wait_ge(S["h2_copied"][p], count("h2_copied", a, 2))
                transpose_tiles(side("f2_rows", a), lambda t: bc(h2[p][:, t, 1:2], [P, P])
                                ).then_inc(S["f2b_made"][p], 1)

            @live
            def rows_of_terms2(a, i):
                p = a[1]
                pe.wait_ge(S["row2_ready"][p], count("row2_ready", a, 2))
                transpose_tiles(side(("R1_rows", "R2_rows")[i], a), lambda t: bc(row2[p][:, i, t:t + 1], [P, P])
                                ).then_inc(S["rows2_made"][p], 1)

            @live
            def attend2(a, i, k):
                p = a[1]
                t = 2 * i + k
                pe.wait_ge(S["att2_ready"][p], count("att2_ready", a, 2))
                for j in range(T):
                    last = nc.tensor.matmul(side(f"gat2_{i}", a)[:, k * (C + 1):(k + 1) * (C + 1)],
                                            att[p][:, j, t * P:(t + 1) * P], h2[p][:, j, 2:],
                                            start=(j == 0), stop=(j == T - 1))
                if k:
                    last.then_inc(S["gat2_made"][p], 1)

            @live
            def transpose_out2(a):
                p = a[1]
                transpose_tiles(side("out2T", a), lambda t: out2[p][:, t * P:(t + 1) * P]
                                ).then_inc(S["out2T_made"][p], 1)

            @live
            def transpose_x1(a):
                p = a[1]
                pe.wait_ge(S["x1_ready"][p], count("x1_ready", a, 2))
                transpose_tiles(side("x1T", a), lambda t: x1[p][:, t, :]).then_inc(S["x1T_made"][p], 1)

            @live
            def project_qk(a, i):
                p = a[1]
                pe.wait_ge(S["x1T_copied"][p], count("x1T_copied", a))
                nc.tensor.matmul(side("qk"[i], a)[:, :], Wqkv[:, i * C:(i + 1) * C], x1T[p][:, :],
                                 start=True, stop=True).then_inc(S[("q_made", "k_made")[i]][p], 1)

            @live
            def project_v(a):
                p = a[1]
                pe.wait_ge(S["x1T_copied"][p], count("x1T_copied", a))
                for t in range(T):
                    last = nc.tensor.matmul(side("v", a)[:, t * P:(t + 1) * P], x1T[p][:, t * P:(t + 1) * P],
                                            Wqkv[:, 2 * C:3 * C], start=True, stop=True)
                last.then_inc(S["v_made"][p], 1)

            @live
            def columns_of_v(a):
                p = a[1]
                pe.wait_ge(S["v_copied"][p], count("v_copied", a))
                for g in range(GROUPS):
                    for t in range(T):
                        last = nc.tensor.matmul(side("vcol", a)[:, g:g + 1],
                                                v[p][:, t, g, :, :].rearrange("p h s -> p (h s)"), ones[:, :],
                                                start=(t == 0), stop=(t == T - 1))
                last.then_inc(S["vcol_made"][p], 1)

            def score_reader(b, k):
                if k >= 2:
                    at, k = (b[0], b[1]), k - 2
                elif b[1]:
                    at, k = (b[0], 0), k + 14
                elif has_former(b):
                    at, k = (b[0] - 1, 1), k + 14
                else:
                    return []
                if k in PE_MASKED:
                    return [(S["probs_ready"][at[1]], count("probs_ready", at, 16, k + 1))]
                return [(S["masked_ready"][at[1]], count("masked_ready", at, MASKED_BY_DVE, masked_so_far(k)))]

            @live
            def scores(b, k):
                p, unit, s = b[1], k // GH, k % GH
                g, jp = unit // 2, unit % 2
                if k == 0:
                    pe.wait_ge(S["stacked"][p], count("stacked", b, 16 * 2 * len(Q_TERMS)))
                for read, value in score_reader(b, k):
                    pe.wait_ge(read, value)
                for i in range(2):
                    j = 2 * jp + i
                    if k in PE_MASKED:
                        nc.tensor.matmul(sc[k % 2][:, i, :], ident_bf[:, :], neg_T[:, j, :],
                                         start=True, stop=False)
                    last = nc.tensor.matmul(sc[k % 2][:, i, :], Ks[p][:, g * GH + s, j * P:(j + 1) * P],
                                            Qs[p][:, g * GH + s, :], start=(k not in PE_MASKED), stop=True)
                last.then_inc(S["scores_made"][p], 1)

            @live
            def attend_heads(b, unit, i):
                p = b[1]
                g, jp = unit // 2, unit % 2
                if i == 0:
                    pe.wait_ge(S["probs_ready"][p], count("probs_ready", b, 16, unit * GH + GH))
                    if jp == 0:
                        if g:
                            pe.wait_ge(S["oT_ready"][p], count("oT_ready", b, 2, 1))
                        elif p:
                            pe.wait_ge(S["oT_ready"][0], count("oT_ready", (b[0], 0), 2))
                        else:
                            if has_former((b[0], 1)):
                                pe.wait_ge(S["oT_ready"][1], count("oT_ready", former((b[0], 1)), 2))
                for s in range(GH):
                    last = nc.tensor.matmul(oacc[s * STRIP:(s + 1) * STRIP, :], v[p][:, 2 * jp + i, g, s, :],
                                            probs[:, unit % 2, s, i, :],
                                            start=(jp == 0 and i == 0), stop=(jp == 1 and i == 1))
                if i:
                    last.then_inc(S["pv_made"][p], 1)

            @live
            def transpose_heads(b, g):
                p = b[1]
                pe.wait_ge(S["oT_ready"][p], count("oT_ready", b, 2, g + 1))
                transpose_tiles(side(f"oT_{g}", b), lambda t: oT[:, g, t * P:(t + 1) * P]
                                ).then_inc(S["oTT_made"][p], 1)

            @live
            def transpose_y1(b):
                p = b[1]
                pe.wait_ge(S["y1n_ready"][p], count("y1n_ready", b, 2))
                transpose_tiles(side("y1T", b), lambda t: y1n[p][:, t, :]).then_inc(S["y1T_made"][p], 1)

            @live
            def feed_hidden(b):
                p = b[1]
                pe.wait_ge(S["y1T_copied"][p], count("y1T_copied", b))
                nc.tensor.matmul(side("hid", b)[:, :], M1[:, :], y1T[p][:, :], start=True, stop=True
                                 ).then_inc(S["hid_made"][p], 1)

            @live
            def feed_out(b):
                p = b[1]
                pe.wait_ge(S["hid_ready"][p], count("hid_ready", b))
                for t in range(T):
                    last = nc.tensor.matmul(side("ff", b)[:, t * P:(t + 1) * P], hid[p][:, t * P:(t + 1) * P],
                                            M2[:, :], start=True, stop=True)
                last.then_inc(S["ff_made"][p], 1)

            def one_round(a, b):
                a0, a1 = a
                b0, b1 = b
                for read, value in last_reader(("vcol_ready", a1, 1, 1, 1)):
                    pe.wait_ge(read, value)
                transpose_x(a0)
                for read, value in last_reader(("y2_ready", b1, 1, 1, 1), ("hid_ready", b1, 1, 1,
                        1), ("y1T_copied", b1, 1, 1, 1), ("vcol_ready", a0, 1, 1, 1)):
                    pe.wait_ge(read, value)
                transpose_x(a1)
                if a0[2]:
                    pe.wait_ge(S["xT_copied"][0], count("xT_copied", a0, 1, 1))
                hidden1(a0, 0)
                if a1[2]:
                    pe.wait_ge(S["xT_copied"][1], count("xT_copied", a1, 1, 1))
                hidden1(a0, 1)
                if a0[2]:
                    pe.wait_ge(S["out1_ready"][0], count("out1_ready", a0, 2, 1))
                hidden1(a1, 0)
                if a0[2]:
                    pe.wait_ge(S["out1_ready"][0], count("out1_ready", a0, 2, 2))
                project1(a0, 0)
                if a1[2]:
                    pe.wait_ge(S["out1_ready"][1], count("out1_ready", a1, 2, 1))
                project1(a0, 1)
                if a0[2]:
                    pe.wait_ge(S["h1_copied"][0], count("h1_copied", a0, 4, 1))
                project1(a0, 2)
                if a0[2]:
                    pe.wait_ge(S["h1_copied"][0], count("h1_copied", a0, 4, 2))
                hidden1(a1, 1)
                if a0[2]:
                    pe.wait_ge(S["h1_copied"][0], count("h1_copied", a0, 4, 3))
                project1(a0, 3)
                if a1[2]:
                    pe.wait_ge(S["out1_ready"][1], count("out1_ready", a1, 2, 2))
                project1(a1, 0)
                if a0[2]:
                    pe.wait_ge(S["h1_copied"][0], count("h1_copied", a0, 4, 4))
                rows_of_f1(a0)
                for read, value in last_reader(("y2_ready", b0, 1, 1, 1), ("hid_ready", b0, 1, 1,
                        1), ("y1T_copied", b0, 1, 1, 1), ("rest_ready", a1, 2, 1, 1)):
                    pe.wait_ge(read, value)
                project1(a1, 1)
                if a1[2]:
                    pe.wait_ge(S["h1_copied"][1], count("h1_copied", a1, 4, 1))
                project1(a1, 2)
                if a0[2]:
                    pe.wait_ge(S["fmax1_ready"][0], count("fmax1_ready", a0, 1, 1))
                rows_of_factors1(a0, 1)
                if a1[2]:
                    pe.wait_ge(S["h1_copied"][1], count("h1_copied", a1, 4, 2))
                rows_of_factors1(a0, 0)
                if a1[2]:
                    pe.wait_ge(S["h1_copied"][1], count("h1_copied", a1, 4, 3))
                project1(a1, 3)
                if a1[2]:
                    pe.wait_ge(S["h1_copied"][1], count("h1_copied", a1, 4, 4))
                rows_of_f1(a1)
                scores(b0, 0)
                if a1[2]:
                    pe.wait_ge(S["fmax1_ready"][1], count("fmax1_ready", a1, 1, 1))
                rows_of_factors1(a1, 1)
                if a0[2]:
                    pe.wait_ge(S["low1_ready"][0], count("low1_ready", a0, 4, 4))
                rows_of_factors1(a1, 0)
                if a0[2]:
                    pe.wait_ge(S["att1_ready"][0], count("att1_ready", a0, 4, 4))
                attend1(a0, 0, 0)
                attend1(a0, 0, 1)
                if a1[2]:
                    pe.wait_ge(S["low1_ready"][1], count("low1_ready", a1, 4, 4))
                attend1(a0, 1, 0)
                attend1(a0, 1, 1)
                if a1[2]:
                    pe.wait_ge(S["att1_ready"][1], count("att1_ready", a1, 4, 4))
                attend1(a0, 2, 0)
                if a0[2]:
                    pe.wait_ge(S["pos1_ready"][0], count("pos1_ready", a0, 4, 1))
                attend1(a1, 0, 0)
                attend1(a0, 2, 1)
                attend1(a1, 0, 1)
                if a0[2]:
                    pe.wait_ge(S["pos1_ready"][0], count("pos1_ready", a0, 4, 2))
                attend1(a0, 3, 0)
                if a0[2]:
                    pe.wait_ge(S["pos1_ready"][0], count("pos1_ready", a0, 4, 3))
                attend1(a1, 1, 0)
                attend1(a0, 3, 1)
                scores(b0, 1)
                attend1(a1, 1, 1)
                scores(b0, 2)
                if a0[2]:
                    pe.wait_ge(S["pos1_ready"][0], count("pos1_ready", a0, 4, 4))
                attend1(a1, 2, 0)
                scores(b0, 3)
                attend1(a1, 2, 1)
                scores(b0, 4)
                if a1[2]:
                    pe.wait_ge(S["pos1_ready"][1], count("pos1_ready", a1, 4, 2))
                attend1(a1, 3, 0)
                scores(b0, 5)
                attend1(a1, 3, 1)
                if a1[2]:
                    pe.wait_ge(S["pos1_ready"][1], count("pos1_ready", a1, 4, 3))
                transpose_gat1(a0, 0)
                scores(b0, 6)
                if a1[2]:
                    pe.wait_ge(S["pos1_ready"][1], count("pos1_ready", a1, 4, 1))
                transpose_gat1(a0, 1)
                attend_heads(b0, 0, 0)
                if a0[2]:
                    pe.wait_ge(S["res1_ready"][0], count("res1_ready", a0, 2, 1))
                hidden2(a0, 0)
                scores(b0, 7)
                hidden2(a0, 1)
                attend_heads(b0, 0, 1)
                scores(b0, 8)
                if a0[2]:
                    pe.wait_ge(S["out2_ready"][0], count("out2_ready", a0, 1, 1))
                project2(a0, 0)
                scores(b0, 9)
                if a0[2]:
                    pe.wait_ge(S["res1_ready"][0], count("res1_ready", a0, 2, 2))
                project2(a0, 1)
                if a0[2]:
                    pe.wait_ge(S["h2_copied"][0], count("h2_copied", a0, 2, 1))
                transpose_gat1(a1, 0)
                scores(b0, 10)
                if a0[2]:
                    pe.wait_ge(S["h2_copied"][0], count("h2_copied", a0, 2, 2))
                rows_of_f2(a0)
                if a1[2]:
                    pe.wait_ge(S["res1_ready"][1], count("res1_ready", a1, 2, 1))
                transpose_gat1(a1, 1)
                if a1[2]:
                    pe.wait_ge(S["pos1_ready"][1], count("pos1_ready", a1, 4, 4))
                hidden2(a1, 0)
                scores(b0, 11)
                attend_heads(b0, 1, 0)
                hidden2(a1, 1)
                scores(b0, 12)
                attend_heads(b0, 1, 1)
                scores(b0, 13)
                if a1[2]:
                    pe.wait_ge(S["out2_ready"][1], count("out2_ready", a1, 1, 1))
                project2(a1, 0)
                attend_heads(b0, 2, 0)
                scores(b0, 14)
                if a1[2]:
                    pe.wait_ge(S["h2_copied"][1], count("h2_copied", a1, 2, 1))
                project2(a1, 1)
                if a0[2]:
                    pe.wait_ge(S["fmax2_ready"][0], count("fmax2_ready", a0, 4, 4))
                rows_of_terms2(a0, 0)
                scores(b0, 15)
                if a1[2]:
                    pe.wait_ge(S["h2_copied"][1], count("h2_copied", a1, 2, 2))
                rows_of_f2(a1)
                if a1[2]:
                    pe.wait_ge(S["res1_ready"][1], count("res1_ready", a1, 2, 2))
                rows_of_terms2(a0, 1)
                attend_heads(b0, 2, 1)
                attend_heads(b0, 3, 0)
                scores(b1, 0)
                attend_heads(b0, 3, 1)
                scores(b1, 1)
                if a0[2]:
                    pe.wait_ge(S["low2_ready"][0], count("low2_ready", a0, 4, 4))
                rows_of_terms2(a1, 0)
                if a1[2]:
                    pe.wait_ge(S["fmax2_ready"][1], count("fmax2_ready", a1, 4, 4))
                rows_of_terms2(a1, 1)
                scores(b1, 2)
                if a0[2]:
                    pe.wait_ge(S["arg2_ready"][0], count("arg2_ready", a0, 4, 4))
                attend2(a0, 0, 0)
                attend2(a0, 0, 1)
                scores(b1, 3)
                if a1[2]:
                    pe.wait_ge(S["low2_ready"][1], count("low2_ready", a1, 4, 4))
                attend2(a0, 1, 0)
                scores(b1, 4)
                attend2(a0, 1, 1)
                scores(b1, 5)
                attend_heads(b1, 0, 0)
                scores(b1, 6)
                if a0[2]:
                    pe.wait_ge(S["pos2_ready"][0], count("pos2_ready", a0, 4, 2))
                attend2(a1, 0, 0)
                scores(b1, 7)
                attend2(a1, 0, 1)
                attend_heads(b1, 0, 1)
                scores(b1, 8)
                if a0[2]:
                    pe.wait_ge(S["pos2_ready"][0], count("pos2_ready", a0, 4, 4))
                attend2(a1, 1, 0)
                if a1[2]:
                    pe.wait_ge(S["pos2_ready"][1], count("pos2_ready", a1, 4, 2))
                transpose_out2(a0)
                attend2(a1, 1, 1)
                scores(b1, 9)
                scores(b1, 10)
                attend_heads(b1, 1, 0)
                scores(b1, 11)
                attend_heads(b1, 1, 1)
                scores(b1, 12)
                if a1[2]:
                    pe.wait_ge(S["pos2_ready"][1], count("pos2_ready", a1, 4, 4))
                transpose_out2(a1)
                scores(b1, 13)
                for read, value in last_reader(("sum2b_ready", a0, 1, 1, 0), ("pos2_ready", a1, 4,
                        2, 0), ("pos2_ready", a0, 4, 2, 0), ("arg2_ready", a0, 4, 4, 0),
                        ("fmax2_ready", a0, 4, 4, 0), ("h2_copied", a0, 2, 2, 0), ("res1_ready", a0,
                        2, 2, 0), ("pos1_ready", a1, 4, 1, 0), ("pos1_ready", a0, 4, 1, 0),
                        ("att1_ready", a0, 4, 4, 0), ("h1_copied", a1, 4, 2, 0), ("y2_ready", b0, 1,
                        1, 1)):
                    pe.wait_ge(read, value)
                transpose_heads(b0, 0)
                scores(b1, 14)
                attend_heads(b1, 2, 0)
                scores(b1, 15)
                if a1[2]:
                    pe.wait_ge(S["sum2b_ready"][1], count("sum2b_ready", a1, 1, 1))
                transpose_x1(a0)
                for read, value in last_reader(("arg2_ready", a1, 4, 4, 0), ("low2_ready", a0, 4, 4,
                        0), ("res1_ready", a1, 2, 2, 0), ("res1_ready", a1, 2, 1, 0), ("h2_copied",
                        a0, 2, 1, 0), ("out2_ready", a0, 1, 1, 0), ("res1_ready", a0, 2, 1, 0),
                        ("pos1_ready", a1, 4, 3, 0), ("pos1_ready", a0, 4, 4, 0), ("pos1_ready", a0,
                        4, 2, 0), ("low1_ready", a1, 4, 4, 0), ("fmax1_ready", a1, 1, 1, 0),
                        ("h1_copied", a1, 4, 4, 0), ("h1_copied", a1, 4, 3, 0), ("h1_copied", a1, 4,
                        1, 0), ("out1_ready", a1, 2, 2, 0), ("h1_copied", a0, 4, 2, 0),
                        ("out1_ready", a1, 2, 1, 0), ("out1_ready", a0, 2, 1, 0), ("xT_copied", a0,
                        1, 1, 0), ("vcol_ready", a1, 1, 1, 1), ("v_copied", a1, 1, 1, 1),
                        ("rest_ready", a1, 2, 2, 1), ("attn_ready", b1, 2, 1, 1)):
                    pe.wait_ge(read, value)
                transpose_heads(b0, 1)
                attend_heads(b1, 2, 1)
                if a0[2]:
                    pe.wait_ge(S["x1T_copied"][0], count("x1T_copied", a0, 1, 1))
                project_qk(a0, 0)
                for read, value in last_reader(("attn_ready", b0, 2, 2, 0), ("arg2_ready", a1, 4, 4,
                        0)):
                    pe.wait_ge(read, value)
                project_qk(a0, 1)
                attend_heads(b1, 3, 0)
                attend_heads(b1, 3, 1)
                for read, value in last_reader(("rest_ready", a0, 2, 2, 0), ("attn_ready", b0, 2, 2,
                        0)):
                    pe.wait_ge(read, value)
                transpose_heads(b1, 0)
                if a0[2]:
                    pe.wait_ge(S["rest_ready"][0], count("rest_ready", a0, 2, 1))
                project_v(a0)
                for read, value in last_reader(("attn_ready", b0, 2, 1, 0), ("sum2b_ready", a0, 1,
                        1, 0)):
                    pe.wait_ge(read, value)
                transpose_x1(a1)
                if a1[2]:
                    pe.wait_ge(S["x1T_copied"][1], count("x1T_copied", a1, 1, 1))
                project_qk(a1, 0)
                for read, value in last_reader(("attn_ready", b1, 2, 1, 0), ("rest_ready", a0, 2, 2,
                        0)):
                    pe.wait_ge(read, value)
                project_qk(a1, 1)
                for read, value in last_reader(("v_copied", a0, 1, 1, 0), ("rest_ready", a0, 2, 1,
                        0), ("x1T_copied", a0, 1, 1, 0), ("sum2b_ready", a1, 1, 1, 0),
                        ("pos2_ready", a1, 4, 4, 0), ("pos2_ready", a0, 4, 4, 0), ("low2_ready", a1,
                        4, 4, 0), ("fmax2_ready", a1, 4, 4, 0), ("h2_copied", a1, 2, 2, 0),
                        ("h2_copied", a1, 2, 1, 0), ("out2_ready", a1, 1, 1, 0), ("pos1_ready", a1,
                        4, 4, 0), ("pos1_ready", a1, 4, 2, 0), ("pos1_ready", a0, 4, 3, 0),
                        ("att1_ready", a1, 4, 4, 0), ("low1_ready", a0, 4, 4, 0), ("fmax1_ready",
                        a0, 1, 1, 0), ("h1_copied", a0, 4, 4, 0), ("h1_copied", a0, 4, 3, 0),
                        ("h1_copied", a0, 4, 1, 0), ("out1_ready", a0, 2, 2, 0), ("xT_copied", a1,
                        1, 1, 0), ("y2_ready", b1, 1, 1, 1)):
                    pe.wait_ge(read, value)
                transpose_heads(b1, 1)
                for read, value in last_reader(("rest_ready", a1, 2, 1, 0), ("x1T_copied", a1, 1, 1,
                        0), ("attn_ready", b0, 2, 1, 0)):
                    pe.wait_ge(read, value)
                transpose_y1(b0)
                for read, value in last_reader(("attn_ready", b1, 2, 2, 0), ("v_copied", a0, 1, 1,
                        0)):
                    pe.wait_ge(read, value)
                columns_of_v(a0)
                if b0[2]:
                    pe.wait_ge(S["y1T_copied"][0], count("y1T_copied", b0, 1, 1))
                feed_hidden(b0)
                if b0[2]:
                    pe.wait_ge(S["hid_ready"][0], count("hid_ready", b0, 1, 1))
                feed_out(b0)
                if a1[2]:
                    pe.wait_ge(S["rest_ready"][1], count("rest_ready", a1, 2, 2))
                project_v(a1)
                if a1[2]:
                    pe.wait_ge(S["v_copied"][1], count("v_copied", a1, 1, 1))
                columns_of_v(a1)
                for read, value in last_reader(("vcol_ready", a0, 1, 1, 0), ("attn_ready", b1, 2, 2,
                        0)):
                    pe.wait_ge(read, value)
                transpose_y1(b1)
                if b1[2]:
                    pe.wait_ge(S["y1T_copied"][1], count("y1T_copied", b1, 1, 1))
                feed_hidden(b1)
                if b1[2]:
                    pe.wait_ge(S["hid_ready"][1], count("hid_ready", b1, 1, 1))
                feed_out(b1)
            rounds(pe, one_round)


_INS = ["x", "adj", "L0_gnn_mlp1_w", "L0_gnn_mlp1_b", "L0_gnn_mlp2_w", "L0_gnn_mlp2_b", "L0_gnn_W_fc",
        "L0_gnn_a_fc", "L0_gnn_W_hand", "L0_gnn_a_hand", "L1_gnn_w_qkv", "L1_gnn_ln1_g", "L1_gnn_ln1_b",
        "L1_gnn_ln2_g", "L1_gnn_ln2_b", "L1_gnn_w1", "L1_gnn_b1", "L1_gnn_w2", "L1_gnn_b2"]


def kernel(**inputs):
    import numpy as _np
    import concourse.bacc as _bacc
    from concourse.bass_utils import run_bass_kernel_spmd as _run

    nc = _bacc.Bacc("TRN2", target_bir_lowering=False, num_devices=1)
    arrays, args = {}, []
    for name in _INS:
        a = _np.ascontiguousarray(inputs[name])
        arrays[f"in_{name}_dram"] = a
        args.append(nc.dram_tensor(f"in_{name}_dram", a.shape, mybir.dt.from_np(a.dtype),
                                   kind="ExternalInput").ap())
    out = nc.dram_tensor("out_dram", (B, N, C), F32, kind="ExternalOutput").ap()
    gnn_kernel(nc, *args, out)
    r = _run(nc, [arrays], core_ids=[0])
    return r.results[0]["out_dram"]
```

```python
from contextlib import ExitStack

import concourse.bass as bass
from concourse import mybir

P = 128
B, N, C = 16, 512, 128
T = N // P
H = 256
HC = H // P
PAIRS = B // 2
HEADS, D = 8, 16
GROUPS, GH = 2, 4
STRIP = 32
ALPHA = 0.2
EPS = 1e-5
SCALE = D ** -0.5
NEG = -2.0 ** 100
Q_TERMS = (0, 1, 2, 0, 1, 0)
K_TERMS = (0, 0, 0, 1, 1, 2)
KP = len(Q_TERMS) * D
KS = KP + 3
SAFE_SCORE = 75.0
TRACE_LIMIT = (SAFE_SCORE / (SCALE * C)) ** 16

PE_MASKED = (1, 3, 4, 6, 7, 9, 11, 12, 14, 15)
DVE_MASKED = tuple(k for k in range(16) if k not in PE_MASKED)
MASKED_BY_DVE = len(DVE_MASKED)
SIDE = {
    "xT": (0, 1), "out1_0": (0, 0), "out1_1": (1, 0), "h1_0": (1, 0), "h1_1": (1, 0), "h1_2": (1,
    1), "h1_3": (2, 0), "f1_rows": (2, 0), "A_rows": (1, 0), "C_rows": (2, 2), "gat1_0": (1, 0),
    "gat1_1": (2, 2), "gat1_2": (1, 1), "gat1_3": (0, 2), "gat1T_0": (1, 2), "gat1T_1": (2, 0),
    "out2": (1, 1), "h2_0": (1, 1), "h2_1": (1, 0), "f2_rows": (2, 0), "R1_rows": (2, 0), "R2_rows":
    (1, 2), "gat2_0": (1, 2), "gat2_1": (2, 1), "out2T": (0, 2), "x1T": (2, 2), "q": (2, 2), "k":
    (2, 1), "v": (2, 1), "vcol": (0, 1), "oT_0": (0, 0), "oT_1": (1, 2), "y1T": (1, 0), "hid": (1,
    0), "ff": (1, 2),
}


INTERLEAVED = ("x_loaded", "parts_stored", "stacked", "stored", "gat1_made", "gat1_ready", "h1_copied",
               "h1_made", "low_ready", "mid_ready", "neg1_ready", "pos1_ready", "rz1_ready", "u1_ready",
               "w1_ready", "y1n_ready")


def masked_so_far(k):
    return sum(j <= k for j in DVE_MASKED)


ALU = mybir.AluOpType
ACT = mybir.ActivationFunctionType
F32 = mybir.dt.float32
BF16 = mybir.dt.bfloat16
I32 = mybir.dt.int32
AX_X = mybir.AxisListType.X


def gnn_kernel(nc, x, adj, mlp1_w, mlp1_b, mlp2_w, mlp2_b, W_fc, a_fc, W_hand, a_hand,
               w_qkv, ln1_g, ln1_b, ln2_g, ln2_b, w1, b1, w2, b2, out):
    x_dram = x.rearrange("b (p t) c -> b p t c", t=T)
    out_dram = out.rearrange("b (p t) c -> b p t c", t=T)
    split_dram = nc.dram_tensor("qk_split_dram", (2, 2, 3, HEADS, D, N), BF16).ap()
    shift_dram = nc.dram_tensor("shift_dram", (2, 3, HEADS, T, P), BF16).ap()

    with ExitStack() as ctx:
        def sb(name, shape, dt=F32):
            return ctx.enter_context(nc.sbuf_tensor(name, shape, dt))

        def psum(name, shape, dt=F32):
            return ctx.enter_context(nc.psum_tensor(name, shape, dt))

        def sem(name):
            return ctx.enter_context(nc.semaphore(name))

        def pair(name, shape, dt=F32):
            return [sb(f"{name}_{p}", shape, dt) for p in range(2)]

        ident = sb("ident", [P, P])
        ident_bf = sb("ident_bf", [P, P], BF16)
        ones = sb("ones", [P, 1])
        minus_half = sb("minus_half", [P, T])
        minus_one = sb("minus_one", [P, 1])
        zero_b = sb("zero_b", [P, 1])
        neg_nat = sb("neg_nat", [P, T, N], BF16)
        neg_T = sb("neg_T", [P, T, N], BF16)
        row_count = sb("row_count", [P, T])
        occupied = sb("occupied", [P, T])
        empty = sb("empty", [P, T])
        empty_b = sb("empty_b", [P, N])
        W1 = sb("W1", [P, H])
        b1c = sb("b1c", [P, HC])
        Wfc = sb("Wfc", [P, HC, 2 + H])
        W2 = sb("W2", [P, HC, C])
        b2c = sb("b2c", [P, 1])
        Wh = sb("Wh", [P, 2 + C])
        Wqkv = sb("Wqkv", [P, 3 * C])
        M1 = sb("M1", [P, C])
        m1c = sb("m1c", [P, 1])
        M2 = sb("M2", [P, C])
        g1c = sb("g1c", [P, 1])
        be1c = sb("be1c", [P, 1])
        g1_b = sb("g1_b", [P, C])
        be1_b = sb("be1_b", [P, C])
        g2_b = sb("g2_b", [P, C])
        be2_b = sb("be2_b", [P, C])
        m2_b = sb("m2_b", [P, C])

        x_nat = pair("x_nat", [P, T, C])
        xT = pair("xT", [P, N])
        y0 = [xT[p][:, :].rearrange("p (t c) -> p t c", t=T) for p in range(2)]
        out1 = pair("out1", [P, HC, N])
        h1 = pair("h1", [P, T, 2 + H + 1])
        h2 = pair("h2", [P, T, 2 + C + 1])
        fmax1 = pair("fmax1", [P, 1])
        arg1 = pair("arg1", [P, 4, T])
        fac1 = pair("fac1", [P, 4, T])
        low = pair("low", [P, T, N])
        att = pair("att", [P, T, N])
        rz1 = pair("rz1", [P, T])
        neg1 = pair("neg1", [P, T, H])
        pos1 = pair("pos1", [P, T, H])
        out2 = pair("out2", [P, N])
        fmax2 = pair("fmax2", [P, T])
        s2 = pair("s2", [P, T])
        m2 = pair("m2", [P, T])
        row2 = pair("row2", [P, 2, T])
        f2s = pair("f2s", [P, T])
        rz2 = pair("rz2", [P, T])
        neg2 = [neg1[p][:, 0:2, :].rearrange("p a (b c) -> p (a b) c", c=C) for p in range(2)]
        pos2 = [pos1[p][:, 0:2, :].rearrange("p a (b c) -> p (a b) c", c=C) for p in range(2)]
        x1 = pair("x1", [P, T, C])
        x1T = out2
        qk_parts = [att[p][:, 0:3, :].bitcast(BF16).rearrange("p s (i n) -> p i s n", i=2) for p in range(2)]
        qk_rest = low
        in_range = sb("in_range", [P, 1], I32)
        row_max = pair("row_max", [P, HEADS, T])
        shift_rest = pair("shift_rest", [P, HEADS, T])
        shift_parts = pair("shift_parts", [P, 3, HEADS, T], BF16)
        Qs = pair("Qs", [KS, HEADS, N], BF16)
        Ks = pair("Ks", [KS, HEADS, N], BF16)
        v = pair("v", [P, T, GROUPS, GH, STRIP])
        Wv_strips = sb("Wv_strips", [P, GROUPS, P])
        ones_sum = sb("ones_sum", [P, GROUPS])
        strip_one = sb("strip_one", [P, 1])
        x1_sum = pair("x1_sum", [P, 1])
        vcol = pair("vcol", [P, GROUPS])
        probs = sb("probs", [P, 2, GH, 2, N])
        oT = sb("oT", [P, GROUPS, N])
        rzh = pair("rzh", [P, GROUPS, T, GH])
        attn = pair("attn", [P, T, C])
        y1n = pair("y1n", [P, T, C])
        xc = pair("xc", [P, T, C])
        y1T = pair("y1T", [P, N])
        hid = pair("hid", [P, N])
        stat = [pair(f"stat{i}", [P, T, 6]) for i in range(4)]
        mv = [pair(f"mv{i}", [P, T, 2]) for i in range(4)]
        var = [pair(f"var{i}", [P, T]) for i in range(4)]
        rstd = [pair(f"rstd{i}", [P, T]) for i in range(4)]
        same_head = probs[:, 0, 0, 0, 0:P]
        head_of = probs[:, 0, 0, 0, P:P + HEADS]
        trace = probs[:, 0, 0, 0, 2 * P:2 * P + 2]
        head_ok = probs[:, 0, 0, 0, 2 * P + 2:2 * P + 3]
        all_ok = probs[:, 0, 0, 0, 2 * P + 3:2 * P + 4]
        gram = probs[:, 0, 1, 0, 0:2 * P].rearrange("p (i c) -> p i c", i=2)
        neg_f32 = low[1]
        adj_i = low[0][:, :, :].bitcast(I32)
        mask_nat = att[0]
        a_fc_b = att[1][:, 0, :]
        a_hand_b = att[1][:, 1, 0:2 * C]
        wa_tmp = att[1][:, 2, 0:H]

        sc = [psum(f"sc{i}", [P, 2, N]) for i in range(2)]
        oacc = psum("oacc", [P, N])
        bank = [psum(f"side{i}", [P, N]) for i in range(3)]

        adj_loaded = sem("adj_loaded")
        w_loaded = sem("w_loaded")
        const_set = sem("const_set")
        prep = sem("prep")
        adj_T = sem("adj_T")
        bound_made = sem("bound_made")
        bound_step = sem("bound_step")
        row_scores_made = sem("row_scores_made")
        row_max_taken = sem("row_max_taken")
        shift_step = sem("shift_step")
        shift_stored = sem("shift_stored")
        shift_loaded = sem("shift_loaded")
        waits_passed = sem("waits_passed")
        dve_const_set = sem("dve_const_set")
        names = """x_loaded xT_made xT_copied out1_made out1_ready h1_made h1_copied f1b_made fmax1_ready
        arg1_ready fac1_ready rows1_made low1_ready att1_ready gat1_made rz1_ready neg1_ready
        pos1_ready u1_ready w1_ready gat1_ready gat1T_made res1_ready out2_made out2_ready h2_made h2_copied
        f2b_made fmax2_ready s2_ready row2_ready rows2_made low2_ready arg2_ready argm0_ready argm1_ready f2s_ready
        att2_ready gat2_made rz2_ready neg2_ready pos2_ready u2_ready w2_ready sum2_ready
        out2T_made sum2b_ready y0_ready x1_ready x1T_made x1T_copied q_made k_made v_made high_ready rest_ready
        mid_ready low_ready parts_stored stacked v_copied vcol_made vcol_ready
        scores_made masked_ready probs_ready pv_made oT_ready oTT_made rzh_ready attn_ready xc_ready y1_ready
        y1n_ready y1g_ready y1m_ready y1T_made y1T_copied hid_made hid_ready ff_made y2_ready
        y2n_ready y2g_ready x1b_ready y3_ready o_ready stored""".split()
        S = {name: [sem(f"{name}_{p}") for p in range(2)] if name in INTERLEAVED else [sem(name)] * 2
             for name in names}
        ln_step = [sem(f"ln{i}_step") for i in range(4)]
        ln_rstd = [sem(f"ln{i}_rstd") for i in range(4)]

        def passed(b, per, k):
            return (2 * b[0] + b[1]) * per + k

        def count(name, b, per=1, k=None):
            k = per if k is None else k
            return b[0] * per + k if name in INTERLEAVED else passed(b, per, k)

        def has_former(b):
            return not isinstance(b[0], int) or b[0] > 0

        def former(b):
            return (b[0] - 1, b[1])

        def probs_readers(b, unit):
            if unit >= 2:
                return [(S["pv_made"][b[1]], count("pv_made", b, 4, unit - 1))]
            if b[1]:
                return [(S["pv_made"][0], count("pv_made", (b[0], 0), 4, unit + 3))]
            if has_former(b):
                return [(S["pv_made"][1], count("pv_made", (b[0] - 1, 1), 4, unit + 3))]
            return []

        block = ctx.enter_context(nc.Block())

        def bc(ap, shape):
            return ap.to_broadcast(shape)

        def live(stage):
            return lambda b, *more: stage(b, *more) if b[2] else None

        def batches(r):
            return [[(r - k, p, not isinstance(r, int) or 0 <= r - k < PAIRS) for p in range(2)]
                    for k in range(3)]

        def rounds(eng, one_round, after_first=lambda: None):
            for r in range(3):
                one_round(*batches(r))
                if r == 0:
                    after_first()
            with eng.Fori(3, PAIRS) as r:
                one_round(*batches(r))
            for r in (PAIRS, PAIRS + 1):
                one_round(*batches(r))

        def row(ap):
            return ap.rearrange("(o n) -> o n", o=1).broadcast_to((P, C))

        def column(ap):
            return ap.rearrange("(p o) -> p o", o=1)

        weights = [(W1[:, :], mlp1_w), (b1c[:, 0:1], column(mlp1_b[0:P])), (b1c[:, 1:2], column(mlp1_b[P:H])),
                   (Wfc[:, :, 2:2 + H], W_fc.rearrange("(k p) n -> p k n", p=P)),
                   (W2[:, :, :], mlp2_w.rearrange("(k p) n -> p k n", p=P)), (b2c[:, :], column(mlp2_b)),
                   (Wh[:, 2:2 + C], W_hand),
                   (a_fc_b, a_fc.rearrange("a o -> o a").broadcast_to((P, 2 * H))),
                   (a_hand_b, a_hand.rearrange("a o -> o a").broadcast_to((P, 2 * C))),
                   (Wqkv[:, :], w_qkv), (M1[:, :], w1), (M2[:, :], w2), (m1c[:, :], column(b1)),
                   (g1c[:, :], column(ln1_g)), (be1c[:, :], column(ln1_b)),
                   (g1_b[:, :], row(ln1_g)), (be1_b[:, :], row(ln1_b)), (g2_b[:, :], row(ln2_g)),
                   (be2_b[:, :], row(ln2_b)), (m2_b[:, :], row(b2))]
        W_ALL = 16 * len(weights)
        PREP = 4 * HC + 4 + 8 + 2 * T + 1 + T + 1
        BOUND_STEPS = 11
        PREP_T = 4 + 2 * T + 1

        def batch_of(ap, b):
            return ap[bass.ds(2 * b[0] + b[1], 1), :, :, :].rearrange("o p t c -> (o p) t c")

        @block.sync
        def _(sp):
            def load_x(r, p):
                if not isinstance(r, int) or r:
                    if has_former((r, p)):
                        sp.wait_ge(S["y0_ready"][p], count("y0_ready", former((r, p))))
                sp.dma_start(x_nat[p][:, :, :], batch_of(x_dram, (r, p))).then_inc(S["x_loaded"][p], 16)

            @live
            def stack_qk(a):
                p = a[1]
                sp.wait_ge(S["high_ready"][p], count("high_ready", a, 2))
                sp.wait_ge(S["mid_ready"][p], count("mid_ready", a, 2))
                sp.wait_ge(S["low_ready"][p], count("low_ready", a, 2))
                for i in range(2):
                    sp.dma_start(split_dram[p, i].rearrange("s h d n -> (h d) s n"),
                                 qk_parts[p][:, i, :, :]).then_inc(S["parts_stored"][p], 16)
                sp.wait_ge(S["parts_stored"][p], count("parts_stored", a, 32))
                if has_former(a):
                    sp.wait_ge(S["scores_made"][p], count("scores_made", former(a), 16))
                for i, (dst, terms) in enumerate(((Qs[p], Q_TERMS), (Ks[p], K_TERMS))):
                    for r, part in enumerate(terms):
                        sp.dma_start(dst[r * D:(r + 1) * D, :, :],
                                     split_dram[p, i, part].rearrange("h d n -> d h n")
                                     ).then_inc(S["stacked"][p], 16)

            @live
            def store_out(b):
                sp.wait_ge(S["o_ready"][p], count("o_ready", b, 2))
                sp.dma_start(batch_of(out_dram, b), y1n[b[1]][:, :, :]).then_inc(S["stored"][b[1]], 16)

            sp.dma_start(adj_i, adj.rearrange("(p t) j -> p t j", t=T)).then_inc(adj_loaded, 16)
            for p in range(2):
                load_x(0, p)
            for dst, src in weights[0::2]:
                sp.dma_start(dst, src).then_inc(w_loaded, 16)

            def load_range():
                sp.wait_ge(bound_step, BOUND_STEPS)
                range_known.append(sp.value_load(in_range[0:1, 0:1], min_val=0, max_val=1))

            def shift_both(a):
                if a[0][2]:
                    with sp.If(range_known[0] < 1):
                        for b in a:
                            p = b[1]
                            sp.wait_ge(shift_step, passed(b, 6, 6))
                            for i in range(3):
                                sp.dma_start(shift_dram[p, i].rearrange("h t p -> p h t"),
                                             shift_parts[p][:, i, :, :], allow_slow_non_contiguous=True
                                             ).then_inc(shift_stored, 16)
                            sp.wait_ge(shift_stored, passed(b, 48, 48))
                            sp.dma_start(Qs[p][KP:KS, :, :], shift_dram[p].rearrange("s h t p -> s h (t p)")
                                         ).then_inc(shift_loaded, 16)

            range_known = []

            def one_round(a, b, c, last_load=False):
                for p in range(2):
                    store_out(c[p])
                for p in range(2):
                    if a[p][2] and not last_load:
                        load_x(a[p][0] + 1, p)
                for p in range(2):
                    stack_qk(a[p])
                if range_known:
                    shift_both(a)

            for r in range(3):
                one_round(*batches(r))
                if r == 0:
                    load_range()
                    shift_both(batches(r)[0])
            with sp.Fori(3, PAIRS - 1) as r:
                one_round(*batches(r))
            one_round(*batches(PAIRS - 1), last_load=True)
            for r in (PAIRS, PAIRS + 1):
                one_round(*batches(r))
            for p in range(2):
                sp.wait_ge(S["stored"][p], 16 * PAIRS)

        @block.gpsimd
        def _(pool):
            nc.gpsimd.memset(ident[:, :], 0.0).then_inc(const_set, 1)
            pool.wait_ge(const_set, 1)
            nc.gpsimd.affine_select(out=ident[:, :], in_=ident[:, :], compare_op=ALU.not_equal, fill=1.0,
                                    base=0, pattern=[[-1, P]], channel_multiplier=1).then_inc(const_set, 1)
            nc.gpsimd.memset(ones[:, :], 1.0).then_inc(const_set, 1)
            nc.gpsimd.memset(minus_half[:, :], -0.5).then_inc(const_set, 1)
            for p in range(2):
                nc.gpsimd.memset(h1[p][:, :, 2 + H:], 1.0).then_inc(const_set, 1)
                nc.gpsimd.memset(h2[p][:, :, 2 + C:], 1.0).then_inc(const_set, 1)
                nc.gpsimd.memset(v[p][:, :, :, :, :], 0.0).then_inc(const_set, 1)
            nc.gpsimd.memset(Wv_strips[:, :, :], 0.0).then_inc(const_set, 1)
            pool.wait_ge(const_set, 11)
            for p in range(2):
                nc.gpsimd.memset(v[p][:, :, :, :, D:D + 1], 1.0).then_inc(const_set, 1)
            pool.wait_ge(const_set, 13)
            nc.gpsimd.tensor_copy(ident_bf[:, :], ident[:, :]).then_inc(const_set, 1)
            for p in range(2):
                pool.wait_ge(const_set, 14 + 2 * p)
                nc.gpsimd.memset(Qs[p][KP:KS, :, :], 0.0).then_inc(const_set, 1)
                pool.wait_ge(const_set, 15 + 2 * p)
                nc.gpsimd.memset(Ks[p][KP:KS, :, :], 1.0).then_inc(const_set, 1)
            pool.wait_ge(w_loaded, W_ALL)
            pool.wait_ge(prep, PREP)

            @live
            def finish_gat1(a, h):
                p = a[1]
                pool.wait_ge(S["w1_ready"][p], count("w1_ready", a, 2, h + 1))
                nc.gpsimd.tensor_tensor(pos1[p][:, 2 * h:2 * h + 2, :], pos1[p][:, 2 * h:2 * h + 2, :],
                                        neg1[p][:, 2 * h:2 * h + 2, :], ALU.add
                                        ).then_inc(S["gat1_ready"][p], 1)

            @live
            def mask_arguments2(a):
                p = a[1]
                pool.wait_ge(S["arg2_ready"][p], count("arg2_ready", a, T, 2))
                nc.gpsimd.tensor_tensor(low[p][:, 0:2, :], low[p][:, 0:2, :], neg_T[:, 0:2, :], ALU.add
                                        ).then_inc(S["argm0_ready"][p], 1)

            @live
            def inverse_deviation(b, i):
                p = b[1]
                pool.wait_ge(ln_step[i], passed(b, 2 * T, 2 * T))
                pool.sem_inc(waits_passed, 1)
                nc.gpsimd.tensor_scalar(var[i][p][:, :], mv[i][p][:, :, 1], EPS, None, ALU.add
                                        ).then_inc(ln_rstd[i], 1)
                pool.wait_ge(ln_rstd[i], passed(b, 2, 1))
                nc.gpsimd.tensor_tensor(rstd[i][p][:, :], var[i][p][:, :], minus_half[:, :], ALU.pow
                                        ).then_inc(ln_rstd[i], 1)

            @live
            def low_part(a, i):
                p = a[1]
                pool.wait_ge(S["mid_ready"][p], count("mid_ready", a, 2, i + 1))
                nc.gpsimd.tensor_tensor(qk_parts[p][:, i, 2, :], qk_rest[p][:, i, :],
                                        qk_parts[p][:, i, 1, :], ALU.subtract
                                        ).then_inc(S["low_ready"][p], 1)

            def over_tiles(row):
                return row[:, :].unsqueeze(1).to_broadcast([P, T, C])

            @live
            def keep_x1(b):
                p = b[1]
                pool.wait_ge(S["x1_ready"][p], count("x1_ready", b, 2))
                if has_former(b):
                    pool.wait_ge(S["y3_ready"][p], count("y3_ready", former(b)))
                nc.gpsimd.tensor_tensor(xc[p][:, :, :], x1[p][:, :, :],
                                        zero_b[:, :].unsqueeze(2).to_broadcast([P, T, C]), ALU.add
                                        ).then_inc(S["xc_ready"][p], 1)

            @live
            def add_bias2(b):
                p = b[1]
                pool.wait_ge(S["y1_ready"][p], count("y1_ready", b))
                nc.gpsimd.tensor_tensor(xc[p][:, :, :], xc[p][:, :, :], over_tiles(be2_b), ALU.add
                                        ).then_inc(S["x1b_ready"][p], 1)

            @live
            def affine1(b, step):
                p = b[1]
                if step == 0:
                    pool.wait_ge(S["y1T_made"][p], count("y1T_made", b))
                    nc.gpsimd.tensor_tensor(y1n[p][:, :, :], y1n[p][:, :, :], over_tiles(g1_b), ALU.mult
                                            ).then_inc(S["y1g_ready"][p], 1)
                else:
                    pool.wait_ge(S["y1g_ready"][p], count("y1g_ready", b))
                    nc.gpsimd.tensor_tensor(y1n[p][:, :, :], y1n[p][:, :, :], over_tiles(be1_b), ALU.add
                                            ).then_inc(S["y1m_ready"][p], 1)

            @live
            def affine2(b):
                p = b[1]
                pool.wait_ge(S["y2n_ready"][p], count("y2n_ready", b, 2))
                nc.gpsimd.tensor_tensor(attn[p][:, :, :], attn[p][:, :, :], over_tiles(g2_b), ALU.mult
                                        ).then_inc(S["y2g_ready"][p], 1)

            def one_round(a, b, c):
                (a0, a1), (b0, b1), (c0, c1) = a, b, c
                add_bias2(c0)
                inverse_deviation(c0, 1)
                inverse_deviation(c1, 1)
                add_bias2(c1)
                finish_gat1(a0, 0)
                finish_gat1(a1, 0)
                finish_gat1(a0, 1)
                finish_gat1(a1, 1)
                affine1(c0, 0)
                mask_arguments2(a0)
                affine1(c0, 1)
                affine1(c1, 0)
                affine1(c1, 1)
                inverse_deviation(c0, 2)
                mask_arguments2(a1)
                affine2(c0)
                keep_x1(b0)
                inverse_deviation(a0, 0)
                inverse_deviation(c1, 2)
                affine2(c1)
                inverse_deviation(a1, 0)
                keep_x1(b1)
                low_part(a0, 0)
                inverse_deviation(c0, 3)
                inverse_deviation(c1, 3)
                low_part(a1, 0)
                low_part(a0, 1)
                low_part(a1, 1)
            rounds(pool, one_round)

        @block.scalar
        def _(act):
            for dst, src in weights[1::2]:
                act.dma_start(dst, src).then_inc(w_loaded, 16)
            act.wait_ge(w_loaded, W_ALL)
            act.wait_ge(dve_const_set, 1)

            @live
            def copy_xT(a):
                p = a[1]
                act.wait_ge(S["xT_made"][p], count("xT_made", a))
                if has_former(a):
                    act.wait_ge(S["x1_ready"][p], count("x1_ready", former(a), 2))
                nc.scalar.copy(xT[p][:, :], bank[SIDE["xT"][p]][:, :]).then_inc(S["xT_copied"][p], 1)

            @live
            def relu_out1(a, f):
                p = a[1]
                act.wait_ge(S["out1_made"][p], count("out1_made", a, HC, f + 1))
                if has_former(a):
                    act.wait_ge(S["out2_made"][p], count("out2_made", former(a)))
                nc.scalar.activation(out1[p][:, f, :], bank[SIDE[f"out1_{f}"][p]][:, :], ACT.Relu,
                                     bias=b1c[:, f:f + 1]).then_inc(S["out1_ready"][p], 1)

            @live
            def copy_h1(a, t):
                p = a[1]
                act.wait_ge(S["h1_made"][p], count("h1_made", a, T, t + 1))
                if has_former(a):
                    act.wait_ge(S["gat1_made"][p], count("gat1_made", former(a), T))
                nc.scalar.copy(h1[p][:, t, 0:2 + H], bank[SIDE[f"h1_{t}"][p]][:, 0:2 + H]
                               ).then_inc(S["h1_copied"][p], 1)

            @live
            def factors1(a):
                p = a[1]
                act.wait_ge(S["arg1_ready"][p], count("arg1_ready", a, 5))
                nc.scalar.activation(fac1[p][:, :, :], arg1[p][:, :, :], ACT.Exp).then_inc(S["fac1_ready"][p], 1)

            @live
            def low_branch1(a, j):
                p = a[1]
                act.wait_ge(S["rows1_made"][p], count("rows1_made", a, 2))
                if has_former(a):
                    act.wait_ge(S["low_ready"][p], count("low_ready", former(a), 2))
                nc.scalar.activation(low[p][:, j, :], bank[SIDE["C_rows"][p]][:, :], ACT.Copy,
                                     scale=fac1[p][:, 3, j:j + 1]).then_inc(S["low1_ready"][p], 1)

            @live
            def positive1(a, t):
                p = a[1]
                act.wait_ge(S["neg1_ready"][p], count("neg1_ready", a, T, t + 1))
                nc.scalar.activation(pos1[p][:, t, :], bank[SIDE[f"gat1_{t}"][p]][:, 0:H], ACT.Relu,
                                     scale=rz1[p][:, t:t + 1]).then_inc(S["pos1_ready"][p], 1)

            @live
            def elu_twice1(a, h, step):
                p = a[1]
                tiles = neg1[p][:, 2 * h:2 * h + 2, :]
                if step == 0:
                    act.wait_ge(S["pos1_ready"][p], count("pos1_ready", a, T, 2 * h + 2))
                    nc.scalar.activation(tiles, tiles, ACT.Exp).then_inc(S["u1_ready"][p], 1)
                else:
                    act.wait_ge(S["u1_ready"][p], count("u1_ready", a, 2, h + 1))
                    nc.scalar.activation(tiles, tiles, ACT.Exp, bias=minus_one[:, 0:1]
                                         ).then_inc(S["w1_ready"][p], 1)

            @live
            def relu_out2(a):
                p = a[1]
                act.wait_ge(S["out2_made"][p], count("out2_made", a))
                if has_former(a):
                    act.wait_ge(S["v_made"][p], count("v_made", former(a)))
                nc.scalar.activation(out2[p][:, :], bank[SIDE["out2"][p]][:, :], ACT.Relu, bias=b2c[:, 0:1]
                                     ).then_inc(S["out2_ready"][p], 1)

            @live
            def copy_h2(a, i):
                p = a[1]
                src = bank[SIDE[f"h2_{i}"][p]][:, 0:2 * (C + 2)].rearrange("p (t c) -> p t c", t=2)
                act.wait_ge(S["h2_made"][p], count("h2_made", a, 2, i + 1))
                nc.scalar.copy(h2[p][:, 2 * i:2 * i + 2, 0:2 + C], src).then_inc(S["h2_copied"][p], 1)

            @live
            def low_branch2(a, j):
                p = a[1]
                act.wait_ge(S["rows2_made"][p], count("rows2_made", a, 2))
                nc.scalar.activation(low[p][:, j, :], bank[SIDE["R2_rows"][p]][:, :], ACT.Identity,
                                     bias=f2s[p][:, j:j + 1]).then_inc(S["low2_ready"][p], 1)

            @live
            def exp_att2(a, h):
                p = a[1]
                act.wait_ge(S[f"argm{h}_ready"][p], count(f"argm{h}_ready", a))
                nc.scalar.activation(att[p][:, 2 * h:2 * h + 2, :], low[p][:, 2 * h:2 * h + 2, :], ACT.Exp
                                     ).then_inc(S["att2_ready"][p], 1)

            @live
            def positive2(a, i):
                p = a[1]
                act.wait_ge(S["neg2_ready"][p], count("neg2_ready", a, T, 2 * i + 2))
                for k in range(2):
                    t = 2 * i + k
                    nc.scalar.activation(pos2[p][:, t, :], bank[SIDE[f"gat2_{i}"][p]][:, k * (C + 1):k * (C + 1) + C],
                                         ACT.Relu, scale=rz2[p][:, t:t + 1]).then_inc(S["pos2_ready"][p], 1)

            @live
            def elu_twice2(a, step):
                p = a[1]
                if step == 0:
                    act.wait_ge(S["pos2_ready"][p], count("pos2_ready", a, T))
                    nc.scalar.activation(neg2[p], neg2[p], ACT.Exp).then_inc(S["u2_ready"][p], 1)
                else:
                    act.wait_ge(S["u2_ready"][p], count("u2_ready", a))
                    nc.scalar.activation(neg2[p], neg2[p], ACT.Exp, bias=minus_one[:, 0:1]
                                         ).then_inc(S["w2_ready"][p], 1)

            @live
            def copy_x1T(a):
                p = a[1]
                act.wait_ge(S["x1T_made"][p], count("x1T_made", a))
                if has_former(a):
                    act.wait_ge(S["vcol_made"][p], count("vcol_made", former(a)))
                nc.scalar.activation(x1T[p][:, :], bank[SIDE["x1T"][p]][:, :], ACT.Copy,
                                     accum_out=x1_sum[p][:, 0:1]).then_inc(S["x1T_copied"][p], 1)

            @live
            def high_part(a, i):
                p = a[1]
                act.wait_ge(S[("q_made", "k_made")[i]][p], count(("q_made", "k_made")[i], a))
                nc.scalar.copy(qk_parts[p][:, i, 0, :], bank[SIDE["qk"[i]][p]][:, :]
                               ).then_inc(S["high_ready"][p], 1)

            @live
            def copy_v(a):
                p = a[1]
                act.wait_ge(S["v_made"][p], count("v_made", a))
                if has_former(a):
                    act.wait_ge(S["pv_made"][p], count("pv_made", former(a), 4))
                nc.scalar.copy(v[p][:, :, :, :, 0:D].rearrange("p t g h d -> p t (g h) d"),
                               bank[SIDE["v"][p]][:, :].rearrange("p (t e d) -> p t e d", t=T, d=D)
                               ).then_inc(S["v_copied"][p], 1)

            @live
            def exp_scores(b, k):
                p, unit, s = b[1], k // GH, k % GH
                if k in PE_MASKED:
                    act.wait_ge(S["scores_made"][p], count("scores_made", b, 16, k + 1))
                    src = sc[k % 2][:, :, :]
                else:
                    act.wait_ge(S["masked_ready"][p], count("masked_ready", b, MASKED_BY_DVE, masked_so_far(k)))
                    src = probs[:, unit % 2, s, :, :]
                if s == 0:
                    for made, value in probs_readers(b, unit):
                        act.wait_ge(made, value)
                nc.scalar.activation(probs[:, unit % 2, s, :, :], src, ACT.Exp,
                                     scale=SCALE).then_inc(S["probs_ready"][p], 1)

            @live
            def copy_y1T(b):
                p = b[1]
                act.wait_ge(S["y1T_made"][p], count("y1T_made", b))
                nc.scalar.activation(y1T[p][:, :], bank[SIDE["y1T"][p]][:, :], ACT.Identity,
                                     scale=g1c[:, 0:1], bias=be1c[:, 0:1]).then_inc(S["y1T_copied"][p], 1)

            @live
            def relu_hid(b):
                p = b[1]
                act.wait_ge(S["hid_made"][p], count("hid_made", b))
                nc.scalar.activation(hid[p][:, :], bank[SIDE["hid"][p]][:, :], ACT.Relu, bias=m1c[:, 0:1]
                                     ).then_inc(S["hid_ready"][p], 1)

            def one_round(a, b, c):
                (a0, a1), (b0, b1), (c0, c1) = a, b, c
                copy_xT(a0)
                copy_xT(a1)
                relu_out1(a0, 0)
                relu_out1(a0, 1)
                relu_out1(a1, 0)
                copy_h1(a0, 0)
                relu_out1(a1, 1)
                copy_h1(a0, 1)
                copy_h1(a0, 2)
                copy_h1(a1, 0)
                copy_h1(a0, 3)
                copy_h1(a1, 1)
                copy_h1(a1, 2)
                factors1(a0)
                copy_h1(a1, 3)
                low_branch1(a0, 0)
                low_branch1(a0, 1)
                factors1(a1)
                low_branch1(a0, 2)
                low_branch1(a0, 3)
                low_branch1(a1, 0)
                low_branch1(a1, 1)
                low_branch1(a1, 2)
                low_branch1(a1, 3)
                exp_scores(b0, 0)
                positive1(a0, 0)
                positive1(a0, 1)
                elu_twice1(a0, 0, 0)
                elu_twice1(a0, 0, 1)
                positive1(a1, 0)
                exp_scores(b0, 1)
                positive1(a0, 2)
                positive1(a1, 1)
                elu_twice1(a1, 0, 0)
                elu_twice1(a1, 0, 1)
                positive1(a0, 3)
                elu_twice1(a0, 1, 0)
                elu_twice1(a0, 1, 1)
                positive1(a1, 2)
                exp_scores(b0, 2)
                positive1(a1, 3)
                exp_scores(b0, 3)
                elu_twice1(a1, 1, 0)
                exp_scores(b0, 4)
                elu_twice1(a1, 1, 1)
                relu_out2(a0)
                exp_scores(b0, 5)
                copy_h2(a0, 0)
                exp_scores(b0, 6)
                copy_h2(a0, 1)
                exp_scores(b0, 7)
                relu_out2(a1)
                exp_scores(b0, 8)
                copy_h2(a1, 0)
                exp_scores(b0, 9)
                copy_h2(a1, 1)
                low_branch2(a0, 0)
                exp_scores(b0, 10)
                low_branch2(a0, 1)
                low_branch2(a0, 2)
                low_branch2(a0, 3)
                exp_scores(b0, 11)
                copy_y1T(c0)
                exp_scores(b0, 12)
                copy_y1T(c1)
                relu_hid(c0)
                exp_att2(a0, 0)
                low_branch2(a1, 0)
                exp_scores(b0, 13)
                exp_att2(a0, 1)
                low_branch2(a1, 1)
                low_branch2(a1, 2)
                low_branch2(a1, 3)
                exp_scores(b0, 14)
                exp_scores(b0, 15)
                positive2(a0, 0)
                exp_att2(a1, 0)
                positive2(a0, 1)
                exp_att2(a1, 1)
                elu_twice2(a0, 0)
                relu_hid(c1)
                elu_twice2(a0, 1)
                exp_scores(b1, 0)
                exp_scores(b1, 1)
                positive2(a1, 0)
                exp_scores(b1, 2)
                exp_scores(b1, 3)
                exp_scores(b1, 4)
                positive2(a1, 1)
                elu_twice2(a1, 0)
                elu_twice2(a1, 1)
                exp_scores(b1, 5)
                exp_scores(b1, 6)
                exp_scores(b1, 7)
                copy_x1T(a0)
                exp_scores(b1, 8)
                high_part(a0, 0)
                exp_scores(b1, 9)
                high_part(a0, 1)
                exp_scores(b1, 10)
                exp_scores(b1, 11)
                exp_scores(b1, 12)
                copy_x1T(a1)
                exp_scores(b1, 13)
                exp_scores(b1, 14)
                high_part(a1, 0)
                exp_scores(b1, 15)
                high_part(a1, 1)
                copy_v(a0)
                copy_v(a1)
            rounds(act, one_round)

        @block.vector
        def _(dve):
            nc.vector.memset(minus_one[:, :], -1.0).then_inc(dve_const_set, 1)
            nc.vector.memset(zero_b[:, :], 0.0).then_inc(dve_const_set, 1)
            dve.wait_ge(dve_const_set, 2)
            dve.wait_ge(adj_loaded, 16)
            chain = [0]

            def link(ins):
                ins.then_inc(prep, 1)
                chain[0] += 1
                dve.wait_ge(prep, chain[0])

            link(nc.vector.tensor_scalar(mask_nat[:, :, :], adj_i, 0.0, None, ALU.is_gt))
            link(nc.vector.tensor_reduce(row_count[:, :], mask_nat[:, :, :], AX_X, ALU.add))
            link(nc.vector.tensor_scalar(empty[:, :], row_count[:, :], 0.5, None, ALU.is_lt))
            link(nc.vector.tensor_scalar(occupied[:, :], empty[:, :], -1.0, 1.0, ALU.mult, ALU.add))
            for t in range(T):
                link(nc.vector.tensor_scalar(
                    neg_f32[:, t, :].rearrange("p (u q) -> p u q", u=T),
                    mask_nat[:, t, :].rearrange("p (q u) -> p u q", u=T), -NEG, NEG, ALU.mult, ALU.add))
            for t in range(T):
                link(nc.vector.tensor_scalar(neg_nat[:, t, :], neg_f32[:, t, :], occupied[:, t:t + 1], None,
                                             ALU.mult))
            link(nc.vector.memset(fmax1[0][:, :], 0.0))
            for k in range(T + 1):
                dve.wait_ge(adj_T, k + 1)
                dst = neg_T[:, k, :] if k < T else empty_b[:, :]
                nc.vector.tensor_copy(dst, bank[k % 3][:, :]).then_inc(prep, 1)
            chain[0] += T + 1
            dve.wait_ge(w_loaded, W_ALL)
            dve.wait_ge(const_set, 14)
            for W, a, width, ks in ((Wfc, a_fc_b, H, range(HC)), (Wh, a_hand_b, C, (None,))):
                for k in ks:
                    Wk = W[:, :] if k is None else W[:, k, :]
                    for side in range(2):
                        link(nc.vector.tensor_tensor(wa_tmp, Wk[:, 2:2 + width],
                                                     a[:, side * width:(side + 1) * width], ALU.mult)
                             if width == H else
                             nc.vector.tensor_tensor(wa_tmp[:, 0:width], Wk[:, 2:2 + width],
                                                     a[:, side * width:(side + 1) * width], ALU.mult))
                        link(nc.vector.tensor_reduce(Wk[:, side:side + 1], wa_tmp[:, 0:width], AX_X, ALU.add))
            link(nc.vector.tensor_tensor(be1_b[:, :], be1_b[:, :], m2_b[:, :], ALU.add))
            link(nc.vector.tensor_copy(
                Wv_strips[:, :, :].rearrange("p g (h s) -> p (g h) s", s=STRIP)[:, :, 0:D],
                Wqkv[:, 2 * C:3 * C].rearrange("p (e d) -> p e d", d=D)))
            link(nc.vector.tensor_reduce(strip_one[:, :], ident[:, D:P:STRIP], AX_X, ALU.add))
            link(nc.vector.tensor_scalar(ones_sum[:, :], strip_one[:, :].to_broadcast([P, GROUPS]), float(N), None,
                                         ALU.mult))
            assert chain[0] == PREP
            dve.wait_ge(prep, PREP)
            nc.vector.tensor_reduce(head_of, ident[:, :].rearrange("p (h d) -> p h d", d=D), AX_X, ALU.add
                                    ).then_inc(bound_step, 1)
            dve.wait_ge(bound_step, 1)
            nc.vector.tensor_copy(same_head.rearrange("p (h d) -> p h d", d=D),
                                  head_of.unsqueeze(2).to_broadcast([P, HEADS, D])).then_inc(bound_step, 1)
            dve.wait_ge(bound_step, 2)

            @live
            def arguments1(a):
                p = a[1]
                g = arg1[p]
                dve.wait_ge(S["f1b_made"][p], count("f1b_made", a))
                nc.vector.reduce_max(fmax1[p][:, :], bank[SIDE["f1_rows"][p]][:, :], AX_X
                                     ).then_inc(S["fmax1_ready"][p], 1)
                dve.wait_ge(S["fmax1_ready"][p], count("fmax1_ready", a))
                nc.vector.tensor_scalar(g[:, 0, :], h1[p][:, :, 0], fmax1[p][:, 0:1], 1.0 - ALPHA,
                                        ALU.add, ALU.mult).then_inc(S["arg1_ready"][p], 1)
                nc.vector.tensor_scalar(g[:, 1, :], h1[p][:, :, 1], fmax1[p][:, 0:1], None,
                                        ALU.subtract).then_inc(S["arg1_ready"][p], 1)
                dve.wait_ge(S["arg1_ready"][p], count("arg1_ready", a, 5, 2))
                nc.vector.tensor_scalar(g[:, 2, :], g[:, 0, :], -1.0, 0.0, ALU.mult, ALU.min
                                        ).then_inc(S["arg1_ready"][p], 1)
                nc.vector.tensor_scalar(g[:, 3, :], g[:, 1, :], ALPHA, None, ALU.mult
                                        ).then_inc(S["arg1_ready"][p], 1)
                dve.wait_ge(S["arg1_ready"][p], count("arg1_ready", a, 5, 3))
                nc.vector.tensor_scalar(g[:, 0, :], g[:, 0, :], 0.0, None, ALU.min
                                        ).then_inc(S["arg1_ready"][p], 1)

            @live
            def weights1(a, j):
                p = a[1]
                dve.wait_ge(S["low1_ready"][p], count("low1_ready", a, T, j + 1))
                if j == 0:
                    if has_former(a):
                        dve.wait_ge(S["parts_stored"][p], count("parts_stored", former(a), 32))
                nc.vector.scalar_tensor_tensor(att[p][:, j, :], bank[SIDE["A_rows"][p]][:, :],
                                               fac1[p][:, 1, j:j + 1], low[p][:, j, :], ALU.mult, ALU.max
                                               ).then_inc(S["att1_ready"][p], 1)

            @live
            def normalise1(a, t):
                p = a[1]
                ps = bank[SIDE[f"gat1_{t}"][p]]
                dve.wait_ge(S["gat1_made"][p], count("gat1_made", a, T, t + 1))
                nc.vector.reciprocal(rz1[p][:, t:t + 1], ps[:, H:H + 1]).then_inc(S["rz1_ready"][p], 1)
                dve.wait_ge(S["rz1_ready"][p], count("rz1_ready", a, T, t + 1))
                nc.vector.tensor_scalar(neg1[p][:, t, :], ps[:, 0:H], rz1[p][:, t:t + 1], 0.0, ALU.mult,
                                        ALU.min).then_inc(S["neg1_ready"][p], 1)

            @live
            def residual0(a, f):
                p = a[1]
                dve.wait_ge(S["gat1T_made"][p], count("gat1T_made", a, HC, f + 1))
                nc.vector.scalar_tensor_tensor(out1[p][:, f, :], bank[SIDE[f"gat1T_{f}"][p]][:, :], -1.0,
                                               out1[p][:, f, :], ALU.add, ALU.add
                                               ).then_inc(S["res1_ready"][p], 1)

            @live
            def neighbour_max(a, h):
                p = a[1]
                if h == 0:
                    dve.wait_ge(S["f2b_made"][p], count("f2b_made", a, 1, 1))
                    dve.sem_inc(waits_passed, 1)
                for t in (2 * h, 2 * h + 1):
                    nc.vector.tensor_tensor_reduce(out=low[p][:, t, :], in0=bank[SIDE["f2_rows"][p]][:, :],
                                                   in1=neg_nat[:, t, :], scale=1.0, scalar=3 * NEG,
                                                   op0=ALU.add, op1=ALU.max, accum_out=fmax2[p][:, t:t + 1]
                                                   ).then_inc(S["fmax2_ready"][p], 1)

            @live
            def row_terms2(a):
                p = a[1]
                dve.wait_ge(S["fmax2_ready"][p], count("fmax2_ready", a, T))
                nc.vector.tensor_tensor(s2[p][:, :], h2[p][:, :, 0], fmax2[p][:, :], ALU.add
                                        ).then_inc(S["s2_ready"][p], 1)
                dve.wait_ge(S["s2_ready"][p], count("s2_ready", a, 3, 1))
                nc.vector.scalar_tensor_tensor(m2[p][:, :], s2[p][:, :], ALPHA, s2[p][:, :], ALU.mult, ALU.max
                                               ).then_inc(S["s2_ready"][p], 1)
                nc.vector.tensor_scalar(f2s[p][:, :], h2[p][:, :, 1], ALPHA, None, ALU.mult
                                        ).then_inc(S["f2s_ready"][p], 1)
                dve.wait_ge(S["s2_ready"][p], count("s2_ready", a, 3, 2))
                nc.vector.scalar_tensor_tensor(m2[p][:, :], empty[:, :], NEG, m2[p][:, :], ALU.mult, ALU.add
                                               ).then_inc(S["s2_ready"][p], 1)
                dve.wait_ge(S["s2_ready"][p], count("s2_ready", a, 3, 3))
                nc.vector.tensor_tensor(row2[p][:, 0, :], h2[p][:, :, 0], m2[p][:, :], ALU.subtract
                                        ).then_inc(S["row2_ready"][p], 1)
                nc.vector.scalar_tensor_tensor(row2[p][:, 1, :], h2[p][:, :, 0], ALPHA, m2[p][:, :], ALU.mult,
                                               ALU.subtract).then_inc(S["row2_ready"][p], 1)

            @live
            def arguments2(a, j):
                p = a[1]
                dve.wait_ge(S["low2_ready"][p], count("low2_ready", a, T, j + 1))
                nc.vector.scalar_tensor_tensor(low[p][:, j, :], bank[SIDE["R1_rows"][p]][:, :],
                                               h2[p][:, j, 1:2], low[p][:, j, :], ALU.add, ALU.max
                                               ).then_inc(S["arg2_ready"][p], 1)

            @live
            def mask_arguments2(a):
                p = a[1]
                dve.wait_ge(S["arg2_ready"][p], count("arg2_ready", a, T))
                nc.vector.tensor_tensor(low[p][:, 2:4, :], low[p][:, 2:4, :], neg_T[:, 2:4, :], ALU.add
                                        ).then_inc(S["argm1_ready"][p], 1)

            @live
            def normalise2(a, i):
                p = a[1]
                ps = bank[SIDE[f"gat2_{i}"][p]][:, 0:2 * (C + 1)].rearrange("p (t c) -> p t c", t=2)
                dve.wait_ge(S["gat2_made"][p], count("gat2_made", a, 2, i + 1))
                nc.vector.reciprocal(rz2[p][:, 2 * i:2 * i + 2], ps[:, :, C]).then_inc(S["rz2_ready"][p], 1)
                dve.wait_ge(S["rz2_ready"][p], count("rz2_ready", a, 2, i + 1))
                for k in range(2):
                    t = 2 * i + k
                    nc.vector.tensor_scalar(neg2[p][:, t, :], ps[:, k, 0:C], rz2[p][:, t:t + 1], 0.0,
                                            ALU.mult, ALU.min).then_inc(S["neg2_ready"][p], 1)

            def flat(ap):
                return ap.rearrange("p t c -> p (t c)")

            @live
            def finish_gat2(a, step):
                p = a[1]
                if step == 0:
                    dve.wait_ge(S["w2_ready"][p], count("w2_ready", a))
                    nc.vector.tensor_tensor(pos2[p], pos2[p], neg2[p], ALU.add).then_inc(S["sum2_ready"][p], 1)
                elif step == 1:
                    dve.wait_ge(S["sum2_ready"][p], count("sum2_ready", a))
                    dve.wait_ge(S["out2T_made"][p], count("out2T_made", a))
                    nc.vector.scalar_tensor_tensor(flat(pos2[p]), bank[SIDE["out2T"][p]][:, :], -1.0,
                                                   flat(pos2[p]), ALU.add, ALU.add
                                                   ).then_inc(S["sum2b_ready"][p], 1)
                else:
                    dve.wait_ge(S["sum2b_ready"][p], count("sum2b_ready", a))
                    dve.wait_ge(S["x_loaded"][p], count("x_loaded", a, 16))
                    nc.vector.scalar_tensor_tensor(flat(y0[p]), flat(pos2[p]), 0.0, flat(x_nat[p][:, :, :]),
                                                   ALU.max, ALU.add).then_inc(S["y0_ready"][p], 1)

            def grams(bank_part):
                return bank_part[:, 0:2 * P].rearrange("p (i c) -> p i c", i=2)

            @live
            def bound_scores(a, k):
                if not isinstance(a[0], int) or a[0]:
                    return
                dve.wait_ge(bound_made, k + 1)
                if k == 0:
                    nc.vector.tensor_tensor(gram, grams(oacc), same_head.unsqueeze(1).to_broadcast([P, 2, P]),
                                            ALU.mult).then_inc(bound_step, 1)
                elif k == 1:
                    nc.vector.tensor_copy(gram, grams(oacc)).then_inc(bound_step, 1)
                elif k == 2:
                    nc.vector.tensor_copy(gram, grams(oacc)).then_inc(bound_step, 1)
                    dve.wait_ge(bound_step, 5)
                    nc.vector.tensor_tensor(gram, gram, gram, ALU.mult).then_inc(bound_step, 1)
                    dve.wait_ge(bound_step, 6)
                    nc.vector.tensor_reduce(trace, gram, AX_X, ALU.add).then_inc(bound_step, 1)
                elif k == 3:
                    nc.vector.tensor_copy(trace, oacc[:, 0:2]).then_inc(bound_step, 1)
                    dve.wait_ge(bound_step, 8)
                    nc.vector.tensor_scalar(head_ok, trace[:, 0:1], trace[:, 1:2], TRACE_LIMIT, ALU.mult,
                                            ALU.is_le).then_inc(bound_step, 1)
                else:
                    nc.vector.tensor_reduce(all_ok, oacc[:, 0:P], AX_X, ALU.add).then_inc(bound_step, 1)
                    dve.wait_ge(bound_step, 10)
                    nc.vector.tensor_scalar(in_range[:, :], all_ok, P - 0.5, None, ALU.is_gt
                                            ).then_inc(bound_step, 1)

            norms = ((("y0_ready", 1), y0, x1, "x1_ready"), (("y1_ready", 1), attn, y1n, "y1n_ready"),
                     (("y2_ready", 1), y1n, attn, "y2n_ready"), (("y3_ready", 1), attn, y1n, "o_ready"))

            @live
            def statistics(b, i):
                p = b[1]
                (ready, per), src, _, _ = norms[i]
                dve.wait_ge(S[ready][p], count(ready, b, per))
                for t in range(T):
                    nc.vector.bn_stats(stat[i][p][:, t, :], src[p][:, t, :]).then_inc(ln_step[i], 1)
                for t in range(T):
                    dve.wait_ge(ln_step[i], passed(b, 2 * T, t + 1))
                    dve.sem_inc(waits_passed, 1)
                    nc.vector.bn_aggr(mv[i][p][:, t, :], stat[i][p][:, t, :]).then_inc(ln_step[i], 1)

            @live
            def normalise(b, i, h):
                p = b[1]
                _, src, dst, signal = norms[i]
                dve.wait_ge(ln_rstd[i], passed(b, 2, 2))
                if i == 0:
                    if has_former(b):
                        dve.wait_ge(S["xc_ready"][p], count("xc_ready", former(b)))
                if i == 1:
                    if has_former(b):
                        dve.wait_ge(S["stored"][p], count("stored", former(b), 16))
                for t in (2 * h, 2 * h + 1):
                    last = nc.vector.tensor_scalar(dst[p][:, t, :], src[p][:, t, :], mv[i][p][:, t, 0:1],
                                                   rstd[i][p][:, t:t + 1], ALU.subtract, ALU.mult)
                last.then_inc(S[signal][p], 1)

            @live
            def rest(a, i):
                p = a[1]
                dve.wait_ge(S["high_ready"][p], count("high_ready", a, 2, i + 1))
                nc.vector.tensor_tensor(qk_rest[p][:, i, :], bank[SIDE["qk"[i]][p]][:, :],
                                        qk_parts[p][:, i, 0, :], ALU.subtract).then_inc(S["rest_ready"][p], 1)

            @live
            def middle_part(a, i):
                p = a[1]
                dve.wait_ge(S["rest_ready"][p], count("rest_ready", a, 2, i + 1))
                nc.vector.tensor_copy(qk_parts[p][:, i, 1, :], qk_rest[p][:, i, :]
                                      ).then_inc(S["mid_ready"][p], 1)

            @live
            def copy_vcol(a):
                p = a[1]
                dve.wait_ge(S["vcol_made"][p], count("vcol_made", a))
                if has_former(a):
                    dve.wait_ge(S["oT_ready"][p], count("oT_ready", former(a), 2))
                nc.vector.tensor_tensor(vcol[p][:, :], bank[SIDE["vcol"][p]][:, 0:GROUPS], ones_sum[:, :],
                                        ALU.add).then_inc(S["vcol_ready"][p], 1)

            @live
            def mask_scores(b, k):
                p, unit, s = b[1], k // GH, k % GH
                dve.wait_ge(S["scores_made"][p], count("scores_made", b, 16, k + 1))
                if not any(j in DVE_MASKED for j in range(unit * GH, k)):
                    for made, value in probs_readers(b, unit):
                        dve.wait_ge(made, value)
                jp = unit % 2
                nc.vector.tensor_tensor(probs[:, unit % 2, s, :, :], sc[k % 2][:, :, :],
                                        neg_T[:, 2 * jp:2 * jp + 2, :], ALU.add
                                        ).then_inc(S["masked_ready"][p], 1)

            @live
            def take_group(b, g):
                p = b[1]
                dve.wait_ge(S["pv_made"][p], count("pv_made", b, 4, 2 * g + 2))
                dve.wait_ge(S["vcol_ready"][p], count("vcol_ready", b))
                if p:
                    dve.wait_ge(S["oTT_made"][0], count("oTT_made", (b[0], 0), 2, g + 1))
                else:
                    if has_former((b[0], 1)):
                        dve.wait_ge(S["oTT_made"][1], count("oTT_made", former((b[0], 1)), 2, g + 1))
                nc.vector.scalar_tensor_tensor(oT[:, g, :], empty_b[:, :], vcol[p][:, g:g + 1],
                                               oacc[:, :], ALU.mult, ALU.add).then_inc(S["oT_ready"][p], 1)

            @live
            def normalise_heads(b, g):
                p = b[1]
                ps = bank[SIDE[f"oT_{g}"][p]][:, :].rearrange("p (t h s) -> p t h s", t=T, s=STRIP)
                dve.wait_ge(S["oTT_made"][p], count("oTT_made", b, 2, g + 1))
                nc.vector.reciprocal(rzh[p][:, g, :, :], ps[:, :, :, D]).then_inc(S["rzh_ready"][p], 1)
                dve.wait_ge(S["rzh_ready"][p], count("rzh_ready", b, 2, g + 1))
                nc.vector.tensor_tensor(
                    attn[p][:, :, g * GH * D:(g + 1) * GH * D].rearrange("p t (h d) -> p t h d", d=D),
                    ps[:, :, :, 0:D], rzh[p][:, g, :, :].unsqueeze(3).to_broadcast([P, T, GH, D]),
                    ALU.mult).then_inc(S["attn_ready"][p], 1)

            @live
            def residual1(b):
                p = b[1]
                dve.wait_ge(S["attn_ready"][p], count("attn_ready", b, 2))
                dve.wait_ge(S["xc_ready"][p], count("xc_ready", b))
                nc.vector.tensor_tensor(attn[p][:, :, :], attn[p][:, :, :], xc[p][:, :, :], ALU.add
                                        ).then_inc(S["y1_ready"][p], 1)

            @live
            def residual2(b):
                p = b[1]
                dve.wait_ge(S["ff_made"][p], count("ff_made", b))
                dve.wait_ge(S["y1m_ready"][p], count("y1m_ready", b))
                nc.vector.tensor_tensor(flat(y1n[p][:, :, :]), bank[SIDE["ff"][p]][:, :],
                                        flat(y1n[p][:, :, :]), ALU.add).then_inc(S["y2_ready"][p], 1)

            @live
            def residual3(b):
                p = b[1]
                dve.wait_ge(S["y2g_ready"][p], count("y2g_ready", b))
                dve.wait_ge(S["x1b_ready"][p], count("x1b_ready", b))
                nc.vector.tensor_tensor(attn[p][:, :, :], attn[p][:, :, :], xc[p][:, :, :], ALU.add
                                        ).then_inc(S["y3_ready"][p], 1)

            def one_round(a, b, c):
                (a0, a1), (b0, b1), (c0, c1) = a, b, c
                statistics(c0, 1)
                statistics(c1, 1)
                normalise(c0, 1, 0)
                normalise(c1, 1, 0)
                normalise(c0, 1, 1)
                normalise(c1, 1, 1)
                arguments1(a0)
                arguments1(a1)
                weights1(a0, 0)
                weights1(a0, 1)
                weights1(a0, 2)
                weights1(a0, 3)
                bound_scores(a0, 0)
                weights1(a1, 0)
                weights1(a1, 1)
                weights1(a1, 2)
                weights1(a1, 3)
                mask_scores(b0, 0)
                normalise1(a0, 0)
                normalise1(a0, 1)
                normalise1(a1, 0)
                normalise1(a0, 2)
                normalise1(a1, 1)
                normalise1(a0, 3)
                normalise1(a1, 2)
                mask_scores(b0, 2)
                normalise1(a1, 3)
                residual0(a0, 0)
                residual0(a0, 1)
                bound_scores(a0, 1)
                mask_scores(b0, 5)
                residual0(a1, 0)
                neighbour_max(a0, 0)
                residual0(a1, 1)
                neighbour_max(a0, 1)
                bound_scores(a0, 2)
                mask_scores(b0, 8)
                row_terms2(a0)
                mask_scores(b0, 10)
                neighbour_max(a1, 0)
                arguments2(a0, 0)
                neighbour_max(a1, 1)
                arguments2(a0, 1)
                row_terms2(a1)
                arguments2(a0, 2)
                take_group(b0, 0)
                arguments2(a0, 3)
                bound_scores(a0, 3)
                mask_scores(b0, 13)
                mask_arguments2(a0)
                arguments2(a1, 0)
                residual2(c0)
                statistics(c0, 2)
                arguments2(a1, 1)
                arguments2(a1, 2)
                normalise2(a0, 0)
                arguments2(a1, 3)
                normalise(c0, 2, 0)
                normalise2(a0, 1)
                mask_arguments2(a1)
                normalise(c0, 2, 1)
                mask_scores(b1, 0)
                take_group(b0, 1)
                residual3(c0)
                finish_gat2(a0, 0)
                normalise2(a1, 0)
                finish_gat2(a0, 1)
                bound_scores(a0, 4)
                mask_scores(b1, 2)
                finish_gat2(a0, 2)
                statistics(a0, 0)
                normalise2(a1, 1)
                residual2(c1)
                mask_scores(b1, 5)
                statistics(c1, 2)
                finish_gat2(a1, 0)
                normalise(a0, 0, 0)
                normalise(a0, 0, 1)
                normalise(c1, 2, 0)
                finish_gat2(a1, 1)
                normalise(c1, 2, 1)
                finish_gat2(a1, 2)
                mask_scores(b1, 8)
                statistics(a1, 0)
                residual3(c1)
                rest(a0, 0)
                mask_scores(b1, 10)
                middle_part(a0, 0)
                normalise(a1, 0, 0)
                rest(a0, 1)
                normalise(a1, 0, 1)
                statistics(c0, 3)
                mask_scores(b1, 13)
                statistics(c1, 3)
                take_group(b1, 0)
                normalise(c0, 3, 0)
                normalise(c0, 3, 1)
                normalise_heads(b0, 0)
                normalise_heads(b0, 1)
                residual1(b0)
                rest(a1, 0)
                normalise(c1, 3, 0)
                normalise(c1, 3, 1)
                rest(a1, 1)
                middle_part(a1, 0)
                take_group(b1, 1)
                normalise_heads(b1, 0)
                copy_vcol(a0)
                copy_vcol(a1)
                normalise_heads(b1, 1)
                residual1(b1)
                middle_part(a0, 1)
                middle_part(a1, 1)
                if range_known:
                    row_maxima(a)

            range_known = []

            def load_range():
                dve.wait_ge(bound_step, BOUND_STEPS)
                range_known.append(dve.value_load(in_range[0:1, 0:1], min_val=0, max_val=1))
                row_maxima([(0, p, True) for p in range(2)])

            def row_maxima(a):
                if not a[0][2]:
                    return
                with dve.If(range_known[0] < 1):
                    for b in a:
                        p = b[1]
                        for n in range(HEADS * T):
                            h, t = n // T, n % T
                            dve.wait_ge(row_scores_made, passed(b, HEADS * T, n + 1))
                            dve.sem_inc(waits_passed, 1)
                            nc.vector.tensor_tensor_reduce(out=low[p][:, 0, :], in0=sc[n % 2][:, 0, :],
                                                           in1=neg_nat[:, t, :], scale=1.0, scalar=3 * NEG,
                                                           op0=ALU.add, op1=ALU.max,
                                                           accum_out=row_max[p][:, h, t:t + 1]
                                                           ).then_inc(row_max_taken, 1)
                            dve.wait_ge(row_max_taken, passed(b, HEADS * T, n + 1))
                        nc.vector.tensor_scalar(shift_rest[p][:, :, :], row_max[p][:, :, :], -1.0, None,
                                                ALU.mult).then_inc(shift_step, 1)
                        dve.wait_ge(shift_step, passed(b, 6, 1))
                        nc.vector.tensor_copy(shift_parts[p][:, 0, :, :], shift_rest[p][:, :, :]
                                              ).then_inc(shift_step, 1)
                        for i in (1, 2):
                            dve.wait_ge(shift_step, passed(b, 6, 2 * i))
                            nc.vector.tensor_tensor(shift_rest[p][:, :, :], shift_rest[p][:, :, :],
                                                    shift_parts[p][:, i - 1, :, :], ALU.subtract
                                                    ).then_inc(shift_step, 1)
                            dve.wait_ge(shift_step, passed(b, 6, 2 * i + 1))
                            nc.vector.tensor_copy(shift_parts[p][:, i, :, :], shift_rest[p][:, :, :]
                                                  ).then_inc(shift_step, 1)

            rounds(dve, one_round, load_range)

        @block.tensor
        def _(pe):
            pe.wait_ge(const_set, 2)
            pe.wait_ge(prep, PREP_T)
            for k in range(T + 1):
                if k >= 3:
                    pe.wait_ge(prep, PREP_T + k - 2)
                for t in range(T):
                    src = neg_f32[:, t, k * P:(k + 1) * P] if k < T else bc(empty[:, t:t + 1], [P, P])
                    last = nc.tensor.transpose(bank[k % 3][:, t * P:(t + 1) * P], src, ident[:, :])
                last.then_inc(adj_T, 1)
            pe.wait_ge(const_set, 18)
            pe.wait_ge(prep, PREP_T + T + 1)
            pe.wait_ge(w_loaded, W_ALL)

            def last_reader(*users):
                for name, b, per, k, back in users:
                    r = b[0] - back
                    if isinstance(r, int) and not 0 <= r < PAIRS:
                        continue
                    return [(S[name][b[1]], count(name, (r, b[1]), per, k))]
                return []

            def transpose_tiles(dst, src):
                for t in range(T):
                    last = nc.tensor.transpose(dst[:, t * P:(t + 1) * P], src(t), ident[:, :])
                return last

            def side(name, b):
                return bank[SIDE[name][b[1]]]

            @live
            def bound_products(a, k):
                if not isinstance(a[0], int) or a[0]:
                    return
                pe.wait_ge(bound_step, (2, 3, 4, 7, 9)[k])
                if k == 0:
                    for i in range(2):
                        W = Wqkv[:, i * C:(i + 1) * C]
                        last = nc.tensor.matmul(oacc[:, i * P:(i + 1) * P], W, W, start=True, stop=True)
                elif k < 3:
                    for i in range(2):
                        last = nc.tensor.matmul(oacc[:, i * P:(i + 1) * P], gram[:, i, :], gram[:, i, :],
                                                start=True, stop=True)
                elif k == 3:
                    last = nc.tensor.matmul(oacc[:, 0:2], same_head, trace, start=True, stop=True)
                else:
                    last = nc.tensor.transpose(oacc[:, 0:P], bc(head_ok, [P, P]), ident[:, :])
                last.then_inc(bound_made, 1)

            @live
            def transpose_x(a):
                p = a[1]
                pe.wait_ge(S["x_loaded"][p], count("x_loaded", a, 16))
                transpose_tiles(side("xT", a), lambda t: x_nat[p][:, t, :]).then_inc(S["xT_made"][p], 1)

            @live
            def hidden1(a, f):
                p = a[1]
                pe.wait_ge(S["xT_copied"][p], count("xT_copied", a))
                nc.tensor.matmul(side(f"out1_{f}", a)[:, :], W1[:, f * P:(f + 1) * P], xT[p][:, :],
                                 start=True, stop=True).then_inc(S["out1_made"][p], 1)

            @live
            def project1(a, t):
                p = a[1]
                if isinstance(a[0], int) and a[0] == 0:
                    pe.wait_ge(prep, PREP)
                pe.wait_ge(S["out1_ready"][p], count("out1_ready", a, HC))
                for k in range(HC):
                    last = nc.tensor.matmul(side(f"h1_{t}", a)[:, 0:2 + H], out1[p][:, k, t * P:(t + 1) * P],
                                            Wfc[:, k, :], start=(k == 0), stop=(k == HC - 1))
                last.then_inc(S["h1_made"][p], 1)

            @live
            def rows_of_f1(a):
                p = a[1]
                pe.wait_ge(S["h1_copied"][p], count("h1_copied", a, T))
                transpose_tiles(side("f1_rows", a), lambda t: bc(h1[p][:, t, 1:2], [P, P])
                                ).then_inc(S["f1b_made"][p], 1)

            @live
            def rows_of_factors1(a, i):
                p = a[1]
                pe.wait_ge(S["fac1_ready"][p], count("fac1_ready", a))
                name, which = (("A_rows", 0), ("C_rows", 2))[i]
                transpose_tiles(side(name, a), lambda t: bc(fac1[p][:, which, t:t + 1], [P, P])
                                ).then_inc(S["rows1_made"][p], 1)

            @live
            def attend1(a, t, h):
                p = a[1]
                pe.wait_ge(S["att1_ready"][p], count("att1_ready", a, T, 2 * h + 2 if t == 0 else T))
                for j in (2 * h, 2 * h + 1):
                    last = nc.tensor.matmul(side(f"gat1_{t}", a)[:, 0:H + 1], att[p][:, j, t * P:(t + 1) * P],
                                            h1[p][:, j, 2:], start=(j == 0), stop=(j == T - 1))
                if h:
                    last.then_inc(S["gat1_made"][p], 1)

            @live
            def transpose_gat1(a, f):
                p = a[1]
                pe.wait_ge(S["gat1_ready"][p], count("gat1_ready", a, 2))
                transpose_tiles(side(f"gat1T_{f}", a), lambda t: pos1[p][:, t, f * P:(f + 1) * P]
                                ).then_inc(S["gat1T_made"][p], 1)

            @live
            def hidden2(a, k):
                p = a[1]
                pe.wait_ge(S["res1_ready"][p], count("res1_ready", a, HC, k + 1))
                last = nc.tensor.matmul(side("out2", a)[:, :], W2[:, k, :], out1[p][:, k, :], start=(k == 0),
                                        stop=(k == HC - 1))
                if k:
                    last.then_inc(S["out2_made"][p], 1)

            @live
            def project2(a, i):
                p = a[1]
                pe.wait_ge(S["out2_ready"][p], count("out2_ready", a))
                for k in range(2):
                    t = 2 * i + k
                    last = nc.tensor.matmul(side(f"h2_{i}", a)[:, k * (C + 2):(k + 1) * (C + 2)],
                                            out2[p][:, t * P:(t + 1) * P], Wh[:, :], start=True, stop=True)
                last.then_inc(S["h2_made"][p], 1)

            @live
            def rows_of_f2(a):
                p = a[1]
                pe.wait_ge(S["h2_copied"][p], count("h2_copied", a, 2))
                transpose_tiles(side("f2_rows", a), lambda t: bc(h2[p][:, t, 1:2], [P, P])
                                ).then_inc(S["f2b_made"][p], 1)

            @live
            def rows_of_terms2(a, i):
                p = a[1]
                pe.wait_ge(S["row2_ready"][p], count("row2_ready", a, 2))
                transpose_tiles(side(("R1_rows", "R2_rows")[i], a), lambda t: bc(row2[p][:, i, t:t + 1], [P, P])
                                ).then_inc(S["rows2_made"][p], 1)

            @live
            def attend2(a, i, k):
                p = a[1]
                t = 2 * i + k
                pe.wait_ge(S["att2_ready"][p], count("att2_ready", a, 2))
                for j in range(T):
                    last = nc.tensor.matmul(side(f"gat2_{i}", a)[:, k * (C + 1):(k + 1) * (C + 1)],
                                            att[p][:, j, t * P:(t + 1) * P], h2[p][:, j, 2:],
                                            start=(j == 0), stop=(j == T - 1))
                if k:
                    last.then_inc(S["gat2_made"][p], 1)

            @live
            def transpose_out2(a):
                p = a[1]
                transpose_tiles(side("out2T", a), lambda t: out2[p][:, t * P:(t + 1) * P]
                                ).then_inc(S["out2T_made"][p], 1)

            @live
            def transpose_x1(a):
                p = a[1]
                pe.wait_ge(S["x1_ready"][p], count("x1_ready", a, 2))
                transpose_tiles(side("x1T", a), lambda t: x1[p][:, t, :]).then_inc(S["x1T_made"][p], 1)

            @live
            def project_qk(a, i):
                p = a[1]
                pe.wait_ge(S["x1T_copied"][p], count("x1T_copied", a))
                nc.tensor.matmul(side("qk"[i], a)[:, :], Wqkv[:, i * C:(i + 1) * C], x1T[p][:, :],
                                 start=True, stop=True).then_inc(S[("q_made", "k_made")[i]][p], 1)

            @live
            def project_v(a):
                p = a[1]
                pe.wait_ge(S["x1T_copied"][p], count("x1T_copied", a))
                for t in range(T):
                    last = nc.tensor.matmul(side("v", a)[:, t * P:(t + 1) * P], x1T[p][:, t * P:(t + 1) * P],
                                            Wqkv[:, 2 * C:3 * C], start=True, stop=True)
                last.then_inc(S["v_made"][p], 1)

            @live
            def columns_of_v(a):
                p = a[1]
                pe.wait_ge(S["x1T_copied"][p], count("x1T_copied", a))
                for g in range(GROUPS):
                    last = nc.tensor.matmul(side("vcol", a)[:, g:g + 1], Wv_strips[:, g, :], x1_sum[p][:, :],
                                            start=True, stop=True)
                last.then_inc(S["vcol_made"][p], 1)

            def score_reader(b, k):
                if k >= 2:
                    at, k = (b[0], b[1]), k - 2
                elif b[1]:
                    at, k = (b[0], 0), k + 14
                elif has_former(b):
                    at, k = (b[0] - 1, 1), k + 14
                else:
                    return []
                if k in PE_MASKED:
                    return [(S["probs_ready"][at[1]], count("probs_ready", at, 16, k + 1))]
                return [(S["masked_ready"][at[1]], count("masked_ready", at, MASKED_BY_DVE, masked_so_far(k)))]

            @live
            def scores(b, k):
                p, unit, s = b[1], k // GH, k % GH
                g, jp = unit // 2, unit % 2
                if k == 0:
                    pe.wait_ge(S["stacked"][p], count("stacked", b, 16 * 2 * len(Q_TERMS)))
                for read, value in score_reader(b, k):
                    pe.wait_ge(read, value)
                for i in range(2):
                    j = 2 * jp + i
                    if k in PE_MASKED:
                        nc.tensor.matmul(sc[k % 2][:, i, :], ident_bf[:, :], neg_T[:, j, :],
                                         start=True, stop=False)
                    last = nc.tensor.matmul(sc[k % 2][:, i, :], Ks[p][:, g * GH + s, j * P:(j + 1) * P],
                                            Qs[p][:, g * GH + s, :], start=(k not in PE_MASKED), stop=True)
                last.then_inc(S["scores_made"][p], 1)

            @live
            def attend_heads(b, unit, i):
                p = b[1]
                g, jp = unit // 2, unit % 2
                if i == 0:
                    pe.wait_ge(S["probs_ready"][p], count("probs_ready", b, 16, unit * GH + GH))
                    if jp == 0:
                        if g:
                            pe.wait_ge(S["oT_ready"][p], count("oT_ready", b, 2, 1))
                        elif p:
                            pe.wait_ge(S["oT_ready"][0], count("oT_ready", (b[0], 0), 2))
                        else:
                            if has_former((b[0], 1)):
                                pe.wait_ge(S["oT_ready"][1], count("oT_ready", former((b[0], 1)), 2))
                for s in range(GH):
                    last = nc.tensor.matmul(oacc[s * STRIP:(s + 1) * STRIP, :], v[p][:, 2 * jp + i, g, s, :],
                                            probs[:, unit % 2, s, i, :],
                                            start=(jp == 0 and i == 0), stop=(jp == 1 and i == 1))
                if i:
                    last.then_inc(S["pv_made"][p], 1)

            @live
            def transpose_heads(b, g):
                p = b[1]
                pe.wait_ge(S["oT_ready"][p], count("oT_ready", b, 2, g + 1))
                transpose_tiles(side(f"oT_{g}", b), lambda t: oT[:, g, t * P:(t + 1) * P]
                                ).then_inc(S["oTT_made"][p], 1)

            @live
            def transpose_y1(b):
                p = b[1]
                pe.wait_ge(S["y1n_ready"][p], count("y1n_ready", b, 2))
                transpose_tiles(side("y1T", b), lambda t: y1n[p][:, t, :]).then_inc(S["y1T_made"][p], 1)

            @live
            def feed_hidden(b):
                p = b[1]
                pe.wait_ge(S["y1T_copied"][p], count("y1T_copied", b))
                nc.tensor.matmul(side("hid", b)[:, :], M1[:, :], y1T[p][:, :], start=True, stop=True
                                 ).then_inc(S["hid_made"][p], 1)

            @live
            def feed_out(b):
                p = b[1]
                pe.wait_ge(S["hid_ready"][p], count("hid_ready", b))
                for t in range(T):
                    last = nc.tensor.matmul(side("ff", b)[:, t * P:(t + 1) * P], hid[p][:, t * P:(t + 1) * P],
                                            M2[:, :], start=True, stop=True)
                last.then_inc(S["ff_made"][p], 1)

            def one_round(a, b, c):
                (a0, a1), (b0, b1), (c0, c1) = a, b, c
                for read, value in last_reader(("vcol_ready", a0, 1, 1, 1)):
                    pe.wait_ge(read, value)
                transpose_x(a0)
                for read, value in last_reader(("vcol_ready", a1, 1, 1, 1)):
                    pe.wait_ge(read, value)
                transpose_x(a1)
                if a0[2]:
                    pe.wait_ge(S["xT_copied"][0], count("xT_copied", a0, 1, 1))
                hidden1(a0, 0)
                if a1[2]:
                    pe.wait_ge(S["xT_copied"][1], count("xT_copied", a1, 1, 1))
                hidden1(a0, 1)
                if a0[2]:
                    pe.wait_ge(S["out1_ready"][0], count("out1_ready", a0, 2, 1))
                hidden1(a1, 0)
                if a0[2]:
                    pe.wait_ge(S["out1_ready"][0], count("out1_ready", a0, 2, 2))
                project1(a0, 0)
                if a1[2]:
                    pe.wait_ge(S["out1_ready"][1], count("out1_ready", a1, 2, 1))
                hidden1(a1, 1)
                if a0[2]:
                    pe.wait_ge(S["h1_copied"][0], count("h1_copied", a0, 4, 1))
                project1(a0, 1)
                if a1[2]:
                    pe.wait_ge(S["out1_ready"][1], count("out1_ready", a1, 2, 2))
                project1(a1, 0)
                if a0[2]:
                    pe.wait_ge(S["h1_copied"][0], count("h1_copied", a0, 4, 2))
                project1(a0, 2)
                for read, value in last_reader(("attn_ready", b1, 2, 2, 1), ("v_copied", a0, 1, 1,
                        1)):
                    pe.wait_ge(read, value)
                project1(a0, 3)
                if a1[2]:
                    pe.wait_ge(S["h1_copied"][1], count("h1_copied", a1, 4, 1))
                project1(a1, 1)
                if a0[2]:
                    pe.wait_ge(S["h1_copied"][0], count("h1_copied", a0, 4, 4))
                rows_of_f1(a0)
                if a0[2]:
                    pe.wait_ge(S["h1_copied"][0], count("h1_copied", a0, 4, 3))
                project1(a1, 2)
                if a1[2]:
                    pe.wait_ge(S["h1_copied"][1], count("h1_copied", a1, 4, 2))
                project1(a1, 3)
                if a0[2]:
                    pe.wait_ge(S["fmax1_ready"][0], count("fmax1_ready", a0, 1, 1))
                rows_of_factors1(a0, 1)
                if a1[2]:
                    pe.wait_ge(S["h1_copied"][1], count("h1_copied", a1, 4, 3))
                rows_of_factors1(a0, 0)
                bound_products(a0, 0)
                if a1[2]:
                    pe.wait_ge(S["h1_copied"][1], count("h1_copied", a1, 4, 4))
                rows_of_f1(a1)
                scores(b0, 0)
                scores(b0, 1)
                if a1[2]:
                    pe.wait_ge(S["fmax1_ready"][1], count("fmax1_ready", a1, 1, 1))
                rows_of_factors1(a1, 0)
                if a0[2]:
                    pe.wait_ge(S["low1_ready"][0], count("low1_ready", a0, 4, 4))
                rows_of_factors1(a1, 1)
                if a0[2]:
                    pe.wait_ge(S["att1_ready"][0], count("att1_ready", a0, 4, 4))
                attend1(a0, 0, 0)
                attend1(a0, 0, 1)
                if a1[2]:
                    pe.wait_ge(S["low1_ready"][1], count("low1_ready", a1, 4, 4))
                attend1(a0, 1, 0)
                attend1(a0, 1, 1)
                if a1[2]:
                    pe.wait_ge(S["att1_ready"][1], count("att1_ready", a1, 4, 4))
                attend1(a1, 0, 0)
                attend1(a1, 0, 1)
                if a0[2]:
                    pe.wait_ge(S["pos1_ready"][0], count("pos1_ready", a0, 4, 1))
                attend1(a0, 2, 0)
                if a0[2]:
                    pe.wait_ge(S["pos1_ready"][0], count("pos1_ready", a0, 4, 2))
                attend1(a1, 1, 0)
                attend1(a0, 2, 1)
                attend1(a1, 1, 1)
                if a1[2]:
                    pe.wait_ge(S["pos1_ready"][1], count("pos1_ready", a1, 4, 1))
                attend1(a0, 3, 0)
                if a0[2]:
                    pe.wait_ge(S["pos1_ready"][0], count("pos1_ready", a0, 4, 3))
                attend1(a1, 2, 0)
                attend1(a0, 3, 1)
                bound_products(a0, 1)
                attend1(a1, 2, 1)
                if a1[2]:
                    pe.wait_ge(S["pos1_ready"][1], count("pos1_ready", a1, 4, 2))
                attend1(a1, 3, 0)
                scores(b0, 2)
                attend1(a1, 3, 1)
                scores(b0, 3)
                if a1[2]:
                    pe.wait_ge(S["pos1_ready"][1], count("pos1_ready", a1, 4, 3))
                transpose_gat1(a0, 0)
                scores(b0, 4)
                if a1[2]:
                    pe.wait_ge(S["pos1_ready"][1], count("pos1_ready", a1, 4, 4))
                transpose_gat1(a0, 1)
                if a0[2]:
                    pe.wait_ge(S["res1_ready"][0], count("res1_ready", a0, 2, 1))
                hidden2(a0, 0)
                scores(b0, 5)
                hidden2(a0, 1)
                bound_products(a0, 2)
                scores(b0, 6)
                if a0[2]:
                    pe.wait_ge(S["out2_ready"][0], count("out2_ready", a0, 1, 1))
                project2(a0, 0)
                scores(b0, 7)
                if a0[2]:
                    pe.wait_ge(S["h2_copied"][0], count("h2_copied", a0, 2, 1))
                project2(a0, 1)
                if a0[2]:
                    pe.wait_ge(S["res1_ready"][0], count("res1_ready", a0, 2, 2))
                transpose_gat1(a1, 0)
                attend_heads(b0, 0, 0)
                if a1[2]:
                    pe.wait_ge(S["res1_ready"][1], count("res1_ready", a1, 2, 1))
                rows_of_f2(a0)
                if a0[2]:
                    pe.wait_ge(S["h2_copied"][0], count("h2_copied", a0, 2, 2))
                hidden2(a1, 0)
                if a0[2]:
                    pe.wait_ge(S["pos1_ready"][0], count("pos1_ready", a0, 4, 4))
                transpose_gat1(a1, 1)
                scores(b0, 8)
                attend_heads(b0, 0, 1)
                hidden2(a1, 1)
                scores(b0, 9)
                if a1[2]:
                    pe.wait_ge(S["out2_ready"][1], count("out2_ready", a1, 1, 1))
                project2(a1, 0)
                scores(b0, 10)
                if a0[2]:
                    pe.wait_ge(S["fmax2_ready"][0], count("fmax2_ready", a0, 4, 4))
                rows_of_terms2(a0, 0)
                if a1[2]:
                    pe.wait_ge(S["res1_ready"][1], count("res1_ready", a1, 2, 2))
                project2(a1, 1)
                if a1[2]:
                    pe.wait_ge(S["h2_copied"][1], count("h2_copied", a1, 2, 1))
                rows_of_terms2(a0, 1)
                bound_products(a0, 3)
                attend_heads(b0, 1, 0)
                if a1[2]:
                    pe.wait_ge(S["h2_copied"][1], count("h2_copied", a1, 2, 2))
                rows_of_f2(a1)
                attend_heads(b0, 1, 1)
                scores(b0, 11)
                scores(b0, 12)
                for read, value in last_reader(("low2_ready", a0, 4, 4, 0), ("h2_copied", a1, 2, 1,
                        0), ("out2_ready", a1, 1, 1, 0), ("h2_copied", a0, 2, 2, 0), ("h2_copied",
                        a0, 2, 1, 0), ("out2_ready", a0, 1, 1, 0), ("res1_ready", a0, 2, 1, 0),
                        ("pos1_ready", a1, 4, 3, 0), ("pos1_ready", a0, 4, 3, 0), ("pos1_ready", a0,
                        4, 1, 0), ("att1_ready", a0, 4, 4, 0), ("h1_copied", a1, 4, 3, 0),
                        ("h1_copied", a0, 4, 3, 0), ("h1_copied", a0, 4, 2, 0), ("h1_copied", a0, 4,
                        1, 0), ("out1_ready", a0, 2, 2, 0), ("xT_copied", a1, 1, 1, 0),
                        ("vcol_ready", a1, 1, 1, 1), ("v_copied", a1, 1, 1, 1), ("rest_ready", a1,
                        2, 2, 1), ("attn_ready", b0, 2, 2, 1), ("pos2_ready", a1, 4, 4, 1),
                        ("pos2_ready", a0, 4, 2, 1), ("y2_ready", c0, 1, 1, 1)):
                    pe.wait_ge(read, value)
                transpose_y1(c0)
                for read, value in last_reader(("fmax2_ready", a1, 4, 4, 0), ("h2_copied", a1, 2, 2,
                        0), ("res1_ready", a1, 2, 2, 0), ("pos1_ready", a0, 4, 4, 0), ("pos1_ready",
                        a1, 4, 1, 0), ("att1_ready", a1, 4, 4, 0), ("fmax1_ready", a1, 1, 1, 0),
                        ("h1_copied", a1, 4, 4, 0), ("h1_copied", a1, 4, 2, 0), ("h1_copied", a1, 4,
                        1, 0), ("out1_ready", a1, 2, 2, 0), ("out1_ready", a1, 2, 1, 0),
                        ("out1_ready", a0, 2, 1, 0), ("xT_copied", a0, 1, 1, 0), ("vcol_ready", a0,
                        1, 1, 1), ("attn_ready", b1, 2, 1, 1), ("attn_ready", b0, 2, 1, 1),
                        ("sum2b_ready", a0, 1, 1, 1), ("hid_ready", c1, 1, 1, 1)):
                    pe.wait_ge(read, value)
                transpose_y1(c1)
                scores(b0, 13)
                if c0[2]:
                    pe.wait_ge(S["y1T_copied"][0], count("y1T_copied", c0, 1, 1))
                feed_hidden(c0)
                scores(b0, 14)
                for read, value in last_reader(("y1T_copied", c1, 1, 1, 0), ("fmax2_ready", a1, 4,
                        4, 0)):
                    pe.wait_ge(read, value)
                rows_of_terms2(a1, 0)
                attend_heads(b0, 2, 0)
                if a0[2]:
                    pe.wait_ge(S["arg2_ready"][0], count("arg2_ready", a0, 4, 4))
                rows_of_terms2(a1, 1)
                if c0[2]:
                    pe.wait_ge(S["hid_ready"][0], count("hid_ready", c0, 1, 1))
                feed_out(c0)
                scores(b0, 15)
                attend_heads(b0, 2, 1)
                for read, value in last_reader(("y2_ready", c0, 1, 1, 0), ("hid_ready", c0, 1, 1,
                        0), ("y1T_copied", c0, 1, 1, 0), ("low2_ready", a0, 4, 4, 0)):
                    pe.wait_ge(read, value)
                attend2(a0, 0, 0)
                attend2(a0, 0, 1)
                if a1[2]:
                    pe.wait_ge(S["low2_ready"][1], count("low2_ready", a1, 4, 4))
                attend2(a0, 1, 0)
                attend2(a0, 1, 1)
                bound_products(a0, 4)
                scores(b1, 0)
                for read, value in last_reader(("arg2_ready", a1, 4, 4, 0), ("y1T_copied", c1, 1, 1,
                        0)):
                    pe.wait_ge(read, value)
                feed_hidden(c1)
                attend_heads(b0, 3, 0)
                scores(b1, 1)
                attend_heads(b0, 3, 1)
                if a0[2]:
                    pe.wait_ge(S["pos2_ready"][0], count("pos2_ready", a0, 4, 4))
                attend2(a1, 0, 0)
                scores(b1, 2)
                attend2(a1, 0, 1)
                for read, value in last_reader(("hid_ready", c1, 1, 1, 0), ("arg2_ready", a1, 4, 4,
                        0)):
                    pe.wait_ge(read, value)
                transpose_out2(a0)
                if a0[2]:
                    pe.wait_ge(S["pos2_ready"][0], count("pos2_ready", a0, 4, 2))
                attend2(a1, 1, 0)
                scores(b1, 3)
                for read, value in last_reader(("pos2_ready", a1, 4, 2, 0), ("pos2_ready", a0, 4, 4,
                        0), ("low2_ready", a1, 4, 4, 0), ("arg2_ready", a0, 4, 4, 0),
                        ("fmax2_ready", a0, 4, 4, 0), ("res1_ready", a1, 2, 1, 0), ("res1_ready",
                        a0, 2, 2, 0), ("pos1_ready", a1, 4, 4, 0), ("pos1_ready", a1, 4, 2, 0),
                        ("pos1_ready", a0, 4, 2, 0), ("low1_ready", a1, 4, 4, 0), ("low1_ready", a0,
                        4, 4, 0), ("fmax1_ready", a0, 1, 1, 0), ("h1_copied", a0, 4, 4, 0),
                        ("attn_ready", b1, 2, 2, 1), ("v_copied", a0, 1, 1, 1), ("rest_ready", a1,
                        2, 1, 1), ("x1T_copied", a1, 1, 1, 1), ("rest_ready", a0, 2, 2, 1),
                        ("rest_ready", a0, 2, 1, 1), ("x1T_copied", a0, 1, 1, 1), ("sum2b_ready",
                        a1, 1, 1, 1), ("y2_ready", c1, 1, 1, 1)):
                    pe.wait_ge(read, value)
                feed_out(c1)
                attend2(a1, 1, 1)
                scores(b1, 4)
                for read, value in last_reader(("sum2b_ready", a0, 1, 1, 0), ("hid_ready", c1, 1, 1,
                        0), ("arg2_ready", a1, 4, 4, 0), ("y1T_copied", c1, 1, 1, 0),
                        ("fmax2_ready", a1, 4, 4, 0), ("h2_copied", a1, 2, 2, 0), ("res1_ready", a1,
                        2, 2, 0), ("pos1_ready", a0, 4, 4, 0), ("pos1_ready", a1, 4, 1, 0),
                        ("att1_ready", a1, 4, 4, 0), ("fmax1_ready", a1, 1, 1, 0), ("h1_copied", a1,
                        4, 4, 0), ("h1_copied", a1, 4, 2, 0), ("h1_copied", a1, 4, 1, 0),
                        ("out1_ready", a1, 2, 2, 0), ("out1_ready", a1, 2, 1, 0), ("out1_ready", a0,
                        2, 1, 0), ("xT_copied", a0, 1, 1, 0), ("vcol_ready", a0, 1, 1, 1),
                        ("attn_ready", b1, 2, 1, 1)):
                    pe.wait_ge(read, value)
                transpose_heads(b0, 0)
                scores(b1, 5)
                attend_heads(b1, 0, 0)
                attend_heads(b1, 0, 1)
                scores(b1, 6)
                for read, value in last_reader(("pos2_ready", a1, 4, 4, 0), ("pos2_ready", a0, 4, 2,
                        0), ("y2_ready", c0, 1, 1, 0), ("hid_ready", c0, 1, 1, 0), ("y1T_copied",
                        c0, 1, 1, 0), ("low2_ready", a0, 4, 4, 0), ("h2_copied", a1, 2, 1, 0),
                        ("out2_ready", a1, 1, 1, 0), ("h2_copied", a0, 2, 2, 0), ("h2_copied", a0,
                        2, 1, 0), ("out2_ready", a0, 1, 1, 0), ("res1_ready", a0, 2, 1, 0),
                        ("pos1_ready", a1, 4, 3, 0), ("pos1_ready", a0, 4, 3, 0), ("pos1_ready", a0,
                        4, 1, 0), ("att1_ready", a0, 4, 4, 0), ("h1_copied", a1, 4, 3, 0),
                        ("h1_copied", a0, 4, 3, 0), ("h1_copied", a0, 4, 2, 0), ("h1_copied", a0, 4,
                        1, 0), ("out1_ready", a0, 2, 2, 0), ("xT_copied", a1, 1, 1, 0),
                        ("vcol_ready", a1, 1, 1, 1), ("v_copied", a1, 1, 1, 1), ("rest_ready", a1,
                        2, 2, 1), ("attn_ready", b0, 2, 2, 1)):
                    pe.wait_ge(read, value)
                transpose_heads(b0, 1)
                for read, value in last_reader(("y2_ready", c1, 1, 1, 0), ("pos2_ready", a1, 4, 2,
                        0)):
                    pe.wait_ge(read, value)
                transpose_out2(a1)
                scores(b1, 7)
                scores(b1, 8)
                if a1[2]:
                    pe.wait_ge(S["sum2b_ready"][1], count("sum2b_ready", a1, 1, 1))
                transpose_x1(a0)
                attend_heads(b1, 1, 0)
                if a0[2]:
                    pe.wait_ge(S["x1T_copied"][0], count("x1T_copied", a0, 1, 1))
                project_qk(a0, 0)
                scores(b1, 9)
                attend_heads(b1, 1, 1)
                scores(b1, 10)
                if a0[2]:
                    pe.wait_ge(S["rest_ready"][0], count("rest_ready", a0, 2, 1))
                project_qk(a0, 1)
                scores(b1, 11)
                scores(b1, 12)
                if a0[2]:
                    pe.wait_ge(S["rest_ready"][0], count("rest_ready", a0, 2, 2))
                transpose_x1(a1)
                scores(b1, 13)
                scores(b1, 14)
                if a1[2]:
                    pe.wait_ge(S["x1T_copied"][1], count("x1T_copied", a1, 1, 1))
                project_qk(a1, 0)
                scores(b1, 15)
                attend_heads(b1, 2, 0)
                attend_heads(b1, 2, 1)
                if b0[2]:
                    pe.wait_ge(S["attn_ready"][0], count("attn_ready", b0, 2, 1))
                transpose_heads(b1, 0)
                attend_heads(b1, 3, 0)
                for read, value in last_reader(("attn_ready", b0, 2, 2, 0), ("pos2_ready", a1, 4, 4,
                        0)):
                    pe.wait_ge(read, value)
                project_qk(a1, 1)
                attend_heads(b1, 3, 1)
                if a1[2]:
                    pe.wait_ge(S["rest_ready"][1], count("rest_ready", a1, 2, 1))
                project_v(a0)
                if a1[2]:
                    pe.wait_ge(S["rest_ready"][1], count("rest_ready", a1, 2, 2))
                project_v(a1)
                for read, value in last_reader(("v_copied", a0, 1, 1, 0), ("rest_ready", a1, 2, 1,
                        0), ("x1T_copied", a1, 1, 1, 0), ("rest_ready", a0, 2, 2, 0), ("rest_ready",
                        a0, 2, 1, 0), ("x1T_copied", a0, 1, 1, 0), ("sum2b_ready", a1, 1, 1, 0),
                        ("y2_ready", c1, 1, 1, 0), ("pos2_ready", a1, 4, 2, 0), ("pos2_ready", a0,
                        4, 4, 0), ("low2_ready", a1, 4, 4, 0), ("arg2_ready", a0, 4, 4, 0),
                        ("fmax2_ready", a0, 4, 4, 0), ("res1_ready", a1, 2, 1, 0), ("res1_ready",
                        a0, 2, 2, 0), ("pos1_ready", a1, 4, 4, 0), ("pos1_ready", a1, 4, 2, 0),
                        ("pos1_ready", a0, 4, 2, 0), ("low1_ready", a1, 4, 4, 0), ("low1_ready", a0,
                        4, 4, 0), ("fmax1_ready", a0, 1, 1, 0), ("h1_copied", a0, 4, 4, 0),
                        ("attn_ready", b1, 2, 2, 1)):
                    pe.wait_ge(read, value)
                transpose_heads(b1, 1)
                for read, value in last_reader(("attn_ready", b1, 2, 1, 0), ("attn_ready", b0, 2, 1,
                        0), ("sum2b_ready", a0, 1, 1, 0)):
                    pe.wait_ge(read, value)
                columns_of_v(a0)
                if a1[2]:
                    pe.wait_ge(S["v_copied"][1], count("v_copied", a1, 1, 1))
                columns_of_v(a1)
                if range_known:
                    row_scores(a)

            range_known = []

            def load_range():
                pe.wait_ge(bound_step, BOUND_STEPS)
                range_known.append(pe.value_load(in_range[0:1, 0:1], min_val=0, max_val=1))
                row_scores([(0, p, True) for p in range(2)])

            def row_scores(a):
                if not a[0][2]:
                    return
                with pe.If(range_known[0] < 1):
                    for b in a:
                        p = b[1]
                        pe.wait_ge(S["stacked"][p], count("stacked", b, 16 * 2 * len(Q_TERMS)))
                        for n in range(HEADS * T):
                            h, t = n // T, n % T
                            if p == 0 and n < 2:
                                for read, value in score_reader((b[0], 0), n):
                                    pe.wait_ge(read, value)
                            elif p == 0 or n >= 2:
                                pe.wait_ge(row_max_taken, passed(b, HEADS * T, n - 1))
                            else:
                                pe.wait_ge(row_max_taken, passed((b[0], 0), HEADS * T, HEADS * T - 1 + n))
                            nc.tensor.matmul(sc[n % 2][:, 0, :], Qs[p][0:KP, h, t * P:(t + 1) * P],
                                             Ks[p][0:KP, h, :], start=True, stop=True
                                             ).then_inc(row_scores_made, 1)
                    pe.wait_ge(row_max_taken, passed(a[1], HEADS * T, HEADS * T))
                    pe.wait_ge(shift_loaded, passed(a[1], 16, 16))

            rounds(pe, one_round, load_range)


_INS = ["x", "adj", "L0_gnn_mlp1_w", "L0_gnn_mlp1_b", "L0_gnn_mlp2_w", "L0_gnn_mlp2_b", "L0_gnn_W_fc",
        "L0_gnn_a_fc", "L0_gnn_W_hand", "L0_gnn_a_hand", "L1_gnn_w_qkv", "L1_gnn_ln1_g", "L1_gnn_ln1_b",
        "L1_gnn_ln2_g", "L1_gnn_ln2_b", "L1_gnn_w1", "L1_gnn_b1", "L1_gnn_w2", "L1_gnn_b2"]


def kernel(**inputs):
    import numpy as _np
    import concourse.bacc as _bacc
    from concourse.bass_utils import run_bass_kernel_spmd as _run

    nc = _bacc.Bacc("TRN2", target_bir_lowering=False, num_devices=1)
    arrays, args = {}, []
    for name in _INS:
        a = _np.ascontiguousarray(inputs[name])
        arrays[f"in_{name}_dram"] = a
        args.append(nc.dram_tensor(f"in_{name}_dram", a.shape, mybir.dt.from_np(a.dtype),
                                   kind="ExternalInput").ap())
    out = nc.dram_tensor("out_dram", (B, N, C), F32, kind="ExternalOutput").ap()
    gnn_kernel(nc, *args, out)
    r = _run(nc, [arrays], core_ids=[0])
    return r.results[0]["out_dram"]
```
